# Optimizing a Trainium2 kernel written in Bass

```python
import numpy as np
import jax
import jax.numpy as jnp

def _softmax(x, axis=-1):
    return jax.nn.softmax(x, axis=axis)

def _gelu(x):
    return jax.nn.gelu(x, approximate=True)

def _silu(x):
    return jax.nn.silu(x)

def _sigmoid(x):
    return jax.nn.sigmoid(x)

def _layernorm(x, axis=-1, eps=1e-05):
    m = jnp.mean(x, axis=axis, keepdims=True)
    v = jnp.var(x, axis=axis, keepdims=True)
    return (x - m) / jnp.sqrt(v + eps)

def _scatter_add(tgt, idx, src, axis=0):
    return tgt.at[idx].add(src)

def _segment_sum(src, seg, n):
    return jax.ops.segment_sum(src, seg, n)
kernel_name = 'mk_macaron_d1_jaxref_r4_9d5a06'

def setup_inputs(seed: int=0):
    np.random.seed(seed)
    _w = jnp.asarray

    def _L0_attn_setup():
        import jax, jax.numpy as jnp
        import numpy as np
        D = 256
        H = 16
        HD = 64
        AHD = H * HD
        B = 4
        S = 256
        EPS = 1e-05
        SMAX = float(D) ** 0.5

        def _ln(x, s, b):
            mu = jnp.mean(x, axis=-1, keepdims=True)
            var = jnp.mean(jnp.square(x - mu), axis=-1, keepdims=True)
            return (x - mu) * jax.lax.rsqrt(var + EPS) * s + b

        def _forward(x, lnq_s, lnq_b, Wq, bq, lnk_s, lnk_b, Wk, bk, lnv_s, lnv_b, Wv, bv, Wo, bo, lnm_s, lnm_b, W1, b1, W2, b2):
            Bq, Sq, _ = x.shape
            q = (_ln(x, lnq_s, lnq_b) @ Wq + bq).reshape(Bq, Sq, H, HD).transpose(0, 2, 1, 3)
            k = (_ln(x, lnk_s, lnk_b) @ Wk + bk).reshape(Bq, Sq, H, HD).transpose(0, 2, 1, 3)
            v = (_ln(x, lnv_s, lnv_b) @ Wv + bv).reshape(Bq, Sq, H, HD).transpose(0, 2, 1, 3)
            scores = jnp.einsum('bhqd,bhkd->bhqk', q, k) / SMAX
            mask = jnp.triu(jnp.full((Sq, Sq), -999.0, dtype=scores.dtype), k=Sq - 1)
            p = jax.nn.softmax(scores + mask, axis=-1)
            att = jnp.einsum('bhqk,bhkd->bhqd', p, v).transpose(0, 2, 1, 3).reshape(Bq, Sq, AHD)
            h = att @ Wo + bo + x
            y = _ln(h, lnm_s, lnm_b)
            m = jax.nn.gelu(y @ W1 + b1) @ W2 + b2
            return m + h
        key = jax.random.key(seed)
        ks = jax.random.split(key, 7)

        def lin(k, fan_in, fan_out):
            lim = 1.0 / np.sqrt(fan_in)
            kw, kb = jax.random.split(k)
            W = jax.random.uniform(kw, (fan_in, fan_out), minval=-lim, maxval=lim, dtype=jnp.float32)
            b = jax.random.uniform(kb, (fan_out,), minval=-lim, maxval=lim, dtype=jnp.float32)
            return (W, b)
        Wq, bq = lin(ks[0], D, AHD)
        Wk, bk = lin(ks[1], D, AHD)
        Wv, bv = lin(ks[2], D, AHD)
        Wo, bo = lin(ks[3], AHD, D)
        W1, b1 = lin(ks[4], D, 2 * D)
        W2, b2 = lin(ks[5], 2 * D, D)
        x = jax.random.normal(ks[6], (B, S, D), dtype=jnp.float32)
        ones = jnp.ones((D,), jnp.float32)
        zeros = jnp.zeros((D,), jnp.float32)
        return {'x': x, 'lnq_s': ones, 'lnq_b': zeros, 'Wq': Wq, 'bq': bq, 'lnk_s': ones, 'lnk_b': zeros, 'Wk': Wk, 'bk': bk, 'lnv_s': ones, 'lnv_b': zeros, 'Wv': Wv, 'bv': bv, 'Wo': Wo, 'bo': bo, 'lnm_s': ones, 'lnm_b': zeros, 'W1': W1, 'b1': b1, 'W2': W2, 'b2': b2}
    _L0_attn_in = _L0_attn_setup()

    def _L0_ffn_setup():
        import jax, jax.numpy as jnp
        import numpy as np
        B, S, D, E, H, K = (4, 512, 256, 8, 128, 2)
        key = jax.random.key(seed)
        ks = jax.random.split(key, 11)
        sc = 0.02
        return {'x': jax.random.normal(ks[0], (B, S, D), dtype=jnp.float32), 'gate_W': jax.random.normal(ks[1], (D, E), dtype=jnp.float32) * sc, 'W1': jax.random.normal(ks[2], (E, D, H), dtype=jnp.float32) * sc, 'b1': jnp.zeros((E, H), dtype=jnp.float32), 'W2': jax.random.normal(ks[3], (E, H, D), dtype=jnp.float32) * sc, 'b2': jnp.zeros((E, D), dtype=jnp.float32), 'Ws1': jax.random.normal(ks[4], (D, H), dtype=jnp.float32) * sc, 'bs1': jnp.zeros((H,), dtype=jnp.float32), 'Ws2': jax.random.normal(ks[5], (H, D), dtype=jnp.float32) * sc, 'bs2': jnp.zeros((D,), dtype=jnp.float32), 'route_scale': jnp.ones((), dtype=jnp.float32)}
    _L0_ffn_in = _L0_ffn_setup()
    _d = {'L0_attn_x': _L0_attn_in['x'], 'L0_attn_lnq_s': _L0_attn_in['lnq_s'], 'L0_attn_lnq_b': _L0_attn_in['lnq_b'], 'L0_attn_Wq': _L0_attn_in['Wq'], 'L0_attn_bq': _L0_attn_in['bq'], 'L0_attn_lnk_s': _L0_attn_in['lnk_s'], 'L0_attn_lnk_b': _L0_attn_in['lnk_b'], 'L0_attn_Wk': _L0_attn_in['Wk'], 'L0_attn_bk': _L0_attn_in['bk'], 'L0_attn_lnv_s': _L0_attn_in['lnv_s'], 'L0_attn_lnv_b': _L0_attn_in['lnv_b'], 'L0_attn_Wv': _L0_attn_in['Wv'], 'L0_attn_bv': _L0_attn_in['bv'], 'L0_attn_Wo': _L0_attn_in['Wo'], 'L0_attn_bo': _L0_attn_in['bo'], 'L0_attn_lnm_s': _L0_attn_in['lnm_s'], 'L0_attn_lnm_b': _L0_attn_in['lnm_b'], 'L0_attn_W1': _L0_attn_in['W1'], 'L0_attn_b1': _L0_attn_in['b1'], 'L0_attn_W2': _L0_attn_in['W2'], 'L0_attn_b2': _L0_attn_in['b2'], 'L0_ffn_gate_W': _L0_ffn_in['gate_W'], 'L0_ffn_W1': _L0_ffn_in['W1'], 'L0_ffn_b1': _L0_ffn_in['b1'], 'L0_ffn_W2': _L0_ffn_in['W2'], 'L0_ffn_b2': _L0_ffn_in['b2'], 'L0_ffn_Ws1': _L0_ffn_in['Ws1'], 'L0_ffn_bs1': _L0_ffn_in['bs1'], 'L0_ffn_Ws2': _L0_ffn_in['Ws2'], 'L0_ffn_bs2': _L0_ffn_in['bs2'], 'L0_ffn_route_scale': _L0_ffn_in['route_scale']}
    _x0 = _d['L0_attn_x']
    _d['L0_attn_x'] = jax.random.normal(jax.random.fold_in(jax.random.key(seed), 1), (4, 1024, 256), dtype=_x0.dtype)
    del _x0
    return _d

def reference(L0_attn_x, L0_attn_lnq_s, L0_attn_lnq_b, L0_attn_Wq, L0_attn_bq, L0_attn_lnk_s, L0_attn_lnk_b, L0_attn_Wk, L0_attn_bk, L0_attn_lnv_s, L0_attn_lnv_b, L0_attn_Wv, L0_attn_bv, L0_attn_Wo, L0_attn_bo, L0_attn_lnm_s, L0_attn_lnm_b, L0_attn_W1, L0_attn_b1, L0_attn_W2, L0_attn_b2, L0_ffn_gate_W, L0_ffn_W1, L0_ffn_b1, L0_ffn_W2, L0_ffn_b2, L0_ffn_Ws1, L0_ffn_bs1, L0_ffn_Ws2, L0_ffn_bs2, L0_ffn_route_scale):

    def _L0_attn_ref(x, lnq_s, lnq_b, Wq, bq, lnk_s, lnk_b, Wk, bk, lnv_s, lnv_b, Wv, bv, Wo, bo, lnm_s, lnm_b, W1, b1, W2, b2):
        import jax, jax.numpy as jnp
        import numpy as np
        D = 256
        H = 16
        HD = 64
        AHD = H * HD
        B = 4
        S = 256
        EPS = 1e-05
        SMAX = float(D) ** 0.5

        def _ln(x, s, b):
            mu = jnp.mean(x, axis=-1, keepdims=True)
            var = jnp.mean(jnp.square(x - mu), axis=-1, keepdims=True)
            return (x - mu) * jax.lax.rsqrt(var + EPS) * s + b

        def _forward(x, lnq_s, lnq_b, Wq, bq, lnk_s, lnk_b, Wk, bk, lnv_s, lnv_b, Wv, bv, Wo, bo, lnm_s, lnm_b, W1, b1, W2, b2):
            Bq, Sq, _ = x.shape
            q = (_ln(x, lnq_s, lnq_b) @ Wq + bq).reshape(Bq, Sq, H, HD).transpose(0, 2, 1, 3)
            k = (_ln(x, lnk_s, lnk_b) @ Wk + bk).reshape(Bq, Sq, H, HD).transpose(0, 2, 1, 3)
            v = (_ln(x, lnv_s, lnv_b) @ Wv + bv).reshape(Bq, Sq, H, HD).transpose(0, 2, 1, 3)
            scores = jnp.einsum('bhqd,bhkd->bhqk', q, k) / SMAX
            mask = jnp.triu(jnp.full((Sq, Sq), -999.0, dtype=scores.dtype), k=Sq - 1)
            p = jax.nn.softmax(scores + mask, axis=-1)
            att = jnp.einsum('bhqk,bhkd->bhqd', p, v).transpose(0, 2, 1, 3).reshape(Bq, Sq, AHD)
            h = att @ Wo + bo + x
            y = _ln(h, lnm_s, lnm_b)
            m = jax.nn.gelu(y @ W1 + b1) @ W2 + b2
            return m + h
        return _forward(x, lnq_s, lnq_b, Wq, bq, lnk_s, lnk_b, Wk, bk, lnv_s, lnv_b, Wv, bv, Wo, bo, lnm_s, lnm_b, W1, b1, W2, b2)

    def _L0_ffn_ref(x, gate_W, W1, b1, W2, b2, Ws1, bs1, Ws2, bs2, route_scale):
        import jax, jax.numpy as jnp
        import numpy as np
        B, S, D, E, H, K = (4, 512, 256, 8, 128, 2)
        scores = jax.nn.sigmoid(x @ gate_W) * route_scale
        topk_scores, topk_idx = jax.lax.top_k(scores, K)
        topk_w = topk_scores / topk_scores.sum(-1, keepdims=True)
        onehot = jax.nn.one_hot(topk_idx, E, dtype=x.dtype)
        gate_full = jnp.einsum('bsk,bske->bse', topk_w, onehot)
        h = jax.nn.gelu(jnp.einsum('bsd,edh->bseh', x, W1) + b1, approximate=False)
        y = jnp.einsum('bseh,ehd->bsed', h, W2) + b2
        expert_out = jnp.einsum('bse,bsed->bsd', gate_full, y)
        shared = jax.nn.gelu(x @ Ws1 + bs1, approximate=False) @ Ws2 + bs2
        return expert_out + shared
    x = L0_attn_x
    x = x + 0.5 * _L0_ffn_ref(_layernorm(x, axis=-1), L0_ffn_gate_W, L0_ffn_W1, L0_ffn_b1, L0_ffn_W2, L0_ffn_b2, L0_ffn_Ws1, L0_ffn_bs1, L0_ffn_Ws2, L0_ffn_bs2, L0_ffn_route_scale)
    x = x + _L0_attn_ref(_layernorm(x, axis=-1), L0_attn_lnq_s, L0_attn_lnq_b, L0_attn_Wq, L0_attn_bq, L0_attn_lnk_s, L0_attn_lnk_b, L0_attn_Wk, L0_attn_bk, L0_attn_lnv_s, L0_attn_lnv_b, L0_attn_Wv, L0_attn_bv, L0_attn_Wo, L0_attn_bo, L0_attn_lnm_s, L0_attn_lnm_b, L0_attn_W1, L0_attn_b1, L0_attn_W2, L0_attn_b2)
    x = x + 0.5 * _L0_ffn_ref(_layernorm(x, axis=-1), L0_ffn_gate_W, L0_ffn_W1, L0_ffn_b1, L0_ffn_W2, L0_ffn_b2, L0_ffn_Ws1, L0_ffn_bs1, L0_ffn_Ws2, L0_ffn_bs2, L0_ffn_route_scale)
    return x

_drawn_inputs = setup_inputs


def setup_inputs(seed=0):
    import zlib

    import numpy as np

    out = dict(_drawn_inputs(seed))
    spreads = {'L0_attn_lnq_s': (1.0, 0.6),
     'L0_attn_lnq_b': (0.0, 0.8),
     'L0_attn_lnk_s': (1.0, 0.6),
     'L0_attn_lnk_b': (0.0, 0.8),
     'L0_attn_lnv_s': (1.0, 0.6),
     'L0_attn_lnv_b': (0.0, 0.473),
     'L0_attn_lnm_s': (1.0, 0.6),
     'L0_attn_lnm_b': (0.0, 0.73),
     'L0_ffn_b1': (0.0, 0.8),
     'L0_ffn_b2': (0.0, 0.1),
     'L0_ffn_bs1': (0.0, 0.8),
     'L0_ffn_bs2': (0.0, 0.1)}
    factors = {'L0_attn_Wq': 8.0,
     'L0_attn_bq': 8.0,
     'L0_attn_Wk': 8.0,
     'L0_attn_bk': 8.0,
     'L0_attn_Wv': 2.949,
     'L0_attn_bv': 5.103,
     'L0_attn_bo': 5.971,
     'L0_attn_b1': 7.95,
     'L0_attn_b2': 4.609,
     'L0_ffn_W1': 2.824}
    for name, (base, spread) in spreads.items():
        noise = np.random.default_rng([zlib.crc32(name.encode()), seed]).standard_normal(out[name].shape)
        drawn = base * np.exp(spread * noise) if base else spread * noise
        out[name] = jnp.asarray(drawn.astype(out[name].dtype))
    for name, factor in factors.items():
        out[name] = (out[name] * factor).astype(out[name].dtype)
    return out
```

```python
from contextlib import ExitStack

import numpy as np

import concourse.bass as bass
from concourse import mybir

F32 = mybir.dt.float32
F32R = mybir.dt.float32r
U32 = mybir.dt.uint32
ALU = mybir.AluOpType
ACT = mybir.ActivationFunctionType
AX = mybir.AxisListType

P = 128
B, S, D = 4, 1024, 256
TOK = B * S
H, HD = 16, 64
AHD = H * HD
E, HID = 8, 128
NE = E + 1
MH = 2 * D
DC = D // P
BT = 512
NT = BT // P
NB = TOK // BT
EPS = 1e-5
MASK = -999.0
TOP = 2
E_NUM = float(np.float32(np.e))


def stand_alone(eng, turns):
    eng.sem_inc(turns, 1)


class Bank:

    def __init__(self, nc, ctx, tag):
        self.nc, self.ctx, self.tag = nc, ctx, tag

    def sb(self, name, shape, dt=F32):
        return self.ctx.enter_context(self.nc.sbuf_tensor(f"{self.tag}_{name}", shape, dt))

    def ps(self, name, shape):
        return self.ctx.enter_context(self.nc.psum_tensor(f"{self.tag}_{name}", shape, F32))

    def sem(self, name):
        return self.ctx.enter_context(self.nc.semaphore(f"{self.tag}_{name}"))


def ffn_phase(nc, tag, src, dst, w, tail):
    with ExitStack() as ctx:
        m = Bank(nc, ctx, tag)
        ident = m.sb("ident", [P, P])
        sel_in = m.sb("sel_in", [P, E * P])
        sel = m.sb("sel", [P, E * P], F32R)
        w1_in = m.sb("w1_in", [P, DC * NE * HID])
        w1p = m.sb("w1p", [P, 2, DC * NE * HID], F32R)
        w2_in = m.sb("w2_in", [P, NE * D])
        w2p = m.sb("w2p", [P, 2, NE * D], F32R)
        gw_in = m.sb("gw_in", [P, DC * E])
        gwp = m.sb("gwp", [P, DC, 2, E], F32R)
        b1 = m.sb("b1", [P, NE])
        b2_in = m.sb("b2_in", [P, D])
        b2hi = m.sb("b2hi", [P, D], F32R)
        b2lo = m.sb("b2lo", [P, D], F32R)
        b2s = m.sb("b2s", [P, D], F32R)
        rows = m.sb("rows", [P, 2])
        rsc = m.sb("rsc", [P, 1])
        iota = m.sb("iota", [P, E])
        mhalf = m.sb("mhalf", [P, NT])
        ebase = m.sb("ebase", [P, NT * E])

        xin = m.sb("xin", [P, 2, NT, D])
        xres = m.sb("xres", [P, NT, D])
        st6 = m.sb("st6", [P, NT, 6])
        mv = m.sb("mv", [P, NT, 2])
        rs = m.sb("rs", [P, NT])
        xn = m.sb("xn", [P, NT, D])
        xT = m.sb("xT", [P, 2, DC, 2, BT], F32R)
        gl = m.sb("gl", [P, NT, E])
        nl = m.sb("nl", [P, NT, E])
        sg = m.sb("sg", [P, NT, E])
        top = m.sb("top", [P, NT, 8])
        idx = m.sb("idx", [P, NT, 8], U32)
        idf = m.sb("idf", [P, NT, 8])
        wt = m.sb("wt", [P, NT, TOP])
        ws = m.sb("ws", [P, NT])
        ga = m.sb("ga", [P, NT, E])
        gb_ = m.sb("gb_", [P, NT, E])
        ghi = m.sb("ghi", [P, NT, E], F32R)
        gpad = m.sb("gpad", [P, NT, P])
        gst = m.sb("gst", [P, 2, BT], F32R)
        act_out = m.sb("act_out", [P, 3, BT])
        gated = m.sb("gated", [P, 3, BT])
        hp = m.sb("hp", [P, 3, 2, BT], F32R)
        res = m.sb("res", [P, NT, D])
        if tail:
            zst6 = m.sb("zst6", [P, NT, 6])
            zmv = m.sb("zmv", [P, NT, 2])
            zrs = m.sb("zrs", [P, NT])
            zz = m.sb("zz", [P, NT, D])
            zn = m.sb("zn", [P, NT, D])
            zT = m.sb("zT", [P, DC, 2, BT], F32R)

        hid = m.ps("hid", [P, 2, BT])
        gbc = m.ps("gbc", [P, 2, BT])
        acc = m.ps("acc", [P, NT, D])
        aux = m.ps("aux", [P, 2, BT])

        s = {n: m.sem(n) for n in (
            "veps z_veps w_in zeroed w_hi w_ready x_in xres bn stats rstd xn xT_ps xT_hi xT_lo logits neg expneg gate gpad gT_ps gst "
            "hid gelu gbc gated h_hi h_lo out res res_out z_bn z_stats z_rstd z z_done "
            "zn zT_ps zT_hi zT_lo zT_out z_out").split()}
        dve_turns, pool_turns = m.sem("dve_turns"), m.sem("pool_turns")
        NW = 14
        GC = 12

        def shared(e):
            return e == E

        block = ctx.enter_context(nc.Block())

        def over_blocks(eng, body):
            body(0, 0, True, False)
            with eng.Fori(0, (NB - 2) // 2) as it:
                body(it * 2 + 1, 1, False, False)
                body(it * 2 + 2, 0, False, False)
            body(NB - 1, 1, False, True)

        def rows_of(ap, i):
            return ap.rearrange("(n t p) d -> n p t d", t=NT, p=P)[bass.ds(i, 1)].rearrange("n p t d -> p (n t) d")

        @block.sync
        def _(sp):
            sp.dma_start(ident[:], w["ident"]).then_inc(s["w_in"], 16)
            sp.dma_start(gw_in[:], w["gw"]).then_inc(s["w_in"], 16)
            sp.dma_start(xin[:, 0], rows_of(src, 0)).then_inc(s["x_in"], 16)
            sp.dma_start(w1_in[:], w["w1"]).then_inc(s["w_in"], 16)
            sp.dma_start(sel_in[:], w["sel"]).then_inc(s["w_in"], 16)
            sp.dma_start(b1[:], w["b1"]).then_inc(s["w_in"], 16)
            sp.dma_start(rows[:], w["rows"]).then_inc(s["w_in"], 16)
            sp.dma_start(iota[:], w["iota"]).then_inc(s["w_in"], 16)
            sp.dma_start(rsc[:], w["rscale"].partition_broadcast(P)).then_inc(s["w_in"], 16)
            sp.wait_ge(s["zeroed"], 1)
            for k in range(3):
                sp.dma_start(b2_in[k * E:(k + 1) * E], w["b2"][0:E]).then_inc(s["w_in"], 16)
            for k in range(2):
                sp.dma_start(b2_in[3 * E + k:3 * E + k + 1], w["b2"][E:NE]).then_inc(s["w_in"], 16)
            sp.dma_start(w2_in[:], w["w2"]).then_inc(s["w_in"], 16)

            def store(i):
                to = rows_of(dst, sp.snap(i) if i is not NB - 1 else i)
                if tail:
                    z_to = rows_of(tail["z"], sp.snap(i) if i is not NB - 1 else i)
                    zT_to = tail["zT"][bass.ds(sp.snap(i) if i is not NB - 1 else i, 1)].rearrange(
                        "n p c k t -> p (n c k) t")
                sp.wait_ge(s["res"], i + 1)
                sp.dma_start(to, res[:]).then_inc(s["res_out"], 16)
                if tail:
                    sp.wait_ge(s["z"], i + 1)
                    sp.dma_start(z_to, zz[:]).then_inc(s["z_out"], 16)
                    sp.wait_ge(s["zT_lo"], i * DC + DC)
                    sp.dma_start(zT_to, zT[:].bitcast(F32).rearrange("p c k t -> p (c k) t")).then_inc(s["zT_out"], 16)

            def body(i, par, first, last):
                if not last:
                    ahead = rows_of(src, 1 if first else sp.snap(i + 1))
                    sp.wait_ge(s["xn"], i + 1)
                    sp.dma_start(xin[:, 1 - par], ahead).then_inc(s["x_in"], 16)
                again = rows_of(src, i if first or last else sp.snap(i))
                if not first:
                    sp.wait_ge(s["res"], i)
                sp.dma_start(xres[:], again).then_inc(s["xres"], 16)
                if not first:
                    store(i - 1)
            over_blocks(sp, body)
            store(NB - 1)
            sp.wait_ge(s["res_out"], NB * 16 + 16)
            if tail:
                sp.wait_ge(s["z_out"], NB * 16 + 16)
                sp.wait_ge(s["zT_out"], NB * 16 + 16)

        @block.scalar
        def _(act):
            if tail:
                act.sem_inc(s["zT_out"], 16)
            act.preload_act_table(ACT.Gelu)
            act.wait_ge(s["w_in"], 16 * NW)
            act.activation(gwp[:, :, 0, :], gw_in[:].rearrange("p (c e) -> p c e", c=DC), ACT.Identity)
            act.activation(w1p[:, 0], w1_in[:], ACT.Identity)
            act.activation(w2p[:, 0], w2_in[:], ACT.Identity)
            act.activation(sel[:], sel_in[:], ACT.Identity)
            act.activation(b2hi[:], b2_in[:], ACT.Identity).then_inc(s["w_hi"], 1)

            def xt_hi(i, par):
                for c in range(DC):
                    act.wait_ge(s["xT_ps"], i * DC + c + 1)
                    act.activation(xT[:, par, c, 0], aux[:, c], ACT.Identity).then_inc(s["xT_hi"], 1)

            def zt_hi(i):
                for c in range(DC):
                    act.wait_ge(s["zT_ps"], i * DC + c + 1)
                    if c == 0:
                        act.wait_ge(s["zT_out"], i * 16 + 16)
                    act.activation(zT[:, c, 0], aux[:, c], ACT.Identity).then_inc(s["zT_hi"], 1)

            def hi(i, e, first):
                if e >= 3 or not first:
                    act.wait_ge(s["out"], i * NE + e - 2)
                if shared(e):
                    act.wait_ge(s["gelu"], i * NE + e + 1)
                    from_ = act_out
                else:
                    act.wait_ge(s["gated"], i * E + e + 1)
                    from_ = gated
                act.activation(hp[:, e % 3, 0], from_[:, e % 3], ACT.Identity).then_inc(s["h_hi"], 1)

            def body(i, par, first, last):
                for e in range(NE):
                    act.wait_ge(s["hid"], i * NE + e + 1)
                    if e >= 3 or not first:
                        act.wait_ge(s["h_lo"], i * NE + e - 2)
                    act.activation(act_out[:, e % 3], hid[:, (par + e) % 2], ACT.Gelu,
                                   bias=b1[:, e:e + 1]).then_inc(s["gelu"], 1)
                    if e > 0:
                        hi(i, e - 1, first)
                    elif not first:
                        hi(i - 1, E, False)
                    if e == 3 and not last:
                        xt_hi(i + 1, 1 - par)
                    if e == 5 and tail and not first:
                        zt_hi(i - 1)
            xt_hi(0, 0)
            over_blocks(act, body)
            hi(NB - 1, E, False)
            if tail:
                zt_hi(NB - 1)

        @block.gpsimd
        def _(pool):
            pool.memset(b2_in[:], 0.0).then_inc(s["zeroed"], 1)
            pool.memset(gpad[:], 0.0).then_inc(s["zeroed"], 1)
            pool.wait_ge(s["zeroed"], 2)
            pool.memset(gpad[:, :, 3 * E:3 * E + 2], 1.0)
            pool.memset(mhalf[:], -0.5)
            pool.memset(ebase[:], E_NUM).then_inc(s["zeroed"], 1)
            pool.wait_ge(s["zeroed"], 3)


            def x_rstd(i):
                pool.wait_ge(s["stats"], i + 1)
                stand_alone(pool, pool_turns)
                pool.tensor_scalar(rs[:], mv[:, :, 1], EPS, None, ALU.add).then_inc(s["veps"], 1)
                pool.wait_ge(s["veps"], i + 1)
                pool.tensor_tensor(rs[:], rs[:], mhalf[:], ALU.pow).then_inc(s["rstd"], 1)

            def expneg(i):
                pool.wait_ge(s["neg"], i + 1)
                pool.tensor_tensor(nl[:].rearrange("p t e -> p (t e)"), ebase[:],
                                   nl[:].rearrange("p t e -> p (t e)"), ALU.pow).then_inc(s["expneg"], 1)

            def z_rstds(i, which):
                pool.wait_ge(s["z_stats"], i * 2 + which + 1)
                stand_alone(pool, pool_turns)
                pool.tensor_scalar(zrs[:], zmv[:, :, 1], EPS, None, ALU.add).then_inc(s["z_veps"], 1)
                pool.wait_ge(s["z_veps"], i * 2 + which + 1)
                pool.tensor_tensor(zrs[:], zrs[:], mhalf[:], ALU.pow).then_inc(s["z_rstd"], 1)

            def body(i, par, first, last):
                if tail and not first:
                    z_rstds(i - 1, 0)
                if not last:
                    x_rstd(i + 1)
                if tail and not first:
                    z_rstds(i - 1, 1)
                if not last:
                    expneg(i + 1)
            x_rstd(0)
            expneg(0)
            over_blocks(pool, body)
            if tail:
                z_rstds(NB - 1, 0)
                z_rstds(NB - 1, 1)

        @block.vector
        def _(dve):
            def norm_stats(x, t6, out, bn, stats, nbn):
                for t in range(NT):
                    o = dve.bn_stats(t6[:, t], x[:, t])
                o.then_inc(bn, 1)
                dve.wait_ge(bn, nbn)
                stand_alone(dve, dve_turns)
                for t in range(NT):
                    o = dve.bn_aggr(out[:, t], t6[:, t])
                o.then_inc(stats, 1)

            def x_stats(i, par):
                dve.wait_ge(s["x_in"], i * 16 + 16)
                norm_stats(xin[:, par], st6, mv, s["bn"], s["stats"], i + 1)

            def x_norm(i, par, first):
                dve.wait_ge(s["rstd"], i + 1)
                if not first:
                    dve.wait_ge(s["xT_ps"], i * DC)
                for t in range(NT):
                    o = dve.tensor_scalar(xn[:, t], xin[:, par, t], mv[:, t, 0:1], rs[:, t:t + 1],
                                          ALU.subtract, ALU.mult)
                o.then_inc(s["xn"], 1)

            def xt_lo(i, par):
                for c in range(DC):
                    dve.wait_ge(s["xT_hi"], i * DC + c + 1)
                    dve.tensor_tensor(xT[:, par, c, 1], aux[:, c], xT[:, par, c, 0].bitcast(F32),
                                      ALU.subtract).then_inc(s["xT_lo"], 1)

            def neg_logits(i):
                ps = aux[:, 0, 0:NT * 2 * E].rearrange("p (t k e) -> p t k e", t=NT, k=2)
                dve.wait_ge(s["logits"], i + 1)
                dve.tensor_scalar(gl[:], ps[:, :, 1], -1.0, None, ALU.mult).then_inc(s["gate"], 1)
                dve.wait_ge(s["gate"], i * GC + 1)
                dve.scalar_tensor_tensor(out=nl[:], in0=ps[:, :, 0], scalar=-1.0, in1=gl[:],
                                         op0=ALU.mult, op1=ALU.add).then_inc(s["neg"], 1)

            def gates(i):
                n = [i * GC + 1]

                def link(o):
                    o.then_inc(s["gate"], 1)
                    n[0] = n[0] + 1
                    dve.wait_ge(s["gate"], n[0])
                dve.wait_ge(s["expneg"], i + 1)
                link(dve.tensor_scalar(sg[:], nl[:], 1.0, None, ALU.add))
                link(dve.reciprocal(sg[:], sg[:]))
                link(dve.tensor_scalar(sg[:], sg[:], rsc[:, 0:1], None, ALU.mult))
                stand_alone(dve, dve_turns)
                for t in range(NT):
                    o = dve.max(top[:, t], sg[:, t])
                link(o)
                stand_alone(dve, dve_turns)
                for t in range(NT):
                    o = dve.max_index(idx[:, t], top[:, t], sg[:, t])
                link(o)
                dve.tensor_tensor(ws[:], top[:, :, 0], top[:, :, 1], ALU.add)
                link(dve.tensor_copy(idf[:], idx[:]))
                link(dve.reciprocal(ws[:], ws[:]))
                for k in range(TOP):
                    o = dve.tensor_tensor(wt[:, :, k], top[:, :, k], ws[:], ALU.mult)
                link(o)
                for t in range(NT):
                    dve.tensor_scalar(ga[:, t], iota[:], idf[:, t, 0:1], wt[:, t, 0:1], ALU.is_equal, ALU.mult)
                    o = dve.tensor_scalar(gb_[:, t], iota[:], idf[:, t, 1:2], wt[:, t, 1:2], ALU.is_equal, ALU.mult)
                link(o)
                link(dve.tensor_tensor(ga[:], ga[:], gb_[:], ALU.add))
                dve.tensor_copy(ghi[:], ga[:]).then_inc(s["gate"], 1)
                dve.wait_ge(s["gate"], (i + 1) * GC)
                g = ghi[:].bitcast(F32)
                dve.tensor_copy(gpad[:, :, 0:E], g)
                dve.tensor_copy(gpad[:, :, 2 * E:3 * E], g)
                dve.tensor_tensor(gpad[:, :, E:2 * E], ga[:], g, ALU.subtract).then_inc(s["gpad"], 1)

            def gate_stack(i, par):
                dve.wait_ge(s["gT_ps"], i + 1)
                dve.tensor_copy(gst[:, par], aux[:, 1]).then_inc(s["gst"], 1)

            def gating(i, e):
                dve.wait_ge(s["gelu"], i * NE + e + 1)
                dve.wait_ge(s["gbc"], i * E + e + 1)
                dve.tensor_tensor(gated[:, e % 3], gbc[:, e % 2], act_out[:, e % 3],
                                  ALU.mult).then_inc(s["gated"], 1)

            def lo(i, e):
                dve.wait_ge(s["h_hi"], i * NE + e + 1)
                from_ = act_out if shared(e) else gated
                dve.tensor_tensor(hp[:, e % 3, 1], from_[:, e % 3], hp[:, e % 3, 0].bitcast(F32),
                                  ALU.subtract).then_inc(s["h_lo"], 1)

            def result(i):
                dve.wait_ge(s["out"], i * NE + NE)
                dve.wait_ge(s["xres"], i * 16 + 16)
                dve.wait_ge(s["res_out"], i * 16 + 16)
                for h in range(2):
                    t = slice(2 * h, 2 * h + 2)
                    o = dve.scalar_tensor_tensor(out=res[:, t], in0=acc[:, t], scalar=0.5,
                                                 in1=xres[:, t], op0=ALU.mult, op1=ALU.add)
                o.then_inc(s["res"], 1)

            def z_stats(i):
                dve.wait_ge(s["res"], i + 1)
                norm_stats(res, zst6, zmv, s["z_bn"], s["z_stats"], i * 2 + 1)

            def z_norm(i):
                dve.wait_ge(s["z_rstd"], i * 2 + 1)
                dve.wait_ge(s["z_out"], i * 16 + 16)
                for t in range(NT):
                    o = dve.tensor_scalar(zz[:, t], res[:, t], zmv[:, t, 0:1], zrs[:, t:t + 1],
                                          ALU.subtract, ALU.mult)
                o.then_inc(s["z"], 1)
                dve.wait_ge(s["z"], i + 1)
                norm_stats(zz, zst6, zmv, s["z_bn"], s["z_stats"], i * 2 + 2)

            def zn_norm(i):
                dve.wait_ge(s["z_rstd"], i * 2 + 2)
                for t in range(NT):
                    o = dve.tensor_scalar(zn[:, t], zz[:, t], zmv[:, t, 0:1], zrs[:, t:t + 1],
                                          ALU.subtract, ALU.mult)
                o.then_inc(s["zn"], 1)

            def zt_lo(i):
                for c in range(DC):
                    dve.wait_ge(s["zT_hi"], i * DC + c + 1)
                    dve.tensor_tensor(zT[:, c, 1], aux[:, c], zT[:, c, 0].bitcast(F32),
                                      ALU.subtract).then_inc(s["zT_lo"], 1)

            dve.sem_inc(s["res_out"], 16)
            if tail:
                dve.sem_inc(s["z_out"], 16)
            x_stats(0, 0)
            x_norm(0, 0, True)
            dve.wait_ge(s["w_hi"], 1)
            dve.tensor_tensor(gwp[:, :, 1, :], gw_in[:].rearrange("p (c e) -> p c e", c=DC),
                              gwp[:, :, 0, :].bitcast(F32), ALU.subtract)
            dve.tensor_tensor(w1p[:, 1], w1_in[:], w1p[:, 0].bitcast(F32), ALU.subtract)
            dve.tensor_tensor(w2p[:, 1], w2_in[:], w2p[:, 0].bitcast(F32), ALU.subtract)
            dve.tensor_tensor(b2lo[:], b2_in[:], b2hi[:].bitcast(F32), ALU.subtract).then_inc(s["w_ready"], 1)
            dve.wait_ge(s["w_ready"], 1)
            dve.tensor_scalar(b2_in[:], b2lo[:].bitcast(F32), rows[:, 1:2], None, ALU.mult).then_inc(s["w_ready"], 1)
            dve.wait_ge(s["w_ready"], 2)
            dve.scalar_tensor_tensor(out=b2s[:], in0=b2hi[:].bitcast(F32), scalar=rows[:, 0:1], in1=b2_in[:],
                                     op0=ALU.mult, op1=ALU.add).then_inc(s["w_ready"], 1)

            def body(i, par, first, last):
                for e in range(NE):
                    if not shared(e):
                        gating(i, e)
                    if e > 0:
                        lo(i, e - 1)
                    elif not first:
                        lo(i - 1, E)
                    if not first:
                        if e == 1:
                            result(i - 1)
                            if tail:
                                z_stats(i - 1)
                        if e == 3 and tail:
                            z_norm(i - 1)
                        if e == 4 and tail:
                            zn_norm(i - 1)
                        if e == 5 and tail:
                            zt_lo(i - 1)
                    if not last:
                        if e == 1:
                            x_stats(i + 1, 1 - par)
                        if e == 2:
                            x_norm(i + 1, 1 - par, False)
                        if e == 3:
                            xt_lo(i + 1, 1 - par)
                        if e == 4:
                            neg_logits(i + 1)
                        if e == 6:
                            gates(i + 1)
                        if e == 7:
                            gate_stack(i + 1, 1 - par)
            xt_lo(0, 0)
            neg_logits(0)
            dve.wait_ge(s["zeroed"], 3)
            gates(0)
            gate_stack(0, 0)
            over_blocks(dve, body)
            lo(NB - 1, E)
            result(NB - 1)
            if tail:
                z_stats(NB - 1)
                z_norm(NB - 1)
                zn_norm(NB - 1)
                zt_lo(NB - 1)

        @block.tensor
        def _(pe):
            def transposes(i, from_, ready, done):
                pe.wait_ge(ready, i + 1)
                for c in range(DC):
                    for t in range(NT):
                        o = pe.transpose(aux[:, c, t * P:(t + 1) * P], from_[:, t, c * P:(c + 1) * P], ident[:])
                    o.then_inc(done, 1)

            def logits(i, par):
                pe.wait_ge(s["xT_lo"], i * DC + DC)
                for t in range(NT):
                    for c in range(DC):
                        for k in range(2):
                            n = 2 * E if k == 0 else E
                            o = pe.matmul(aux[:, 0, t * 2 * E:t * 2 * E + n],
                                          xT[:, par, c, k, t * P:(t + 1) * P],
                                          gwp[:, c].rearrange("p k e -> p (k e)")[:, 0:n],
                                          start=(t == 0 and c == 0 and k == 0), stop=(c == DC - 1 and k == 1),
                                          skip_group_check=True)
                o.then_inc(s["logits"], 1)

            def gates_up(i):
                pe.wait_ge(s["gpad"], i + 1)
                for t in range(NT):
                    o = pe.transpose(aux[:, 1, t * P:(t + 1) * P], gpad[:, t], ident[:])
                o.then_inc(s["gT_ps"], 1)

            PARTS = ((0, 0), (0, 1), (1, 0))

            def first_layer(i, e, par, start):
                if not start:
                    pe.wait_ge(s["gelu"], i * NE + e - 1)
                n = 0
                for c in range(DC):
                    for a, b in PARTS:
                        o = pe.matmul(hid[:, (par + e) % 2], w1p[:, a, (c * NE + e) * HID:(c * NE + e + 1) * HID],
                                      xT[:, par, c, b], start=(n == 0), stop=(n == 5))
                        n += 1
                o.then_inc(s["hid"], 1)
                if not shared(e):
                    if e == 0:
                        pe.wait_ge(s["gst"], i + 1)
                    if e >= 2 or not start:
                        pe.wait_ge(s["gated"], i * E + e - 1)
                    pe.matmul(gbc[:, e % 2], sel[:, e * P:(e + 1) * P], gst[:, par],
                              start=True, stop=True).then_inc(s["gbc"], 1)

            def second_layer(i, e, par, first):
                if e == 0:
                    if not first:
                        pe.wait_ge(s["res"], i)
                    for t in range(NT):
                        pe.matmul(acc[:, t], gst[:, par, t * P:(t + 1) * P], b2s[:],
                                  start=(t % 2 == 0), stop=False, skip_group_check=True)
                pe.wait_ge(s["h_lo"], i * NE + e + 1)
                for t in range(NT):
                    for a, b in PARTS:
                        o = pe.matmul(acc[:, t], hp[:, e % 3, a, t * P:(t + 1) * P],
                                      w2p[:, b, e * D:(e + 1) * D], start=False, stop=(shared(e) and (a, b) == (1, 0)),
                                      skip_group_check=True)
                o.then_inc(s["out"], 1)

            def body(i, par, first, last):
                for e in range(NE):
                    first_layer(i, e, par, first and e < 2)
                    if e >= 2:
                        second_layer(i, e - 2, par, first)
                    elif not first:
                        second_layer(i - 1, E - 1 + e, 1 - par, False)
                    if not last:
                        if e == 3:
                            pe_next_transposes(i + 1, first)
                        if e == 4:
                            logits(i + 1, 1 - par)
                        if e == 7:
                            if tail and not first:
                                pe.wait_ge(s["zT_lo"], i * DC)
                            gates_up(i + 1)
                    if e == 5 and tail and not first:
                        if not last:
                            pe.wait_ge(s["neg"], i + 2)
                        transposes(i - 1, zn, s["zn"], s["zT_ps"])

            def pe_next_transposes(i, first):
                pe.wait_ge(s["gst"], i)
                transposes(i, xn, s["xn"], s["xT_ps"])

            pe.wait_ge(s["w_in"], 16 * NW)
            transposes(0, xn, s["xn"], s["xT_ps"])
            pe.wait_ge(s["w_ready"], 3)
            logits(0, 0)
            gates_up(0)
            over_blocks(pe, body)
            second_layer(NB - 1, E - 1, 1, False)
            second_layer(NB - 1, E, 1, False)
            if tail:
                pe.wait_ge(s["zT_lo"], (NB - 1) * DC)
                transposes(NB - 1, zn, s["zn"], s["zT_ps"])


def qkv_weights_phase(nc, tag, w, wqk, wv, bias):
    PAIRS = AHD // P
    QS = float(D) ** -0.5
    with ExitStack() as ctx:
        m = Bank(nc, ctx, tag)
        w_in = m.sb("w_in", [P, 3, DC, AHD])
        scaled = m.sb("scaled", [P, 3, DC, AHD])
        split = m.sb("split", [P, 3, DC, 2, AHD], F32R)
        ln = m.sb("ln", [P, 3, DC, 2])
        c_in = m.sb("c_in", [P, 3, PAIRS])
        b_sb = m.sb("b_sb", [P, PAIRS, 3])
        pb = m.ps("pb", [P, 3, PAIRS])
        s_in, s_sc, s_hi, s_lo, s_pb, s_b, s_out = (m.sem(n) for n in "in scaled hi lo pb b out".split())
        block = ctx.enter_context(nc.Block())

        @block.sync
        def _(sp):
            sp.dma_start(ln[:], w["ln_qkv"]).then_inc(s_in, 16)
            sp.dma_start(c_in[:], w["c_qkv"]).then_inc(s_in, 16)
            for k in range(3):
                sp.dma_start(w_in[:, k], w["w_qkv"][k]).then_inc(s_in, 16)
            sp.wait_ge(s_lo, 1)
            for g in range(PAIRS):
                for k in range(2):
                    sp.dma_start(wqk[g, :, k], split[:, k, :, :, g * P:(g + 1) * P].bitcast(F32)).then_inc(s_out, 16)
            for g in range(PAIRS // 2):
                sp.dma_start(wv[g], split[:, 2, :, :, g * 2 * P:(g + 1) * 2 * P].bitcast(F32)).then_inc(s_out, 16)
            sp.wait_ge(s_b, 3)
            sp.dma_start(bias, b_sb[:]).then_inc(s_out, 16)
            sp.wait_ge(s_out, 16 * (PAIRS * 2 + PAIRS // 2 + 1))

        @block.scalar
        def _(act):
            act.wait_ge(s_sc, 1)
            act.activation(split[:, :, :, 0], scaled[:], ACT.Identity).then_inc(s_hi, 1)

        @block.vector
        def _(dve):
            dve.wait_ge(s_in, 80)
            for k in range(3):
                for c in range(DC):
                    o = dve.tensor_scalar(scaled[:, k, c], w_in[:, k, c], ln[:, k, c, 0:1],
                                          QS if k == 0 else 1.0, ALU.mult, ALU.mult)
            o.then_inc(s_sc, 1)
            dve.wait_ge(s_pb, 1)
            dve.tensor_tensor(b_sb[:].rearrange("p g k -> p k g"), pb[:], c_in[:], ALU.add).then_inc(s_b, 1)
            dve.wait_ge(s_b, 1)
            dve.tensor_scalar(b_sb[:, :, 0], b_sb[:, :, 0], QS, None, ALU.mult).then_inc(s_b, 2)
            dve.wait_ge(s_hi, 1)
            dve.tensor_tensor(split[:, :, :, 1], scaled[:], split[:, :, :, 0].bitcast(F32),
                              ALU.subtract).then_inc(s_lo, 1)

        @block.tensor
        def _(pe):
            pe.wait_ge(s_in, 80)
            for k in range(3):
                for g in range(PAIRS):
                    for c in range(DC):
                        o = pe.matmul(pb[:, k, g:g + 1], w_in[:, k, c, g * P:(g + 1) * P], ln[:, k, c, 1:2],
                                      start=(c == 0), stop=(c == DC - 1))
            o.then_inc(s_pb, 1)


def attention_phase(nc, tag, w, zT, wqk, wv, bias, att):
    PAIRS = AHD // P
    STEPS = 16
    ITER = 2 * STEPS
    NIT = B * PAIRS // 2
    LAG = 3
    QT = S // P
    NP = 4
    with ExitStack() as ctx:
        m = Bank(nc, ctx, tag)
        ident = m.sb("ident", [P, P])
        bsb = m.sb("bsb", [P, PAIRS, 3])
        bqk_s = m.sb("bqk_s", [P, 2])
        wqk_s = m.sb("wqk_s", [P, 2, DC, 2, P], F32R)
        wv_s = m.sb("wv_s", [P, DC, 2, 2 * P], F32R)
        z_s = m.sb("z_s", [P, DC * 2, 2, BT], F32R)
        q_s = m.sb("q_s", [P, 2, 2, S], F32R)
        k_s = m.sb("k_s", [P, 2, 2, 2, S], F32R)
        v_s = m.sb("v_s", [P, 2, QT, 4, HD], F32R)
        v_b = m.sb("v_b", [P, QT, 4, HD], F32R)
        pr = m.sb("pr", [P, NP, S])
        nmax = m.sb("nmax", [P, NP])
        den = m.sb("den", [P, NP])
        rden = m.sb("rden", [P, NP])
        pT = m.sb("pT", [P, 2, 2, QT, BT], F32R)
        half = m.sb("half", [P, BT])
        ao = m.sb("ao", [P, 2, BT])
        sc = m.ps("sc", [P, 2, S])
        ring = m.ps("ring", [P, 2, BT])
        ov = m.ps("ov", [P, 2, BT])

        s = {n: m.sem(n) for n in (
            "const z_in wqk_in wv_in v_in k_dup sc masked negmax exp rden normed chunk hi lo "
            "proj pv halved att att_out").split()}
        turns = m.sem("turns")

        PROJ = {7: [("Q", 0)], 8: [("Q", 1)], 9: [("K", 0)], 10: [("K", 1)]}
        VALS = {11: [("V", 0)], 12: [("V", 1)], 13: [("V", 2)], 14: [("V", 3)]}

        def chunks_of(step):
            t = step % STEPS
            return [("T", 0), ("T", 1)] + PROJ.get(t, []) + (VALS.get(t, []) if step >= STEPS else [])
        PLAN = [chunks_of(k) for k in range(ITER)]
        PER = sum(len(x) for x in PLAN)
        START = [sum(len(x) for x in PLAN[:k]) for k in range(ITER)]
        FIRST = [("Q", 0), ("Q", 1), ("K", 0), ("K", 1), ("V", 0), ("V", 1), ("V", 2), ("V", 3)]
        BASE = len(FIRST) - 2 * LAG
        assert PER % 2 == 0 and BASE % 2 == 0

        def number(it, step, n):
            return it * PER + BASE + START[step] + n

        def steps(it, first=False, last=False):
            for k in range(LAG + 5 if last else ITER):
                plan = [(*x, number(it, k, n), (START[k] + n) % 2) for n, x in enumerate(PLAN[k])]
                if last:
                    plan = plan[:2] if k < LAG else []
                yield k, plan[2:] if first and k < LAG else plan

        def over_iterations(eng, body):
            body(0, True, False)
            with eng.Fori(1, NIT) as it:
                body(it, False, False)
            body(NIT, False, True)

        def values_at(k, first):
            j = k - LAG - 4
            if first and j < 0:
                return None
            block = j // 4
            return (block // 4) % 2, (block // 2) % 2, block, j % 4

        def finished_at(k, first):
            v = values_at(k - 1, first) if k > 0 or not first else None
            return v if v and v[3] == 3 else None

        block_ = ctx.enter_context(nc.Block())

        def pair_of(it, slot):
            return it // 4, (it % 4) * 2 + slot

        def after(it):
            return (it + 1) % NIT

        @block_.sync
        def _(sp):
            def fixed(x):
                return x if isinstance(x, int) else sp.snap(x)

            def load_z(it):
                sp.dma_start(z_s[:].bitcast(F32), zT[bass.ds(fixed((it // 4) * 2), 2)].rearrange("h p c k t -> p (c k) h t"))\
                    .then_inc(s["z_in"], 16)

            def load_wqk(it, slot):
                g = fixed((it % 4) * 2 + slot)
                sp.dma_start(wqk_s[:].bitcast(F32).rearrange("p k c l f -> p (k c l f)"),
                             wqk[bass.ds(g, 1)].rearrange("g p k c l f -> p (g k c l f)")).then_inc(s["wqk_in"], 16)
                sp.dma_start(bqk_s[:], bias[:, bass.ds(g, 1), 0:2].rearrange("p g k -> p (g k)"))\
                    .then_inc(s["wqk_in"], 16)

            def load_wv(it):
                sp.dma_start(wv_s[:].bitcast(F32).rearrange("p c l f -> p (c l f)"),
                             wv[bass.ds(fixed(it % 4), 1)].rearrange("g p c l f -> p (g c l f)")).then_inc(s["wv_in"], 16)

            def double_k(slot):
                for head, (a, b) in enumerate(((0, HD), (HD, 0))):
                    sp.dma_start(k_s[b:b + HD, slot, head].bitcast(F32), k_s[a:a + HD, slot, head].bitcast(F32))\
                        .then_inc(s["k_dup"], 16)

            def move_v():
                sp.dma_start(v_s[:, 1].bitcast(F32).rearrange("p t k f -> p (t k f)"),
                             v_b[:].bitcast(F32).rearrange("p t k f -> p (t k f)")).then_inc(s["v_in"], 16)

            def store(it, slot, blocks):
                b, hp = pair_of(it, slot)
                to = att[bass.ds(fixed(hp), 1), :, bass.ds(fixed(b * S), S)].rearrange("g p t -> p (g t)")
                sp.wait_ge(s["att"], blocks)
                sp.dma_start(to, ao[:].rearrange("p h t -> p (h t)")).then_inc(s["att_out"], 16)

            sp.dma_start(ident[:], w["ident"]).then_inc(s["const"], 16)
            sp.dma_start(bsb[:], bias).then_inc(s["const"], 16)
            load_z(0)
            load_wqk(0, 0)
            load_wv(0)
            sp.wait_ge(s["lo"], 4)
            double_k(0)
            load_wqk(0, 1)
            sp.wait_ge(s["lo"], 8)
            load_wv(1)
            move_v()

            def body(it, first, last):
                if not first:
                    if not last:
                        sp.wait_ge(s["pv"], it * 8)
                        move_v()
                    store(it - 1, 1, it * 8)
                if last:
                    return
                sp.wait_ge(s["lo"], number(it, 10, 3))
                double_k(1)
                load_wqk(after(it), 0)
                load_z(after(it))
                store(it, 0, it * 8 + 4)
                sp.wait_ge(s["lo"], number(it, STEPS + 10, 3))
                double_k(0)
                load_wqk(after(it), 1)
                sp.wait_ge(s["lo"], number(it, STEPS + 14, 3))
                load_wv(after(it + 1))
            over_iterations(sp, body)
            sp.wait_ge(s["att_out"], 16 * B * PAIRS)
            sp.wait_ge(s["wv_in"], 16 * (NIT + 2))
            sp.wait_ge(s["wqk_in"], 32 * (2 * NIT + 2))
            sp.wait_ge(s["z_in"], 16 * (NIT + 1))
            sp.wait_ge(s["k_dup"], 32 * (2 * NIT + 1))

        def v_parts(slot, t):
            to = (v_s[:, 0] if slot == 0 else v_b[:])[:, 2 * t:2 * t + 2]
            return to[:, :, 0::3], to[:, :, 1:3]

        def rows_of_head(head):
            return slice(head * HD, head * HD + HD)

        @block_.scalar
        def _(act):
            act.preload_act_table(ACT.Exp)
            act.wait_ge(s["const"], 32)

            def hi(it, k, kind, part, n, bank):
                act.wait_ge(s["chunk"], n + 1)
                cols = slice(part * BT, part * BT + BT)
                if kind == "T":
                    u = (k - LAG) % ITER
                    o = act.activation(pT[:, (u // 4) % 2, 0, 4 * part:4 * part + 4, (u % 4) * P:(u % 4 + 1) * P],
                                       ring[:, bank].rearrange("p (t q) -> p t q", t=4), ACT.Identity)
                elif kind in "QK":
                    slot = ((k // STEPS) + 1) % 2
                    for head in range(2):
                        r = rows_of_head(head)
                        to = q_s[r, slot, head, cols] if kind == "Q" else k_s[r, slot, head, 0, cols]
                        o = act.activation(to, ring[r, bank], ACT.Identity, bias=bqk_s[r, "QK".index(kind):"QK".index(kind) + 1])
                else:
                    from_ = ring[:, bank].rearrange("p (t s h f) -> p t s h f", t=2, s=2, h=2)
                    for slot in range(2):
                        o = act.activation(v_parts(slot, part)[0], from_[:, :, slot], ACT.Identity)
                o.then_inc(s["hi"], 1)

            act.wait_ge(s["wqk_in"], 32)
            for n, (kind, part) in enumerate(FIRST):
                hi(0, STEPS, kind, part, n, n % 2)

            def body(it, first, last):
                for k, chunks in steps(it, first, last):
                    v = finished_at(k, first)
                    if v:
                        act.wait_ge(s["pv"], it * 8 + v[2] + 1)
                        if not (first and v[2] == 0):
                            act.wait_ge(s["att"], it * 8 + v[2])
                        act.activation(half[rows_of_head(v[1])], ov[rows_of_head(1 - v[1]), v[2] % 2],
                                       ACT.Identity).then_inc(s["halved"], 1)
                    for kind, part, n, bank in chunks:
                        hi(it, k, kind, part, n, bank)
                    if not last:
                        u = it * ITER + k
                        act.wait_ge(s["negmax"], u + 1)
                        act.activation(pr[:, k % NP], sc[:, k % 2], ACT.Exp, bias=nmax[:, k % NP:k % NP + 1],
                                       accum_out=den[:, k % NP:k % NP + 1]).then_inc(s["exp"], 1)
            over_iterations(act, body)

        @block_.gpsimd
        def _(pool):
            def body(it, first, last):
                for k in range(0 if last else ITER):
                    pool.wait_ge(s["rden"], it * ITER + k + 1)
                    stand_alone(pool, turns)
                    pool.tensor_scalar(pr[:, k % NP], pr[:, k % NP], rden[:, k % NP:k % NP + 1], 1.0,
                                       ALU.mult, ALU.mult).then_inc(s["normed"], 1)
            over_iterations(pool, body)

        @block_.vector
        def _(dve):
            dve.wait_ge(s["const"], 32)

            def lo(it, k, kind, part, n, bank, g):
                dve.wait_ge(s["hi"], n + 1)
                cols = slice(part * BT, part * BT + BT)
                if kind == "T":
                    u = (k - LAG) % ITER
                    to = pT[:, (u // 4) % 2, :, 4 * part:4 * part + 4, (u % 4) * P:(u % 4 + 1) * P]
                    o = dve.tensor_tensor(to[:, 1], ring[:, bank].rearrange("p (t q) -> p t q", t=4),
                                          to[:, 0].bitcast(F32), ALU.subtract)
                elif kind in "QK":
                    slot = ((k // STEPS) + 1) % 2
                    j = "QK".index(kind)
                    for head in range(2):
                        r, other = rows_of_head(head), rows_of_head(1 - head)
                        hi_, to = ((q_s[r, slot, head, cols], q_s[other, slot, head, cols]) if kind == "Q" else
                                   (k_s[r, slot, head, 0, cols], k_s[r, slot, head, 1, cols]))
                        o = dve.scalar_tensor_tensor(out=to, in0=ring[r, bank], scalar=bqk_s[r, j:j + 1],
                                                     in1=hi_.bitcast(F32), op0=ALU.add, op1=ALU.subtract)
                else:
                    from_ = ring[:, bank].rearrange("p (t s h f) -> p t s h f", t=2, s=2, h=2)
                    for slot in range(2):
                        h, l = v_parts(slot, part)
                        o = dve.tensor_tensor(l, from_[:, :, slot], h.bitcast(F32), ALU.subtract)
                o.then_inc(s["lo"], 1)

            def recip(u, k):
                dve.wait_ge(s["exp"], u + 1)
                dve.reciprocal(rden[:, k % NP:k % NP + 1], den[:, k % NP:k % NP + 1]).then_inc(s["rden"], 1)

            dve.wait_ge(s["wqk_in"], 32)
            for n, (kind, part) in enumerate(FIRST):
                lo(0, STEPS, kind, part, n, n % 2, 0)

            def body(it, first, last):
                for k, chunks in steps(it, first, last):
                    u = it * ITER + k
                    if not last:
                        dve.wait_ge(s["sc"], u + 1)
                        if k % QT == 0:
                            dve.tensor_scalar(sc[0:1, k % 2, S - 1:S], sc[0:1, k % 2, S - 1:S], MASK, None,
                                              ALU.add).then_inc(s["masked"], 1)
                            dve.wait_ge(s["masked"], it * (ITER // QT) + k // QT + 1)
                        dve.tensor_reduce(nmax[:, k % NP:k % NP + 1], sc[:, k % 2], AX.X, ALU.max,
                                          negate=True).then_inc(s["negmax"], 1)
                    if (k == 0 and not first) or (k > 0 and not last):
                        recip(u - 1, (k - 1) % ITER)
                    v = finished_at(k, first)
                    if v:
                        r = rows_of_head(v[1])
                        n = it * 8 + v[2]
                        g = (2 * it + v[2] // 4) % PAIRS
                        if v[2] % 4 == 0 and not (first and v[2] == 0):
                            dve.wait_ge(s["att_out"], it * 32 + (v[2] // 4) * 16)
                        dve.wait_ge(s["halved"], n + 1)
                        dve.scalar_tensor_tensor(
                            out=ao[r, v[2] % 2], in0=ov[r, v[2] % 2],
                            scalar=bsb[r, g, 2:3] if isinstance(g, int) else bsb[r, bass.ds(g, 1), 2],
                            in1=half[r], op0=ALU.add, op1=ALU.add).then_inc(s["att"], 1)
                    for kind, part, n, bank in chunks:
                        lo(it, k, kind, part, n, bank, None)
            over_iterations(dve, body)

        @block_.tensor
        def _(pe):
            PARTS = ((0, 0), (0, 1), (1, 0))
            pe.wait_ge(s["const"], 32)

            def project(kind, part, n, bank):
                if kind in "QK":
                    i = 0
                    for c in range(DC):
                        for a, b in PARTS:
                            o = pe.matmul(ring[:, bank], wqk_s[:, "QK".index(kind), c, a], z_s[:, c * 2 + b, part],
                                          start=(i == 0), stop=(i == 5))
                            i += 1
                else:
                    for t in range(2):
                        col = ((2 * part + t) % NT) * P
                        i = 0
                        for c in range(DC):
                            for a, b in PARTS:
                                o = pe.matmul(ring[:, bank, t * 2 * P:(t + 1) * 2 * P],
                                              z_s[:, c * 2 + a, part // 2, col:col + P], wv_s[:, c, b],
                                              start=(i == 0), stop=(i == 5))
                                i += 1
                o.then_inc(s["chunk"], 1)

            pe.wait_ge(s["z_in"], 16)
            pe.wait_ge(s["wqk_in"], 32)
            pe.wait_ge(s["wv_in"], 16)
            for n, (kind, part) in enumerate(FIRST):
                if n >= 2:
                    pe.wait_ge(s["lo"], n - 1)
                project(kind, part, n, n % 2)

            def body(it, first, last):
                for k, chunks in steps(it, first, last):
                    u = it * ITER + k
                    slot, head, tile = k // STEPS, (k // QT) % 2, k % QT
                    if not last:
                        if k % STEPS == 0:
                            pe.wait_ge(s["k_dup"], it * 64 + slot * 32 + 32)
                        if not (first and k < 2):
                            pe.wait_ge(s["exp"], u - 1)
                        for kb in range(S // BT):
                            for a in range(2):
                                o = pe.matmul(sc[:, k % 2, kb * BT:(kb + 1) * BT],
                                              q_s[:, slot, head, tile * P:(tile + 1) * P],
                                              k_s[:, slot, head, a, kb * BT:(kb + 1) * BT],
                                              start=(a == 0), stop=(a == 1))
                        o.then_inc(s["sc"], 1)
                    for kind, part, n, bank in chunks:
                        if kind != "T":
                            continue
                        if part == 0:
                            pe.wait_ge(s["normed"], u - LAG + 1)
                        pe.wait_ge(s["lo"], n - 1)
                        for j in range(4):
                            o = pe.transpose(ring[:, bank, j * P:(j + 1) * P],
                                             pr[:, (k - LAG) % NP, (4 * part + j) * P:(4 * part + j + 1) * P], ident[:])
                        o.then_inc(s["chunk"], 1)
                    v = values_at(k, first)
                    if v and not (last and v[2] >= 0):
                        vslot, vhead, blk, q = v
                        if q == 0:
                            pe.wait_ge(s["lo"], number(it, (k - 1) % ITER, 2) - (PER if k == 0 else 0))
                            if vslot == 1 and blk % 4 == 0:
                                pe.wait_ge(s["v_in"], it * 16 + 16)
                            if not (first and blk < 2):
                                pe.wait_ge(s["att"], it * 8 + blk - 1)
                        for kt in (2 * q, 2 * q + 1):
                            for a in range(2):
                                o = pe.matmul(ov[:, blk % 2], v_s[:, vslot, kt, 2 * vhead:2 * vhead + 2]
                                              .rearrange("p k f -> p (k f)"), pT[:, blk % 2, a, kt],
                                              start=(kt == 0 and a == 0), stop=(kt == QT - 1 and a == 1))
                        if q == 3:
                            o.then_inc(s["pv"], 1)
                    for kind, part, n, bank in chunks:
                        if kind == "T":
                            continue
                        if kind == "Q" and part == 0:
                            pe.wait_ge(s["wqk_in"], it * 64 + (k // STEPS) * 32 + 64)
                            if k >= STEPS:
                                pe.wait_ge(s["z_in"], it * 16 + 32)
                        if kind == "V" and part == 0:
                            pe.wait_ge(s["wv_in"], it * 16 + 32)
                        pe.wait_ge(s["lo"], n - 1)
                        project(kind, part, n, bank)
            over_iterations(pe, body)


def mlp_phase(nc, tag, w, att, z, x1, x2):
    PAIRS = AHD // P
    HP = PAIRS // 2
    HC = MH // P
    PARTS = ((0, 0), (0, 1), (1, 0))
    with ExitStack() as ctx:
        m = Bank(nc, ctx, tag)
        ident = m.sb("ident", [P, P])
        wo_in = m.sb("wo_in", [P, PAIRS, D])
        wo = m.sb("wo", [P, 2, PAIRS, D], F32R)
        w1_in = m.sb("w1_in", [P, DC, MH])
        w1 = m.sb("w1", [P, 2, DC, MH], F32R)
        w2_in = m.sb("w2_in", [P, HC, D])
        w2 = m.sb("w2", [P, 2, HC, D], F32R)
        ln = m.sb("ln", [P, DC, 2])
        b1_in = m.sb("b1_in", [P, HC])
        b1 = m.sb("b1", [P, HC])
        bo = m.sb("bo", [P, D])
        b2 = m.sb("b2", [P, D])
        mhalf = m.sb("mhalf", [P, NT])

        att_in = m.sb("att_in", [P, 2, HP, BT])
        att_s = m.sb("att_s", [P, 2, 2, PAIRS, BT], F32R)
        zin = m.sb("zin", [P, 2, NT, D])
        xin = m.sb("xin", [P, 2, NT, D])
        h = m.sb("h", [P, NT, D])
        st6 = m.sb("st6", [P, NT, 6])
        mv = m.sb("mv", [P, NT, 2])
        rs = m.sb("rs", [P, NT])
        hn = m.sb("hn", [P, NT, D])
        hT = m.sb("hT", [P, DC, 2, BT], F32R)
        act_out = m.sb("act_out", [P, HC, BT])
        hid_s = m.sb("hid_s", [P, HC, 2, BT], F32R)
        res = m.sb("res", [P, NT, D])
        proj = m.ps("proj", [P, NT, D])
        hT_ps = m.ps("hT_ps", [P, DC, BT])
        hid = m.ps("hid", [P, 2, BT])
        acc = m.ps("acc", [P, NT, D])

        s = {n: m.sem(n) for n in (
            "w_in mhalf w1_scaled w_hi w_ready b1_ps att_in0 att_in1 att_hi att_lo z_in x_in zb x_b proj h bn stats "
            "veps rstd hn hT_ps hT_hi hT_lo hid gelu hid_hi hid_lo acc x_h res res_out").split()}
        dve_turns, pool_turns = m.sem("dve_turns"), m.sem("pool_turns")
        NW = 8
        block = ctx.enter_context(nc.Block())

        def over_steps(eng, body):
            body(0, 0)
            with eng.Fori(0, (NB - 4) // 2) as it:
                body(it * 2 + 1, 1)
                body(it * 2 + 2, 0)
            for i in range(NB - 3, NB + 1):
                body(i, i % 2)

        def has(i, ahead=0):
            return not isinstance(i, int) or 0 <= i + ahead < NB

        @block.sync
        def _(sp):
            def fixed(i):
                return i if isinstance(i, int) else sp.snap(i)

            def rows_of(ap, i):
                return ap.rearrange("(n t p) d -> n p t d", t=NT, p=P)[bass.ds(i, 1)].rearrange("n p t d -> p (n t) d")

            def load_att(token, half):
                from_ = att[half * HP:(half + 1) * HP, :, bass.ds(token, BT)].rearrange("g p t -> p g t")
                sp.dma_start(att_in[:, half], from_).then_inc(s["att_in%d" % half], 16)

            load_att(0, 0)
            load_att(0, 1)
            sp.dma_start(wo_in[:], w["wo"]).then_inc(s["w_in"], 16)
            sp.dma_start(ln[:], w["ln_m"]).then_inc(s["w_in"], 16)
            sp.dma_start(bo[:], w["bo"].partition_broadcast(P)).then_inc(s["w_in"], 16)
            sp.dma_start(b2[:], w["b2m"].partition_broadcast(P)).then_inc(s["w_in"], 16)
            sp.dma_start(b1_in[:], w["b1m"]).then_inc(s["w_in"], 16)
            sp.dma_start(ident[:], w["ident"]).then_inc(s["w_in"], 16)
            sp.dma_start(w1_in[:], w["w1m"]).then_inc(s["w_in"], 16)
            sp.dma_start(w2_in[:], w["w2m"]).then_inc(s["w_in"], 16)
            sp.dma_start(zin[:, 0], rows_of(z, 0)).then_inc(s["z_in"], 16)
            sp.dma_start(xin[:, 0], rows_of(x1, 0)).then_inc(s["x_in"], 16)
            for half in range(2):
                sp.wait_ge(s["att_lo"], half + 1)
                load_att(BT, half)
            for half in range(2):
                sp.wait_ge(s["att_lo"], 2 + half + 1)
                load_att(2 * BT, half)

            def body(i, par):
                if has(i, 3):
                    ahead = fixed((i + 3) * BT)
                if has(i, -1):
                    to = rows_of(x2, fixed(i - 1))
                if has(i, 1):
                    z_from, x_from = rows_of(z, fixed(i + 1)), rows_of(x1, fixed(i + 1))
                    sp.wait_ge(s["h"], i + 1)
                    sp.dma_start(zin[:, 1 - par], z_from).then_inc(s["z_in"], 16)
                if has(i, 3):
                    for half in range(2):
                        sp.wait_ge(s["att_lo"], (i + 2) * 2 + half + 1)
                        load_att(ahead, half)
                if has(i, -1):
                    sp.wait_ge(s["res"], i)
                    sp.dma_start(to, res[:]).then_inc(s["res_out"], 16)
                if has(i, 1):
                    sp.wait_ge(s["x_b"], i + 1)
                    sp.dma_start(xin[:, 1 - par], x_from).then_inc(s["x_in"], 16)
            over_steps(sp, body)
            sp.wait_ge(s["res_out"], NB * 16 + 16)

        @block.scalar
        def _(act):
            act.preload_act_table(ACT.Gelu_apprx_tanh)

            def att_hi(i, par, half):
                act.wait_ge(s["att_in%d" % half], i * 16 + 16)
                if has(i, -2):
                    act.wait_ge(s["proj"], i - 1)
                act.activation(att_s[:, par, 0, half * HP:(half + 1) * HP], att_in[:, half],
                               ACT.Identity).then_inc(s["att_hi"], 1)

            def gelu(i, hc):
                act.wait_ge(s["hid"], i * HC + hc + 1)
                act.activation(act_out[:, hc], hid[:, hc % 2], ACT.Gelu_apprx_tanh,
                               bias=b1[:, hc:hc + 1]).then_inc(s["gelu"], 1)

            def hid_hi(i, hc):
                act.wait_ge(s["gelu"], i * HC + hc + 1)
                if has(i, -1):
                    act.wait_ge(s["acc"], i)
                act.activation(hid_s[:, hc, 0], act_out[:, hc], ACT.Identity).then_inc(s["hid_hi"], 1)

            def hT_hi(i):
                for c in range(DC):
                    act.wait_ge(s["hT_ps"], i * DC + c + 1)
                    if c == 0 and has(i, -1):
                        act.wait_ge(s["hid"], i * HC)
                    act.activation(hT[:, c, 0], hT_ps[:, c], ACT.Identity).then_inc(s["hT_hi"], 1)

            act.wait_ge(s["att_in0"], 16)
            act.activation(att_s[:, 0, 0, 0:HP], att_in[:, 0], ACT.Identity).then_inc(s["att_hi"], 1)
            act.wait_ge(s["att_in1"], 16)
            act.activation(att_s[:, 0, 0, HP:PAIRS], att_in[:, 1], ACT.Identity).then_inc(s["att_hi"], 1)
            act.wait_ge(s["w_in"], 16 * NW)
            act.activation(wo[:, 0], wo_in[:], ACT.Identity).then_inc(s["w_hi"], 1)
            act.activation(w2[:, 0], w2_in[:], ACT.Identity).then_inc(s["w_hi"], 1)
            act.wait_ge(s["w1_scaled"], 1)
            act.activation(w1[:, 0], w1_in[:], ACT.Identity).then_inc(s["w_hi"], 1)
            for half in range(2):
                att_hi(1, 1, half)
            act.wait_ge(s["w_ready"], 3)

            def body(i, par):
                if has(i, -1):
                    gelu(i - 1, 0)
                    for hc in range(1, HC):
                        gelu(i - 1, hc)
                        hid_hi(i - 1, hc - 1)
                    hid_hi(i - 1, HC - 1)
                if has(i, 2):
                    att_hi(i + 2, par, 0)
                if has(i):
                    hT_hi(i)
                if has(i, 2):
                    att_hi(i + 2, par, 1)
            over_steps(act, body)

        @block.gpsimd
        def _(pool):
            pool.memset(mhalf[:], -0.5).then_inc(s["mhalf"], 1)
            pool.wait_ge(s["mhalf"], 1)
            pool.wait_ge(s["w_in"], 16 * NW)

            def add_rows(x, row):
                for t in range(NT):
                    o = pool.tensor_tensor(x[:, t], x[:, t], row[:], ALU.add)
                return o

            def z_bias(i, par):
                pool.wait_ge(s["z_in"], i * 16 + 16)
                add_rows(zin[:, par], bo).then_inc(s["zb"], 1)

            def x_bias(i, par):
                pool.wait_ge(s["x_in"], i * 16 + 16)
                add_rows(xin[:, par], b2).then_inc(s["x_b"], 1)
            z_bias(0, 0)

            def body(i, par):
                if has(i):
                    x_bias(i, par)
                    pool.wait_ge(s["stats"], i + 1)
                    stand_alone(pool, pool_turns)
                    pool.tensor_scalar(rs[:], mv[:, :, 1], EPS, None, ALU.add).then_inc(s["veps"], 1)
                    pool.wait_ge(s["veps"], i + 1)
                    pool.tensor_tensor(rs[:], rs[:], mhalf[:], ALU.pow).then_inc(s["rstd"], 1)
                    pool.wait_ge(s["x_b"], i + 1)
                    pool.tensor_tensor(xin[:, par], xin[:, par], h[:], ALU.add).then_inc(s["x_h"], 1)
                if has(i, 1):
                    z_bias(i + 1, 1 - par)
            over_steps(pool, body)

        @block.vector
        def _(dve):
            def att_lo(i, par, half):
                dve.wait_ge(s["att_hi"], i * 2 + half + 1)
                g = slice(half * HP, (half + 1) * HP)
                dve.tensor_tensor(att_s[:, par, 1, g], att_in[:, half], att_s[:, par, 0, g].bitcast(F32),
                                  ALU.subtract).then_inc(s["att_lo"], 1)

            def hid_lo(i, hc):
                dve.wait_ge(s["hid_hi"], i * HC + hc + 1)
                dve.tensor_tensor(hid_s[:, hc, 1], act_out[:, hc], hid_s[:, hc, 0].bitcast(F32),
                                  ALU.subtract).then_inc(s["hid_lo"], 1)

            dve.sem_inc(s["res_out"], 16)
            att_lo(0, 0, 0)
            att_lo(0, 0, 1)
            dve.wait_ge(s["w_in"], 16 * NW)
            dve.wait_ge(s["w_hi"], 1)
            dve.tensor_tensor(wo[:, 1], wo_in[:], wo[:, 0].bitcast(F32), ALU.subtract).then_inc(s["w_ready"], 1)
            dve.wait_ge(s["b1_ps"], 1)
            dve.tensor_tensor(b1[:], hid[:, 0, 0:HC], b1_in[:], ALU.add)
            for c in range(DC):
                o = dve.tensor_scalar(w1_in[:, c], w1_in[:, c], ln[:, c, 0:1], None, ALU.mult)
            o.then_inc(s["w1_scaled"], 1)
            dve.wait_ge(s["w_hi"], 2)
            dve.tensor_tensor(w2[:, 1], w2_in[:], w2[:, 0].bitcast(F32), ALU.subtract).then_inc(s["w_ready"], 1)
            dve.wait_ge(s["w_hi"], 3)
            dve.tensor_tensor(w1[:, 1], w1_in[:], w1[:, 0].bitcast(F32), ALU.subtract).then_inc(s["w_ready"], 1)
            for half in range(2):
                att_lo(1, 1, half)

            def body(i, par):
                if has(i):
                    dve.wait_ge(s["proj"], i + 1)
                    dve.wait_ge(s["zb"], i + 1)
                    if has(i, -1):
                        dve.wait_ge(s["x_h"], i)
                    dve.tensor_tensor(h[:], proj[:], zin[:, par], ALU.add).then_inc(s["h"], 1)
                    dve.wait_ge(s["h"], i + 1)
                    for t in range(NT):
                        o = dve.bn_stats(st6[:, t], h[:, t])
                    o.then_inc(s["bn"], 1)
                    dve.wait_ge(s["bn"], i + 1)
                    stand_alone(dve, dve_turns)
                    for t in range(NT):
                        o = dve.bn_aggr(mv[:, t], st6[:, t])
                    o.then_inc(s["stats"], 1)
                if has(i, -1):
                    hid_lo(i - 1, 0)
                    hid_lo(i - 1, 1)
                if has(i):
                    dve.wait_ge(s["rstd"], i + 1)
                    if has(i, -1):
                        dve.wait_ge(s["hT_ps"], i * DC)
                    for t in range(NT):
                        o = dve.tensor_scalar(hn[:, t], h[:, t], mv[:, t, 0:1], rs[:, t:t + 1],
                                              ALU.subtract, ALU.mult)
                    o.then_inc(s["hn"], 1)
                if has(i, -1):
                    hid_lo(i - 1, 2)
                    hid_lo(i - 1, 3)
                if has(i, 2):
                    att_lo(i + 2, par, 0)
                if has(i):
                    for c in range(DC):
                        dve.wait_ge(s["hT_hi"], i * DC + c + 1)
                        dve.tensor_tensor(hT[:, c, 1], hT_ps[:, c], hT[:, c, 0].bitcast(F32),
                                          ALU.subtract).then_inc(s["hT_lo"], 1)
                if has(i, 2):
                    att_lo(i + 2, par, 1)
                if has(i, -1):
                    dve.wait_ge(s["acc"], i)
                    dve.wait_ge(s["x_h"], i)
                    dve.wait_ge(s["res_out"], i * 16)
                    dve.tensor_tensor(res[:], acc[:], xin[:, 1 - par], ALU.add).then_inc(s["res"], 1)
            over_steps(dve, body)

        @block.tensor
        def _(pe):
            def project(i, par, tiles):
                for t in tiles:
                    for g in range(PAIRS):
                        for a, b in PARTS:
                            o = pe.matmul(proj[:, t], att_s[:, par, a, g, t * P:(t + 1) * P], wo[:, b, g],
                                          start=(t % 2 == 0 and g == 0 and (a, b) == (0, 0)),
                                          stop=(g == PAIRS - 1 and (a, b) == PARTS[-1]), skip_group_check=True)
                return o

            pe.wait_ge(s["w_in"], 16 * NW)
            for hc in range(HC):
                for c in range(DC):
                    o = pe.matmul(hid[:, 0, hc:hc + 1], w1_in[:, c, hc * P:(hc + 1) * P], ln[:, c, 1:2],
                                  start=(c == 0), stop=(c == DC - 1))
            o.then_inc(s["b1_ps"], 1)
            pe.wait_ge(s["att_lo"], 2)
            pe.wait_ge(s["w_ready"], 1)
            project(0, 0, range(NT)).then_inc(s["proj"], 1)
            pe.wait_ge(s["w_ready"], 3)

            def body(i, par):
                if has(i, 1):
                    pe.wait_ge(s["att_lo"], (i + 1) * 2 + 2)
                    pe.wait_ge(s["h"], i + 1)
                    project(i + 1, 1 - par, (0, 1))
                if has(i):
                    pe.wait_ge(s["hn"], i + 1)
                    if has(i, -1):
                        pe.wait_ge(s["hT_lo"], i * DC)
                    for c in range(DC):
                        for t in range(NT):
                            o = pe.transpose(hT_ps[:, c, t * P:(t + 1) * P], hn[:, t, c * P:(c + 1) * P], ident[:])
                        o.then_inc(s["hT_ps"], 1)
                if has(i, -1):
                    pe.wait_ge(s["hid_lo"], i * HC)
                    if not has(i):
                        pe.wait_ge(s["res"], i - 1)
                    for t in range(NT):
                        for hc in range(HC):
                            for a, b in PARTS:
                                o = pe.matmul(acc[:, t], hid_s[:, hc, a, t * P:(t + 1) * P], w2[:, b, hc],
                                              start=(t % 2 == 0 and hc == 0 and (a, b) == (0, 0)),
                                              stop=(hc == HC - 1 and (a, b) == PARTS[-1]), skip_group_check=True)
                    o.then_inc(s["acc"], 1)
                if has(i, 1):
                    project(i + 1, 1 - par, (2, 3)).then_inc(s["proj"], 1)
                if has(i):
                    pe.wait_ge(s["hT_lo"], i * DC + DC)
                    for hc in range(HC):
                        if hc >= 2 or has(i, -1):
                            pe.wait_ge(s["gelu"], i * HC + hc - 1)
                        n = 0
                        for c in range(DC):
                            for a, b in PARTS:
                                o = pe.matmul(hid[:, hc % 2], w1[:, a, c, hc * P:(hc + 1) * P], hT[:, c, b],
                                              start=(n == 0), stop=(n == 5))
                                n += 1
                        o.then_inc(s["hid"], 1)
            over_steps(pe, body)


def kernel(**inputs):
    import numpy as _np
    import concourse.bacc as _bacc
    from concourse import mybir as _mybir
    from concourse.bass_utils import run_bass_kernel_spmd as _run

    nc = _bacc.Bacc("TRN2", target_bir_lowering=False, num_devices=1)
    arrays, w = {}, {}

    def give(name, a):
        a = _np.ascontiguousarray(a)
        arrays[f"in_{name}"] = a
        w[name] = nc.dram_tensor(f"in_{name}", a.shape, _mybir.dt.from_np(a.dtype), kind="ExternalInput").ap()

    def scratch(name, shape, dt=F32):
        return nc.dram_tensor(name, shape, dt, kind="Internal").ap()

    i = {k: _np.asarray(v) for k, v in inputs.items()}
    rows_in = lambda a: a.reshape(a.shape[0] // P, P, -1).transpose(1, 0, 2).reshape(P, -1)
    give("x", i["L0_attn_x"].reshape(TOK, D))
    w1 = _np.concatenate([i["L0_ffn_W1"], i["L0_ffn_Ws1"][None]]).transpose(1, 0, 2).reshape(D, NE * HID)
    give("w1", rows_in(w1))
    give("w2", _np.concatenate([i["L0_ffn_W2"], i["L0_ffn_Ws2"][None]]).transpose(1, 0, 2).reshape(HID, NE * D))
    give("b1", _np.concatenate([i["L0_ffn_b1"], i["L0_ffn_bs1"][None]]).T)
    give("b2", _np.concatenate([i["L0_ffn_b2"], i["L0_ffn_bs2"][None]]))
    give("gw", rows_in(i["L0_ffn_gate_W"]))
    give("rscale", i["L0_ffn_route_scale"].reshape(1, 1))
    give("ident", _np.eye(P, dtype=_np.float32))
    give("iota", _np.tile(_np.arange(E, dtype=_np.float32), (P, 1)))
    sel = _np.zeros((P, E, P), _np.float32)
    for e in range(E):
        sel[e, e] = sel[E + e, e] = 1.0
    give("sel", sel.reshape(P, E * P))
    rows = _np.zeros((P, 2), _np.float32)
    rows[[*range(2 * E), 3 * E], 0] = 1.0
    rows[[*range(2 * E, 3 * E), 3 * E + 1], 1] = 1.0
    give("rows", rows)
    give("w_qkv", _np.stack([rows_in(i[f"L0_attn_W{c}"]).reshape(P, DC, AHD) for c in "qkv"]))
    give("ln_qkv", _np.stack([_np.stack([rows_in(i[f"L0_attn_ln{c}_{x}"][:, None]) for x in "sb"], -1) for c in "qkv"], 1))
    give("c_qkv", _np.stack([rows_in(i[f"L0_attn_b{c}"][:, None]) for c in "qkv"], 1))
    give("wo", rows_in(i["L0_attn_Wo"]).reshape(P, AHD // P, D))
    give("w1m", rows_in(i["L0_attn_W1"]).reshape(P, DC, MH))
    give("w2m", rows_in(i["L0_attn_W2"]).reshape(P, MH // P, D))
    give("ln_m", _np.stack([rows_in(i[f"L0_attn_lnm_{x}"][:, None]) for x in "sb"], -1))
    give("b1m", rows_in(i["L0_attn_b1"][:, None]))
    give("bo", i["L0_attn_bo"][None])
    give("b2m", i["L0_attn_b2"][None])
    x1, z, x2 = (scratch(n, (TOK, D)) for n in ("x1", "z", "x2"))
    zT = scratch("zT", (NB, P, DC, 2, BT))
    wqk = scratch("wqk", (AHD // P, P, 2, DC, 2, P))
    wv = scratch("wv", (AHD // P // 2, P, DC, 2, 2 * P))
    bias = scratch("bias", (P, AHD // P, 3))
    att = scratch("att", (AHD // P, P, TOK))
    out = nc.dram_tensor("out", (TOK, D), F32, kind="ExternalOutput").ap()

    ffn_phase(nc, "f", w["x"], x1, w, {"z": z, "zT": zT})
    qkv_weights_phase(nc, "w", w, wqk, wv, bias)
    attention_phase(nc, "a", w, zT, wqk, wv, bias, att)
    mlp_phase(nc, "m", w, att, z, x1, x2)
    ffn_phase(nc, "g", x2, out, w, None)
    r = _run(nc, [arrays], core_ids=[0])
    return r.results[0]["out"].reshape(B, S, D)
```

```python
from contextlib import ExitStack

import numpy as np

import concourse.bass as bass
from concourse import mybir

F32 = mybir.dt.float32
F32R = mybir.dt.float32r
U32 = mybir.dt.uint32
ALU = mybir.AluOpType
ACT = mybir.ActivationFunctionType
AX = mybir.AxisListType

P = 128
B, S, D = 4, 1024, 256
TOK = B * S
H, HD = 16, 64
AHD = H * HD
E, HID = 8, 128
NE = E + 1
MH = 2 * D
DC = D // P
BT = 512
NT = BT // P
NB = TOK // BT
EPS = 1e-5
MASK = -999.0
TOP = 2
E_NUM = float(np.float32(np.e))


def stand_alone(eng, turns):
    eng.sem_inc(turns, 1)


class Bank:

    def __init__(self, nc, ctx, tag):
        self.nc, self.ctx, self.tag = nc, ctx, tag

    def sb(self, name, shape, dt=F32):
        return self.ctx.enter_context(self.nc.sbuf_tensor(f"{self.tag}_{name}", shape, dt))

    def ps(self, name, shape):
        return self.ctx.enter_context(self.nc.psum_tensor(f"{self.tag}_{name}", shape, F32))

    def sem(self, name):
        return self.ctx.enter_context(self.nc.semaphore(f"{self.tag}_{name}"))


def ffn_phase(nc, turns, tag, src, dst, w, tail):
    with ExitStack() as ctx:
        m = Bank(nc, ctx, tag)
        ident = m.sb("ident", [P, P])
        sel_in = m.sb("sel_in", [P, E * P])
        sel = m.sb("sel", [P, E * P], F32R)
        w1_in = m.sb("w1_in", [P, DC * NE * HID])
        w1p = m.sb("w1p", [P, 2, DC * NE * HID], F32R)
        w2_in = m.sb("w2_in", [P, NE * D])
        w2p = m.sb("w2p", [P, 2, NE * D], F32R)
        gw_in = m.sb("gw_in", [P, DC * E])
        gwp = m.sb("gwp", [P, DC, 2, E], F32R)
        b1 = m.sb("b1", [P, NE])
        b2_in = m.sb("b2_in", [P, D])
        b2hi = m.sb("b2hi", [P, D], F32R)
        b2lo = m.sb("b2lo", [P, D], F32R)
        b2s = m.sb("b2s", [P, D], F32R)
        rows = m.sb("rows", [P, 2])
        rsc = m.sb("rsc", [P, 1])
        iota = m.sb("iota", [P, E])
        mhalf = m.sb("mhalf", [P, NT])
        ebase = m.sb("ebase", [P, NT * E])

        xin = m.sb("xin", [P, 2, NT, D])
        xres = m.sb("xres", [P, NT, D])
        st6 = m.sb("st6", [P, NT, 6])
        mv = m.sb("mv", [P, NT, 2])
        rs = m.sb("rs", [P, NT])
        xn = m.sb("xn", [P, NT, D])
        xT = m.sb("xT", [P, 2, DC, 2, BT], F32R)
        gl = m.sb("gl", [P, NT, E])
        nl = m.sb("nl", [P, NT, E])
        sg = m.sb("sg", [P, NT, E])
        top = m.sb("top", [P, NT, 8])
        idx = m.sb("idx", [P, NT, 8], U32)
        idf = m.sb("idf", [P, NT, 8])
        wt = m.sb("wt", [P, NT, TOP])
        ws = m.sb("ws", [P, NT])
        ga = m.sb("ga", [P, NT, E])
        gb_ = m.sb("gb_", [P, NT, E])
        ghi = m.sb("ghi", [P, NT, E], F32R)
        gpad = m.sb("gpad", [P, NT, P])
        gst = m.sb("gst", [P, 2, BT], F32R)
        act_out = m.sb("act_out", [P, 3, BT])
        gated = m.sb("gated", [P, 3, BT])
        hp = m.sb("hp", [P, 3, 2, BT], F32R)
        res = m.sb("res", [P, NT, D])
        if tail:
            zst6 = m.sb("zst6", [P, NT, 6])
            zmv = m.sb("zmv", [P, NT, 2])
            zrs = m.sb("zrs", [P, NT])
            zz = m.sb("zz", [P, NT, D])
            zn = m.sb("zn", [P, NT, D])
            zT = m.sb("zT", [P, DC, 2, BT], F32R)

        hid = m.ps("hid", [P, 2, BT])
        gbc = m.ps("gbc", [P, 2, BT])
        acc = m.ps("acc", [P, NT, D])
        aux = m.ps("aux", [P, 2, BT])

        names = ("veps w_in zeroed w_hi w_ready x_in xres bn stats rstd xn xT_ps xT_hi xT_lo logits neg expneg "
                 "gate gpad gT_ps gst hid gelu gbc gated h_hi h_lo out res res_out")
        if tail:
            names += " z_veps z_bn z_stats z_rstd z zn zT_ps zT_hi zT_lo zT_out z_out"
        s = {n: m.sem(n) for n in names.split()}
        NW = 14
        GC = 12

        def shared(e):
            return e == E

        block = ctx.enter_context(nc.Block())

        def over_blocks(eng, body):
            body(0, 0, True, False)
            with eng.Fori(0, (NB - 2) // 2) as it:
                body(it * 2 + 1, 1, False, False)
                body(it * 2 + 2, 0, False, False)
            body(NB - 1, 1, False, True)

        def rows_of(ap, i):
            return ap.rearrange("(n t p) d -> n p t d", t=NT, p=P)[bass.ds(i, 1)].rearrange("n p t d -> p (n t) d")

        @block.sync
        def _(sp):
            sp.dma_start(ident[:], w["ident"]).then_inc(s["w_in"], 16)
            sp.dma_start(gw_in[:], w["gw"]).then_inc(s["w_in"], 16)
            sp.dma_start(xin[:, 0], rows_of(src, 0)).then_inc(s["x_in"], 16)
            sp.dma_start(w1_in[:], w["w1"]).then_inc(s["w_in"], 16)
            sp.dma_start(sel_in[:], w["sel"]).then_inc(s["w_in"], 16)
            sp.dma_start(b1[:], w["b1"]).then_inc(s["w_in"], 16)
            sp.dma_start(rows[:], w["rows"]).then_inc(s["w_in"], 16)
            sp.dma_start(iota[:], w["iota"]).then_inc(s["w_in"], 16)
            sp.dma_start(rsc[:], w["rscale"].partition_broadcast(P)).then_inc(s["w_in"], 16)
            sp.wait_ge(s["zeroed"], 1)
            for k in range(3):
                sp.dma_start(b2_in[k * E:(k + 1) * E], w["b2"][0:E]).then_inc(s["w_in"], 16)
            for k in range(2):
                sp.dma_start(b2_in[3 * E + k:3 * E + k + 1], w["b2"][E:NE]).then_inc(s["w_in"], 16)
            sp.dma_start(w2_in[:], w["w2"]).then_inc(s["w_in"], 16)

            def store(i):
                to = rows_of(dst, sp.snap(i) if i is not NB - 1 else i)
                if tail:
                    z_to = rows_of(tail["z"], sp.snap(i) if i is not NB - 1 else i)
                    zT_to = tail["zT"][bass.ds(sp.snap(i) if i is not NB - 1 else i, 1)].rearrange(
                        "n p c k t -> p (n c k) t")
                sp.wait_ge(s["res"], i + 1)
                sp.dma_start(to, res[:]).then_inc(s["res_out"], 16)
                if tail:
                    sp.wait_ge(s["z"], i + 1)
                    sp.dma_start(z_to, zz[:]).then_inc(s["z_out"], 16)
                    sp.wait_ge(s["zT_lo"], i * DC + DC)
                    sp.dma_start(zT_to, zT[:].bitcast(F32).rearrange("p c k t -> p (c k) t")).then_inc(s["zT_out"], 16)

            def body(i, par, first, last):
                if not last:
                    ahead = rows_of(src, 1 if first else sp.snap(i + 1))
                    sp.wait_ge(s["xn"], i + 1)
                    sp.dma_start(xin[:, 1 - par], ahead).then_inc(s["x_in"], 16)
                again = rows_of(src, i if first or last else sp.snap(i))
                if not first:
                    sp.wait_ge(s["res"], i)
                sp.dma_start(xres[:], again).then_inc(s["xres"], 16)
                if not first:
                    store(i - 1)
            over_blocks(sp, body)
            store(NB - 1)
            sp.wait_ge(s["res_out"], NB * 16 + 16)
            if tail:
                sp.wait_ge(s["z_out"], NB * 16 + 16)
                sp.wait_ge(s["zT_out"], NB * 16 + 16)

        @block.scalar
        def _(act):
            if tail:
                act.sem_inc(s["zT_out"], 16)
            act.preload_act_table(ACT.Gelu)
            act.wait_ge(s["w_in"], 16 * NW)
            act.activation(gwp[:, :, 0, :], gw_in[:].rearrange("p (c e) -> p c e", c=DC), ACT.Identity)
            act.activation(w1p[:, 0], w1_in[:], ACT.Identity)
            act.activation(w2p[:, 0], w2_in[:], ACT.Identity)
            act.activation(sel[:], sel_in[:], ACT.Identity)
            act.activation(b2hi[:], b2_in[:], ACT.Identity).then_inc(s["w_hi"], 1)

            def xt_hi(i, par):
                for c in range(DC):
                    act.wait_ge(s["xT_ps"], i * DC + c + 1)
                    act.activation(xT[:, par, c, 0], aux[:, c], ACT.Identity).then_inc(s["xT_hi"], 1)

            def zt_hi(i):
                for c in range(DC):
                    act.wait_ge(s["zT_ps"], i * DC + c + 1)
                    if c == 0:
                        act.wait_ge(s["zT_out"], i * 16 + 16)
                    act.activation(zT[:, c, 0], aux[:, c], ACT.Identity).then_inc(s["zT_hi"], 1)

            def hi(i, e, first):
                if e >= 3 or not first:
                    act.wait_ge(s["out"], i * NE + e - 2)
                if shared(e):
                    act.wait_ge(s["gelu"], i * NE + e + 1)
                    from_ = act_out
                else:
                    act.wait_ge(s["gated"], i * E + e + 1)
                    from_ = gated
                act.activation(hp[:, e % 3, 0], from_[:, e % 3], ACT.Identity).then_inc(s["h_hi"], 1)

            def body(i, par, first, last):
                for e in range(NE):
                    act.wait_ge(s["hid"], i * NE + e + 1)
                    if e >= 3 or not first:
                        act.wait_ge(s["h_lo"], i * NE + e - 2)
                    act.activation(act_out[:, e % 3], hid[:, (par + e) % 2], ACT.Gelu,
                                   bias=b1[:, e:e + 1]).then_inc(s["gelu"], 1)
                    if e > 0:
                        hi(i, e - 1, first)
                    elif not first:
                        hi(i - 1, E, False)
                    if e == 3 and not last:
                        xt_hi(i + 1, 1 - par)
                    if e == 5 and tail and not first:
                        zt_hi(i - 1)
            xt_hi(0, 0)
            over_blocks(act, body)
            hi(NB - 1, E, False)
            if tail:
                zt_hi(NB - 1)

        @block.gpsimd
        def _(pool):
            pool.memset(b2_in[:], 0.0).then_inc(s["zeroed"], 1)
            pool.memset(gpad[:], 0.0).then_inc(s["zeroed"], 1)
            pool.wait_ge(s["zeroed"], 2)
            pool.memset(gpad[:, :, 3 * E:3 * E + 2], 1.0)
            pool.memset(mhalf[:], -0.5)
            pool.memset(ebase[:], E_NUM).then_inc(s["zeroed"], 1)
            pool.wait_ge(s["zeroed"], 3)


            def x_rstd(i):
                pool.wait_ge(s["stats"], i + 1)
                stand_alone(pool, turns)
                pool.tensor_scalar(rs[:], mv[:, :, 1], EPS, None, ALU.add).then_inc(s["veps"], 1)
                pool.wait_ge(s["veps"], i + 1)
                pool.tensor_tensor(rs[:], rs[:], mhalf[:], ALU.pow).then_inc(s["rstd"], 1)

            def expneg(i):
                pool.wait_ge(s["neg"], i + 1)
                pool.tensor_tensor(nl[:].rearrange("p t e -> p (t e)"), ebase[:],
                                   nl[:].rearrange("p t e -> p (t e)"), ALU.pow).then_inc(s["expneg"], 1)

            def z_rstds(i, which):
                pool.wait_ge(s["z_stats"], i * 2 + which + 1)
                stand_alone(pool, turns)
                pool.tensor_scalar(zrs[:], zmv[:, :, 1], EPS, None, ALU.add).then_inc(s["z_veps"], 1)
                pool.wait_ge(s["z_veps"], i * 2 + which + 1)
                pool.tensor_tensor(zrs[:], zrs[:], mhalf[:], ALU.pow).then_inc(s["z_rstd"], 1)

            def body(i, par, first, last):
                if tail and not first:
                    z_rstds(i - 1, 0)
                if not last:
                    x_rstd(i + 1)
                if tail and not first:
                    z_rstds(i - 1, 1)
                if not last:
                    expneg(i + 1)
            x_rstd(0)
            expneg(0)
            over_blocks(pool, body)
            if tail:
                z_rstds(NB - 1, 0)
                z_rstds(NB - 1, 1)

        @block.vector
        def _(dve):
            def norm_stats(x, t6, out, bn, stats, nbn):
                for t in range(NT):
                    o = dve.bn_stats(t6[:, t], x[:, t])
                o.then_inc(bn, 1)
                dve.wait_ge(bn, nbn)
                stand_alone(dve, turns)
                for t in range(NT):
                    o = dve.bn_aggr(out[:, t], t6[:, t])
                o.then_inc(stats, 1)

            def x_stats(i, par):
                dve.wait_ge(s["x_in"], i * 16 + 16)
                norm_stats(xin[:, par], st6, mv, s["bn"], s["stats"], i + 1)

            def x_norm(i, par, first):
                dve.wait_ge(s["rstd"], i + 1)
                if not first:
                    dve.wait_ge(s["xT_ps"], i * DC)
                for t in range(NT):
                    o = dve.tensor_scalar(xn[:, t], xin[:, par, t], mv[:, t, 0:1], rs[:, t:t + 1],
                                          ALU.subtract, ALU.mult)
                o.then_inc(s["xn"], 1)

            def xt_lo(i, par):
                for c in range(DC):
                    dve.wait_ge(s["xT_hi"], i * DC + c + 1)
                    dve.tensor_tensor(xT[:, par, c, 1], aux[:, c], xT[:, par, c, 0].bitcast(F32),
                                      ALU.subtract).then_inc(s["xT_lo"], 1)

            def neg_logits(i):
                ps = aux[:, 0, 0:NT * 2 * E].rearrange("p (t k e) -> p t k e", t=NT, k=2)
                dve.wait_ge(s["logits"], i + 1)
                dve.tensor_scalar(gl[:], ps[:, :, 1], -1.0, None, ALU.mult).then_inc(s["gate"], 1)
                dve.wait_ge(s["gate"], i * GC + 1)
                dve.scalar_tensor_tensor(out=nl[:], in0=ps[:, :, 0], scalar=-1.0, in1=gl[:],
                                         op0=ALU.mult, op1=ALU.add).then_inc(s["neg"], 1)

            def gates(i):
                n = [i * GC + 1]

                def link(o):
                    o.then_inc(s["gate"], 1)
                    n[0] = n[0] + 1
                    dve.wait_ge(s["gate"], n[0])
                dve.wait_ge(s["expneg"], i + 1)
                link(dve.tensor_scalar(sg[:], nl[:], 1.0, None, ALU.add))
                link(dve.reciprocal(sg[:], sg[:]))
                link(dve.tensor_scalar(sg[:], sg[:], rsc[:, 0:1], None, ALU.mult))
                stand_alone(dve, turns)
                for t in range(NT):
                    o = dve.max(top[:, t], sg[:, t])
                link(o)
                stand_alone(dve, turns)
                for t in range(NT):
                    o = dve.max_index(idx[:, t], top[:, t], sg[:, t])
                link(o)
                dve.tensor_tensor(ws[:], top[:, :, 0], top[:, :, 1], ALU.add)
                link(dve.tensor_copy(idf[:], idx[:]))
                link(dve.reciprocal(ws[:], ws[:]))
                for k in range(TOP):
                    o = dve.tensor_tensor(wt[:, :, k], top[:, :, k], ws[:], ALU.mult)
                link(o)
                for t in range(NT):
                    dve.tensor_scalar(ga[:, t], iota[:], idf[:, t, 0:1], wt[:, t, 0:1], ALU.is_equal, ALU.mult)
                    o = dve.tensor_scalar(gb_[:, t], iota[:], idf[:, t, 1:2], wt[:, t, 1:2], ALU.is_equal, ALU.mult)
                link(o)
                link(dve.tensor_tensor(ga[:], ga[:], gb_[:], ALU.add))
                dve.tensor_copy(ghi[:], ga[:]).then_inc(s["gate"], 1)
                dve.wait_ge(s["gate"], (i + 1) * GC)
                g = ghi[:].bitcast(F32)
                dve.tensor_copy(gpad[:, :, 0:E], g)
                dve.tensor_copy(gpad[:, :, 2 * E:3 * E], g)
                dve.tensor_tensor(gpad[:, :, E:2 * E], ga[:], g, ALU.subtract).then_inc(s["gpad"], 1)

            def gate_stack(i, par):
                dve.wait_ge(s["gT_ps"], i + 1)
                dve.tensor_copy(gst[:, par], aux[:, 1]).then_inc(s["gst"], 1)

            def gating(i, e):
                dve.wait_ge(s["gelu"], i * NE + e + 1)
                dve.wait_ge(s["gbc"], i * E + e + 1)
                dve.tensor_tensor(gated[:, e % 3], gbc[:, e % 2], act_out[:, e % 3],
                                  ALU.mult).then_inc(s["gated"], 1)

            def lo(i, e):
                dve.wait_ge(s["h_hi"], i * NE + e + 1)
                from_ = act_out if shared(e) else gated
                dve.tensor_tensor(hp[:, e % 3, 1], from_[:, e % 3], hp[:, e % 3, 0].bitcast(F32),
                                  ALU.subtract).then_inc(s["h_lo"], 1)

            def result(i):
                dve.wait_ge(s["out"], i * NE + NE)
                dve.wait_ge(s["xres"], i * 16 + 16)
                dve.wait_ge(s["res_out"], i * 16 + 16)
                for h in range(2):
                    t = slice(2 * h, 2 * h + 2)
                    o = dve.scalar_tensor_tensor(out=res[:, t], in0=acc[:, t], scalar=0.5,
                                                 in1=xres[:, t], op0=ALU.mult, op1=ALU.add)
                o.then_inc(s["res"], 1)

            def z_stats(i):
                dve.wait_ge(s["res"], i + 1)
                norm_stats(res, zst6, zmv, s["z_bn"], s["z_stats"], i * 2 + 1)

            def z_norm(i):
                dve.wait_ge(s["z_rstd"], i * 2 + 1)
                dve.wait_ge(s["z_out"], i * 16 + 16)
                for t in range(NT):
                    o = dve.tensor_scalar(zz[:, t], res[:, t], zmv[:, t, 0:1], zrs[:, t:t + 1],
                                          ALU.subtract, ALU.mult)
                o.then_inc(s["z"], 1)
                dve.wait_ge(s["z"], i + 1)
                norm_stats(zz, zst6, zmv, s["z_bn"], s["z_stats"], i * 2 + 2)

            def zn_norm(i):
                dve.wait_ge(s["z_rstd"], i * 2 + 2)
                for t in range(NT):
                    o = dve.tensor_scalar(zn[:, t], zz[:, t], zmv[:, t, 0:1], zrs[:, t:t + 1],
                                          ALU.subtract, ALU.mult)
                o.then_inc(s["zn"], 1)

            def zt_lo(i):
                for c in range(DC):
                    dve.wait_ge(s["zT_hi"], i * DC + c + 1)
                    dve.tensor_tensor(zT[:, c, 1], aux[:, c], zT[:, c, 0].bitcast(F32),
                                      ALU.subtract).then_inc(s["zT_lo"], 1)

            dve.sem_inc(s["res_out"], 16)
            if tail:
                dve.sem_inc(s["z_out"], 16)
            x_stats(0, 0)
            x_norm(0, 0, True)
            dve.wait_ge(s["w_hi"], 1)
            dve.tensor_tensor(gwp[:, :, 1, :], gw_in[:].rearrange("p (c e) -> p c e", c=DC),
                              gwp[:, :, 0, :].bitcast(F32), ALU.subtract)
            dve.tensor_tensor(w1p[:, 1], w1_in[:], w1p[:, 0].bitcast(F32), ALU.subtract)
            dve.tensor_tensor(w2p[:, 1], w2_in[:], w2p[:, 0].bitcast(F32), ALU.subtract)
            dve.tensor_tensor(b2lo[:], b2_in[:], b2hi[:].bitcast(F32), ALU.subtract).then_inc(s["w_ready"], 1)
            dve.wait_ge(s["w_ready"], 1)
            dve.tensor_scalar(b2_in[:], b2lo[:].bitcast(F32), rows[:, 1:2], None, ALU.mult).then_inc(s["w_ready"], 1)
            dve.wait_ge(s["w_ready"], 2)
            dve.scalar_tensor_tensor(out=b2s[:], in0=b2hi[:].bitcast(F32), scalar=rows[:, 0:1], in1=b2_in[:],
                                     op0=ALU.mult, op1=ALU.add).then_inc(s["w_ready"], 1)

            def body(i, par, first, last):
                for e in range(NE):
                    if not shared(e):
                        gating(i, e)
                    if e > 0:
                        lo(i, e - 1)
                    elif not first:
                        lo(i - 1, E)
                    if not first:
                        if e == 1:
                            result(i - 1)
                            if tail:
                                z_stats(i - 1)
                        if e == 3 and tail:
                            z_norm(i - 1)
                        if e == 4 and tail:
                            zn_norm(i - 1)
                        if e == 5 and tail:
                            zt_lo(i - 1)
                    if not last:
                        if e == 1:
                            x_stats(i + 1, 1 - par)
                        if e == 2:
                            x_norm(i + 1, 1 - par, False)
                        if e == 3:
                            xt_lo(i + 1, 1 - par)
                        if e == 4:
                            neg_logits(i + 1)
                        if e == 6:
                            gates(i + 1)
                        if e == 7:
                            gate_stack(i + 1, 1 - par)
            xt_lo(0, 0)
            neg_logits(0)
            dve.wait_ge(s["zeroed"], 3)
            gates(0)
            gate_stack(0, 0)
            over_blocks(dve, body)
            lo(NB - 1, E)
            result(NB - 1)
            if tail:
                z_stats(NB - 1)
                z_norm(NB - 1)
                zn_norm(NB - 1)
                zt_lo(NB - 1)

        @block.tensor
        def _(pe):
            def transposes(i, from_, ready, done):
                pe.wait_ge(ready, i + 1)
                for c in range(DC):
                    for t in range(NT):
                        o = pe.transpose(aux[:, c, t * P:(t + 1) * P], from_[:, t, c * P:(c + 1) * P], ident[:])
                    o.then_inc(done, 1)

            def logits(i, par):
                pe.wait_ge(s["xT_lo"], i * DC + DC)
                for t in range(NT):
                    for c in range(DC):
                        for k in range(2):
                            n = 2 * E if k == 0 else E
                            o = pe.matmul(aux[:, 0, t * 2 * E:t * 2 * E + n],
                                          xT[:, par, c, k, t * P:(t + 1) * P],
                                          gwp[:, c].rearrange("p k e -> p (k e)")[:, 0:n],
                                          start=(t == 0 and c == 0 and k == 0), stop=(c == DC - 1 and k == 1),
                                          skip_group_check=True)
                o.then_inc(s["logits"], 1)

            def gates_up(i):
                pe.wait_ge(s["gpad"], i + 1)
                for t in range(NT):
                    o = pe.transpose(aux[:, 1, t * P:(t + 1) * P], gpad[:, t], ident[:])
                o.then_inc(s["gT_ps"], 1)

            PARTS = ((0, 0), (0, 1), (1, 0))

            def first_layer(i, e, par, start):
                if not start:
                    pe.wait_ge(s["gelu"], i * NE + e - 1)
                n = 0
                for c in range(DC):
                    for a, b in PARTS:
                        o = pe.matmul(hid[:, (par + e) % 2], w1p[:, a, (c * NE + e) * HID:(c * NE + e + 1) * HID],
                                      xT[:, par, c, b], start=(n == 0), stop=(n == 5))
                        n += 1
                o.then_inc(s["hid"], 1)
                if not shared(e):
                    if e == 0:
                        pe.wait_ge(s["gst"], i + 1)
                    if e >= 2 or not start:
                        pe.wait_ge(s["gated"], i * E + e - 1)
                    pe.matmul(gbc[:, e % 2], sel[:, e * P:(e + 1) * P], gst[:, par],
                              start=True, stop=True).then_inc(s["gbc"], 1)

            def second_layer(i, e, par, first):
                if e == 0:
                    if not first:
                        pe.wait_ge(s["res"], i)
                    for t in range(NT):
                        pe.matmul(acc[:, t], gst[:, par, t * P:(t + 1) * P], b2s[:],
                                  start=(t % 2 == 0), stop=False, skip_group_check=True)
                pe.wait_ge(s["h_lo"], i * NE + e + 1)
                for t in range(NT):
                    for a, b in PARTS:
                        o = pe.matmul(acc[:, t], hp[:, e % 3, a, t * P:(t + 1) * P],
                                      w2p[:, b, e * D:(e + 1) * D], start=False, stop=(shared(e) and (a, b) == (1, 0)),
                                      skip_group_check=True)
                o.then_inc(s["out"], 1)

            def body(i, par, first, last):
                for e in range(NE):
                    first_layer(i, e, par, first and e < 2)
                    if e >= 2:
                        second_layer(i, e - 2, par, first)
                    elif not first:
                        second_layer(i - 1, E - 1 + e, 1 - par, False)
                    if not last:
                        if e == 3:
                            pe_next_transposes(i + 1, first)
                        if e == 4:
                            logits(i + 1, 1 - par)
                        if e == 7:
                            if tail and not first:
                                pe.wait_ge(s["zT_lo"], i * DC)
                            gates_up(i + 1)
                    if e == 5 and tail and not first:
                        if not last:
                            pe.wait_ge(s["neg"], i + 2)
                        transposes(i - 1, zn, s["zn"], s["zT_ps"])

            def pe_next_transposes(i, first):
                pe.wait_ge(s["gst"], i)
                transposes(i, xn, s["xn"], s["xT_ps"])

            pe.wait_ge(s["w_in"], 16 * NW)
            transposes(0, xn, s["xn"], s["xT_ps"])
            pe.wait_ge(s["w_ready"], 3)
            logits(0, 0)
            gates_up(0)
            over_blocks(pe, body)
            second_layer(NB - 1, E - 1, 1, False)
            second_layer(NB - 1, E, 1, False)
            if tail:
                pe.wait_ge(s["zT_lo"], (NB - 1) * DC)
                transposes(NB - 1, zn, s["zn"], s["zT_ps"])


def qkv_weights_phase(nc, tag, w, wqk, wv, bias):
    PAIRS = AHD // P
    QS = float(D) ** -0.5
    with ExitStack() as ctx:
        m = Bank(nc, ctx, tag)
        w_in = m.sb("w_in", [P, 3, DC, AHD])
        scaled = m.sb("scaled", [P, 3, DC, AHD])
        split = m.sb("split", [P, 3, DC, 2, AHD], F32R)
        ln = m.sb("ln", [P, 3, DC, 2])
        c_in = m.sb("c_in", [P, 3, PAIRS])
        b_sb = m.sb("b_sb", [P, PAIRS, 3])
        pb = m.ps("pb", [P, 3, PAIRS])
        s_in, s_sc, s_hi, s_lo, s_pb, s_b, s_out = (m.sem(n) for n in "in scaled hi lo pb b out".split())
        block = ctx.enter_context(nc.Block())

        @block.sync
        def _(sp):
            sp.dma_start(ln[:], w["ln_qkv"]).then_inc(s_in, 16)
            sp.dma_start(c_in[:], w["c_qkv"]).then_inc(s_in, 16)
            for k in range(3):
                sp.dma_start(w_in[:, k], w["w_qkv"][k]).then_inc(s_in, 16)
            sp.wait_ge(s_lo, 1)
            for g in range(PAIRS):
                for k in range(2):
                    sp.dma_start(wqk[g, :, k], split[:, k, :, :, g * P:(g + 1) * P].bitcast(F32)).then_inc(s_out, 16)
            for g in range(PAIRS // 2):
                sp.dma_start(wv[g], split[:, 2, :, :, g * 2 * P:(g + 1) * 2 * P].bitcast(F32)).then_inc(s_out, 16)
            sp.wait_ge(s_b, 3)
            sp.dma_start(bias, b_sb[:]).then_inc(s_out, 16)
            sp.wait_ge(s_out, 16 * (PAIRS * 2 + PAIRS // 2 + 1))

        @block.scalar
        def _(act):
            act.wait_ge(s_sc, 1)
            act.activation(split[:, :, :, 0], scaled[:], ACT.Identity).then_inc(s_hi, 1)

        @block.vector
        def _(dve):
            dve.wait_ge(s_in, 80)
            for k in range(3):
                for c in range(DC):
                    o = dve.tensor_scalar(scaled[:, k, c], w_in[:, k, c], ln[:, k, c, 0:1],
                                          QS if k == 0 else 1.0, ALU.mult, ALU.mult)
            o.then_inc(s_sc, 1)
            dve.wait_ge(s_pb, 1)
            dve.tensor_tensor(b_sb[:].rearrange("p g k -> p k g"), pb[:], c_in[:], ALU.add).then_inc(s_b, 1)
            dve.wait_ge(s_b, 1)
            dve.tensor_scalar(b_sb[:, :, 0], b_sb[:, :, 0], QS, None, ALU.mult).then_inc(s_b, 2)
            dve.wait_ge(s_hi, 1)
            dve.tensor_tensor(split[:, :, :, 1], scaled[:], split[:, :, :, 0].bitcast(F32),
                              ALU.subtract).then_inc(s_lo, 1)

        @block.tensor
        def _(pe):
            pe.wait_ge(s_in, 80)
            for k in range(3):
                for g in range(PAIRS):
                    for c in range(DC):
                        o = pe.matmul(pb[:, k, g:g + 1], w_in[:, k, c, g * P:(g + 1) * P], ln[:, k, c, 1:2],
                                      start=(c == 0), stop=(c == DC - 1))
            o.then_inc(s_pb, 1)


def attention_phase(nc, turns, tag, w, zT, wqk, wv, bias, att):
    PAIRS = AHD // P
    STEPS = 16
    ITER = 2 * STEPS
    NIT = B * PAIRS // 2
    LAG = 3
    QT = S // P
    NP = 4
    BLOCKS = 8
    with ExitStack() as ctx:
        m = Bank(nc, ctx, tag)
        ident = m.sb("ident", [P, P])
        bsb = m.sb("bsb", [P, PAIRS, 3])
        bqk_s = m.sb("bqk_s", [P, 2])
        wqk_s = m.sb("wqk_s", [P, 2, DC, 2, P], F32R)
        wv_s = m.sb("wv_s", [P, DC, 2, 2 * P], F32R)
        z_s = m.sb("z_s", [P, DC * 2, 2, BT], F32R)
        staged = m.sb("staged", [P, 2, BT])
        q_s = m.sb("q_s", [P, 2, 2, S], F32R)
        k_s = m.sb("k_s", [P, 2, 2, 2, S], F32R)
        v_s = m.sb("v_s", [P, 2, QT, 4, HD], F32R)
        v_b = m.sb("v_b", [P, QT, 4, HD], F32R)
        pr = m.sb("pr", [P, NP, S])
        nmax = m.sb("nmax", [P, NP])
        den = m.sb("den", [P, NP])
        rden = m.sb("rden", [P, NP])
        pT = m.sb("pT", [P, 2, 2, QT, BT], F32R)
        half = m.sb("half", [P, 2, BT])
        ao = m.sb("ao", [P, 2, 2, BT])
        sc = m.ps("sc", [P, 2, S])
        tr = m.ps("tr", [P, 2, BT])
        pj = m.ps("pj", [P, BT])
        ov = m.ps("ov", [P, BT])

        s = {n: m.sem(n) for n in (
            "const z_in wqk_in wv_in v_in k_dup sc masked negmax exp rden normed tr tr_hi tr_lo "
            "pj staged head0_hi head1_hi head0_lo v_hi split pv half ov_read att att_out").split()}

        PROJ = {2: ("Q", 0), 5: ("Q", 1), 8: ("K", 0), 11: ("K", 1)}
        VALS = {7: ("V", 0), 9: ("V", 1), 12: ("V", 2), 14: ("V", 3)}
        FIRST = [("Q", 0), ("Q", 1), ("K", 0), ("K", 1), ("V", 0), ("V", 1), ("V", 2), ("V", 3)]
        PLAN = [PROJ.get(k % STEPS) or (VALS.get(k % STEPS) if k >= STEPS else None) for k in range(ITER)]
        PER = sum(x is not None for x in PLAN)
        assert PER % 2 == 0 and len(FIRST) % 2 == 0

        def before(it, k):
            return it * PER + len(FIRST) + sum(x is not None for x in PLAN[:k])

        def piece_at(it, k):
            return PLAN[k] and (*PLAN[k], before(it, k), (before(0, k)) % 2)

        def over_iterations(eng, body):
            body(0, True, False)
            with eng.Fori(1, NIT) as it:
                body(it, False, False)
            body(NIT, False, True)

        def steps(last):
            return range(LAG + 5 if last else ITER)

        def transposes_at(k, first, last):
            return not (first and k < LAG) and not (last and k >= LAG)

        def values_at(k, first):
            j = k - LAG - 4
            if first and j < 0:
                return None
            block = j // 4
            return (block // 4) % 2, (block // 2) % 2, block, j % 4

        def finished_at(k, first):
            v = values_at(k - 1, first) if k > 0 or not first else None
            return v if v and v[3] == 3 else None

        block_ = ctx.enter_context(nc.Block())

        def pair_of(it, slot):
            return it // 4, (it % 4) * 2 + slot

        def after(it):
            return (it + 1) % NIT

        @block_.sync
        def _(sp):
            def fixed(x):
                return x if isinstance(x, int) else sp.snap(x)

            def load_z(it):
                sp.dma_start(z_s[:].bitcast(F32), zT[bass.ds(fixed((it // 4) * 2), 2)].rearrange("h p c k t -> p (c k) h t"))\
                    .then_inc(s["z_in"], 16)

            def load_wqk(it, slot):
                g = fixed((it % 4) * 2 + slot)
                sp.dma_start(wqk_s[:].bitcast(F32).rearrange("p k c l f -> p (k c l f)"),
                             wqk[bass.ds(g, 1)].rearrange("g p k c l f -> p (g k c l f)")).then_inc(s["wqk_in"], 16)
                sp.dma_start(bqk_s[:], bias[:, bass.ds(g, 1), 0:2].rearrange("p g k -> p (g k)"))\
                    .then_inc(s["wqk_in"], 16)

            def load_wv(it):
                sp.dma_start(wv_s[:].bitcast(F32).rearrange("p c l f -> p (c l f)"),
                             wv[bass.ds(fixed(it % 4), 1)].rearrange("g p c l f -> p (g c l f)")).then_inc(s["wv_in"], 16)

            def double_k(slot):
                for head, (a, b) in enumerate(((0, HD), (HD, 0))):
                    sp.dma_start(k_s[b:b + HD, slot, head].bitcast(F32), k_s[a:a + HD, slot, head].bitcast(F32))\
                        .then_inc(s["k_dup"], 16)

            def move_v():
                sp.dma_start(v_s[:, 1].bitcast(F32).rearrange("p t k f -> p (t k f)"),
                             v_b[:].bitcast(F32).rearrange("p t k f -> p (t k f)")).then_inc(s["v_in"], 16)

            def store(it, slot, pairs):
                b, hp = pair_of(it, slot)
                to = att[bass.ds(fixed(hp), 1), :, bass.ds(fixed(b * S), S)].rearrange("g p t -> p (g t)")
                sp.wait_ge(s["att"], pairs)
                sp.dma_start(to, ao[:, slot].rearrange("p h t -> p (h t)")).then_inc(s["att_out"], 16)

            sp.dma_start(ident[:], w["ident"]).then_inc(s["const"], 16)
            sp.dma_start(bsb[:], bias).then_inc(s["const"], 16)
            load_z(0)
            load_wqk(0, 0)
            load_wv(0)
            sp.wait_ge(s["split"], 4)
            double_k(0)
            load_wqk(0, 1)
            sp.wait_ge(s["split"], 8)
            load_wv(1)
            move_v()

            def body(it, first, last):
                if not first:
                    if not last:
                        sp.wait_ge(s["pv"], it * BLOCKS)
                        move_v()
                    store(it - 1, 1, it * 2)
                if last:
                    return
                sp.wait_ge(s["split"], before(it, STEPS))
                double_k(1)
                load_wqk(after(it), 0)
                load_z(after(it))
                store(it, 0, it * 2 + 1)
                sp.wait_ge(s["split"], before(it, STEPS + 12))
                double_k(0)
                load_wqk(after(it), 1)
                sp.wait_ge(s["split"], before(it, ITER))
                load_wv(after(it + 1))
            over_iterations(sp, body)
            sp.wait_ge(s["att_out"], 16 * B * PAIRS)
            sp.wait_ge(s["wv_in"], 16 * (NIT + 2))
            sp.wait_ge(s["wqk_in"], 32 * (2 * NIT + 2))
            sp.wait_ge(s["z_in"], 16 * (NIT + 1))
            sp.wait_ge(s["k_dup"], 32 * (2 * NIT + 1))

        def rows_of_head(head):
            return slice(head * HD, head * HD + HD)

        @block_.scalar
        def _(act):
            act.preload_act_table(ACT.Exp)
            act.wait_ge(s["const"], 32)

            def stage(kind, n, slot, start):
                act.wait_ge(s["pj"], n + 1)
                if not (start and n < 2):
                    act.wait_ge(s["split"], n - 1)
                if kind == "V":
                    o = act.activation(staged[:, slot], pj[:], ACT.Identity)
                else:
                    o = act.activation(staged[:, slot], pj[:], ACT.Identity, bias=bqk_s[:, "QK".index(kind):"QK".index(kind) + 1])
                o.then_inc(s["staged"], 1)

            act.wait_ge(s["wqk_in"], 32)
            for n, (kind, part) in enumerate(FIRST):
                stage(kind, n, n % 2, True)

            def body(it, first, last):
                for k in steps(last):
                    tile = it * ITER + k - LAG
                    v = finished_at(k, first)
                    if v:
                        vslot, vhead, blk, _ = v
                        r, other = rows_of_head(vhead), rows_of_head(1 - vhead)
                        n = it * BLOCKS + blk
                        act.wait_ge(s["pv"], n + 1)
                        if blk % 4 == 0 and not (first and blk < 4):
                            act.wait_ge(s["att"], it * 2 + blk // 4)
                        act.activation(half[r, blk % 2], ov[other], ACT.Identity).then_inc(s["half"], 1)
                        if blk % 4 == 0 and not (first and blk < 8) and not blk < 0:
                            act.wait_ge(s["att_out"], it * 32 + (blk // 4) * 16 - 16)
                            stand_alone(act, turns)
                        g = (2 * it + blk // 4) % PAIRS
                        act.activation(ao[r, vslot, blk % 2], ov[r], ACT.Identity,
                                       bias=bsb[r, g, 2:3] if isinstance(g, int) else bsb[r, bass.ds(g, 1), 2])\
                            .then_inc(s["ov_read"], 1)
                    if transposes_at(k, first, last):
                        for part in range(2):
                            act.wait_ge(s["tr"], 2 * tile + part + 1)
                            u = (k - LAG) % ITER
                            act.activation(pT[:, (u // 4) % 2, 0, 4 * part:4 * part + 4, (u % 4) * P:(u % 4 + 1) * P],
                                           tr[:, part].rearrange("p (t q) -> p t q", t=4), ACT.Identity)\
                                .then_inc(s["tr_hi"], 1)
                    if not last:
                        u = it * ITER + k
                        act.wait_ge(s["negmax"], u + 1)
                        act.activation(pr[:, k % NP], sc[:, k % 2], ACT.Exp, bias=nmax[:, k % NP:k % NP + 1],
                                       accum_out=den[:, k % NP:k % NP + 1]).then_inc(s["exp"], 1)
                        if PLAN[k]:
                            kind, _, n, slot = piece_at(it, k)
                            stage(kind, n, slot, False)
            over_iterations(act, body)

        @block_.gpsimd
        def _(pool):
            def v_parts(slot, t):
                to = (v_s[:, 0] if slot == 0 else v_b[:])[:, 2 * t:2 * t + 2]
                return to[:, :, 0::3], to[:, :, 1:3]

            def split_values(part, n, slot, nv):
                from_ = staged[:, slot].rearrange("p (t s h f) -> p t s h f", t=2, s=2, h=2)
                pool.wait_ge(s["staged"], n + 1)
                stand_alone(pool, turns)
                for x in range(2):
                    o = pool.tensor_scalar(v_parts(x, part)[0], from_[:, :, x], 1.0, 1.0, ALU.mult, ALU.mult)
                o.then_inc(s["v_hi"], 1)
                pool.wait_ge(s["v_hi"], nv + 1)
                for x in range(2):
                    hi, lo = v_parts(x, part)
                    o = pool.tensor_tensor(lo, from_[:, :, x], hi.bitcast(F32), ALU.subtract)
                o.then_inc(s["split"], 1)

            def split_qk(kind, part, n, slot, pair_slot, nqk):
                cols = slice(part * BT, part * BT + BT)
                r0, r1 = rows_of_head(0), rows_of_head(1)
                if kind == "Q":
                    hi = [q_s[r0, pair_slot, 0, cols], q_s[r1, pair_slot, 1, cols]]
                    lo = [q_s[r1, pair_slot, 0, cols], q_s[r0, pair_slot, 1, cols]]
                else:
                    hi = [k_s[r0, pair_slot, 0, 0, cols], k_s[r1, pair_slot, 1, 0, cols]]
                    lo = [k_s[r0, pair_slot, 0, 1, cols], k_s[r1, pair_slot, 1, 1, cols]]
                pool.wait_ge(s["staged"], n + 1)
                stand_alone(pool, turns)
                pool.tensor_scalar(hi[0], staged[r0, slot], 1.0, 1.0, ALU.mult, ALU.mult).then_inc(s["head0_hi"], 1)
                pool.wait_ge(s["head0_hi"], nqk + 1)
                stand_alone(pool, turns)
                pool.tensor_scalar(hi[1], staged[r1, slot], 1.0, 1.0, ALU.mult, ALU.mult).then_inc(s["head1_hi"], 1)
                pool.wait_ge(s["head1_hi"], nqk + 1)
                pool.tensor_tensor(lo[0], staged[r0, slot], hi[0].bitcast(F32), ALU.subtract).then_inc(s["head0_lo"], 1)
                pool.wait_ge(s["head0_lo"], nqk + 1)
                pool.tensor_tensor(lo[1], staged[r1, slot], hi[1].bitcast(F32), ALU.subtract).then_inc(s["split"], 1)
                pool.wait_ge(s["split"], n + 1)

            for n, (kind, part) in enumerate(FIRST):
                if kind == "V":
                    split_values(part, n, n % 2, n - 4)
                else:
                    split_qk(kind, part, n, n % 2, 0, n)

            def normalise(u, k):
                pool.wait_ge(s["rden"], u + 1)
                stand_alone(pool, turns)
                pool.tensor_scalar(pr[:, k % NP], pr[:, k % NP], rden[:, k % NP:k % NP + 1], 1.0,
                                   ALU.mult, ALU.mult).then_inc(s["normed"], 1)

            def body(it, first, last):
                for k in steps(last):
                    if (k > 0 and not last) or (k == 0 and not first):
                        normalise(it * ITER + k - 1, (k - 1) % ITER)
                    v = finished_at(k, first)
                    if v and v[2] % 4 == 3:
                        pool.wait_ge(s["ov_read"], it * BLOCKS + v[2] + 1)
                        pool.tensor_tensor(ao[:, v[0]], ao[:, v[0]], half[:], ALU.add).then_inc(s["att"], 1)
                    if not last and PLAN[k]:
                        kind, part, n, slot = piece_at(it, k)
                        kinds = [x and x[0] == "V" for x in PLAN[:k]]
                        nv = sum(x is True for x in kinds)
                        if kind == "V":
                            split_values(part, n, slot, it * 4 + 4 + nv)
                        else:
                            pool.wait_ge(s["normed"], it * ITER + k)
                            split_qk(kind, part, n, slot, (k // STEPS + 1) % 2, it * 8 + 4 + sum(x is False for x in kinds))
            over_iterations(pool, body)

        @block_.vector
        def _(dve):
            def body(it, first, last):
                for k in steps(last):
                    u = it * ITER + k
                    if not last:
                        dve.wait_ge(s["sc"], u + 1)
                        if k % QT == 0:
                            dve.tensor_scalar(sc[0:1, k % 2, S - 1:S], sc[0:1, k % 2, S - 1:S], MASK, None,
                                              ALU.add).then_inc(s["masked"], 1)
                            dve.wait_ge(s["masked"], it * (ITER // QT) + k // QT + 1)
                        dve.tensor_reduce(nmax[:, k % NP:k % NP + 1], sc[:, k % 2], AX.X, ALU.max,
                                          negate=True).then_inc(s["negmax"], 1)
                    if (k == 0 and not first) or (k > 0 and not last):
                        j = (k - 1) % NP
                        dve.wait_ge(s["exp"], u)
                        dve.reciprocal(rden[:, j:j + 1], den[:, j:j + 1]).then_inc(s["rden"], 1)
                    if transposes_at(k, first, last):
                        t = (k - LAG) % ITER
                        for part in range(2):
                            dve.wait_ge(s["tr_hi"], 2 * (u - LAG) + part + 1)
                            to = pT[:, (t // 4) % 2, :, 4 * part:4 * part + 4, (t % 4) * P:(t % 4 + 1) * P]
                            dve.tensor_tensor(to[:, 1], tr[:, part].rearrange("p (t q) -> p t q", t=4),
                                              to[:, 0].bitcast(F32), ALU.subtract).then_inc(s["tr_lo"], 1)
            over_iterations(dve, body)

        @block_.tensor
        def _(pe):
            PARTS = ((0, 0), (0, 1), (1, 0))
            pe.wait_ge(s["const"], 32)

            def project(kind, part, n, start):
                if not (start and n == 0):
                    pe.wait_ge(s["staged"], n)
                if kind in "QK":
                    i = 0
                    for c in range(DC):
                        for a, b in PARTS:
                            o = pe.matmul(pj[:], wqk_s[:, "QK".index(kind), c, a], z_s[:, c * 2 + b, part],
                                          start=(i == 0), stop=(i == 5))
                            i += 1
                else:
                    for t in range(2):
                        col = ((2 * part + t) % NT) * P
                        i = 0
                        for c in range(DC):
                            for a, b in PARTS:
                                o = pe.matmul(pj[:, t * 2 * P:(t + 1) * 2 * P],
                                              z_s[:, c * 2 + a, part // 2, col:col + P], wv_s[:, c, b],
                                              start=(i == 0), stop=(i == 5))
                                i += 1
                o.then_inc(s["pj"], 1)

            pe.wait_ge(s["z_in"], 16)
            pe.wait_ge(s["wqk_in"], 32)
            pe.wait_ge(s["wv_in"], 16)
            for n, (kind, part) in enumerate(FIRST):
                project(kind, part, n, True)

            def body(it, first, last):
                for k in steps(last):
                    u = it * ITER + k
                    slot, head, tile = k // STEPS, (k // QT) % 2, k % QT
                    if not last:
                        if k % STEPS == 0:
                            pe.wait_ge(s["k_dup"], it * 64 + slot * 32 + 32)
                        if not (first and k < 2):
                            pe.wait_ge(s["exp"], u - 1)
                        for kb in range(S // BT):
                            for a in range(2):
                                o = pe.matmul(sc[:, k % 2, kb * BT:(kb + 1) * BT],
                                              q_s[:, slot, head, tile * P:(tile + 1) * P],
                                              k_s[:, slot, head, a, kb * BT:(kb + 1) * BT],
                                              start=(a == 0), stop=(a == 1))
                        o.then_inc(s["sc"], 1)
                    if transposes_at(k, first, last):
                        pe.wait_ge(s["normed"], u - LAG + 1)
                        for part in range(2):
                            if not (first and k == LAG):
                                pe.wait_ge(s["tr_lo"], 2 * (u - LAG) + part - 1)
                            for j in range(4):
                                o = pe.transpose(tr[:, part, j * P:(j + 1) * P],
                                                 pr[:, (k - LAG) % NP, (4 * part + j) * P:(4 * part + j + 1) * P], ident[:])
                            o.then_inc(s["tr"], 1)
                    v = values_at(k, first)
                    if v and not (last and v[2] >= 0):
                        vslot, vhead, blk, q = v
                        if q == 0:
                            pe.wait_ge(s["tr_lo"], 2 * (u - LAG))
                            if blk == 0:
                                pe.wait_ge(s["split"], before(it, 0))
                            if blk == 4:
                                pe.wait_ge(s["v_in"], it * 16 + 16)
                            if not (first and blk == 0):
                                pe.wait_ge(s["ov_read"], it * BLOCKS + blk)
                        for kt in (2 * q, 2 * q + 1):
                            for a in range(2):
                                o = pe.matmul(ov[:], v_s[:, vslot, kt, 2 * vhead:2 * vhead + 2]
                                              .rearrange("p k f -> p (k f)"), pT[:, blk % 2, a, kt],
                                              start=(kt == 0 and a == 0), stop=(kt == QT - 1 and a == 1))
                        if q == 3:
                            o.then_inc(s["pv"], 1)
                    if not last and PLAN[k]:
                        kind, part, n, _ = piece_at(it, k)
                        if kind == "Q" and part == 0:
                            pe.wait_ge(s["wqk_in"], it * 64 + (k // STEPS) * 32 + 64)
                            if k >= STEPS:
                                pe.wait_ge(s["z_in"], it * 16 + 32)
                        if kind == "V" and part == 0:
                            pe.wait_ge(s["wv_in"], it * 16 + 32)
                        project(kind, part, n, False)
            over_iterations(pe, body)


def mlp_phase(nc, turns, tag, w, att, z, x1, x2):
    PAIRS = AHD // P
    HP = PAIRS // 2
    HC = MH // P
    PARTS = ((0, 0), (0, 1), (1, 0))
    with ExitStack() as ctx:
        m = Bank(nc, ctx, tag)
        ident = m.sb("ident", [P, P])
        wo_in = m.sb("wo_in", [P, PAIRS, D])
        wo = m.sb("wo", [P, 2, PAIRS, D], F32R)
        w1_in = m.sb("w1_in", [P, DC, MH])
        w1 = m.sb("w1", [P, 2, DC, MH], F32R)
        w2_in = m.sb("w2_in", [P, HC, D])
        w2 = m.sb("w2", [P, 2, HC, D], F32R)
        ln = m.sb("ln", [P, DC, 2])
        b1_in = m.sb("b1_in", [P, HC])
        b1 = m.sb("b1", [P, HC])
        bo = m.sb("bo", [P, D])
        b2 = m.sb("b2", [P, D])
        mhalf = m.sb("mhalf", [P, NT])

        att_in = m.sb("att_in", [P, 2, HP, BT])
        att_s = m.sb("att_s", [P, 2, 2, PAIRS, BT], F32R)
        zin = m.sb("zin", [P, 2, NT, D])
        xin = m.sb("xin", [P, 2, NT, D])
        h = m.sb("h", [P, NT, D])
        st6 = m.sb("st6", [P, NT, 6])
        mv = m.sb("mv", [P, NT, 2])
        rs = m.sb("rs", [P, NT])
        hn = m.sb("hn", [P, NT, D])
        hT = m.sb("hT", [P, DC, 2, BT], F32R)
        act_out = m.sb("act_out", [P, HC, BT])
        hid_s = m.sb("hid_s", [P, HC, 2, BT], F32R)
        res = m.sb("res", [P, NT, D])
        proj = m.ps("proj", [P, NT, D])
        hT_ps = m.ps("hT_ps", [P, DC, BT])
        hid = m.ps("hid", [P, 2, BT])
        acc = m.ps("acc", [P, NT, D])

        s = {n: m.sem(n) for n in (
            "w_in mhalf w1_scaled w_hi w_ready b1_ps att_in0 att_in1 att_hi att_lo z_in x_in zb x_b proj h bn stats "
            "veps rstd hn hT_ps hT_hi hT_lo hid gelu hid_hi hid_lo acc x_h res res_out").split()}
        NW = 8
        block = ctx.enter_context(nc.Block())

        def over_steps(eng, body):
            body(0, 0)
            with eng.Fori(0, (NB - 4) // 2) as it:
                body(it * 2 + 1, 1)
                body(it * 2 + 2, 0)
            for i in range(NB - 3, NB + 1):
                body(i, i % 2)

        def has(i, ahead=0):
            return not isinstance(i, int) or 0 <= i + ahead < NB

        @block.sync
        def _(sp):
            def fixed(i):
                return i if isinstance(i, int) else sp.snap(i)

            def rows_of(ap, i):
                return ap.rearrange("(n t p) d -> n p t d", t=NT, p=P)[bass.ds(i, 1)].rearrange("n p t d -> p (n t) d")

            def load_att(token, half):
                from_ = att[half * HP:(half + 1) * HP, :, bass.ds(token, BT)].rearrange("g p t -> p g t")
                sp.dma_start(att_in[:, half], from_).then_inc(s["att_in%d" % half], 16)

            load_att(0, 0)
            load_att(0, 1)
            sp.dma_start(wo_in[:], w["wo"]).then_inc(s["w_in"], 16)
            sp.dma_start(ln[:], w["ln_m"]).then_inc(s["w_in"], 16)
            sp.dma_start(bo[:], w["bo"].partition_broadcast(P)).then_inc(s["w_in"], 16)
            sp.dma_start(b2[:], w["b2m"].partition_broadcast(P)).then_inc(s["w_in"], 16)
            sp.dma_start(b1_in[:], w["b1m"]).then_inc(s["w_in"], 16)
            sp.dma_start(ident[:], w["ident"]).then_inc(s["w_in"], 16)
            sp.dma_start(w1_in[:], w["w1m"]).then_inc(s["w_in"], 16)
            sp.dma_start(w2_in[:], w["w2m"]).then_inc(s["w_in"], 16)
            sp.dma_start(zin[:, 0], rows_of(z, 0)).then_inc(s["z_in"], 16)
            sp.dma_start(xin[:, 0], rows_of(x1, 0)).then_inc(s["x_in"], 16)
            for half in range(2):
                sp.wait_ge(s["att_lo"], half + 1)
                load_att(BT, half)
            for half in range(2):
                sp.wait_ge(s["att_lo"], 2 + half + 1)
                load_att(2 * BT, half)

            def body(i, par):
                if has(i, 3):
                    ahead = fixed((i + 3) * BT)
                if has(i, -1):
                    to = rows_of(x2, fixed(i - 1))
                if has(i, 1):
                    z_from, x_from = rows_of(z, fixed(i + 1)), rows_of(x1, fixed(i + 1))
                    sp.wait_ge(s["h"], i + 1)
                    sp.dma_start(zin[:, 1 - par], z_from).then_inc(s["z_in"], 16)
                if has(i, 3):
                    for half in range(2):
                        sp.wait_ge(s["att_lo"], (i + 2) * 2 + half + 1)
                        load_att(ahead, half)
                if has(i, -1):
                    sp.wait_ge(s["res"], i)
                    sp.dma_start(to, res[:]).then_inc(s["res_out"], 16)
                if has(i, 1):
                    sp.wait_ge(s["x_b"], i + 1)
                    sp.dma_start(xin[:, 1 - par], x_from).then_inc(s["x_in"], 16)
            over_steps(sp, body)
            sp.wait_ge(s["res_out"], NB * 16 + 16)

        @block.scalar
        def _(act):
            act.preload_act_table(ACT.Gelu_apprx_tanh)

            def att_hi(i, par, half):
                act.wait_ge(s["att_in%d" % half], i * 16 + 16)
                if has(i, -2):
                    act.wait_ge(s["proj"], i - 1)
                act.activation(att_s[:, par, 0, half * HP:(half + 1) * HP], att_in[:, half],
                               ACT.Identity).then_inc(s["att_hi"], 1)

            def gelu(i, hc):
                act.wait_ge(s["hid"], i * HC + hc + 1)
                act.activation(act_out[:, hc], hid[:, hc % 2], ACT.Gelu_apprx_tanh,
                               bias=b1[:, hc:hc + 1]).then_inc(s["gelu"], 1)

            def hid_hi(i, hc):
                act.wait_ge(s["gelu"], i * HC + hc + 1)
                if has(i, -1):
                    act.wait_ge(s["acc"], i)
                act.activation(hid_s[:, hc, 0], act_out[:, hc], ACT.Identity).then_inc(s["hid_hi"], 1)

            def hT_hi(i):
                for c in range(DC):
                    act.wait_ge(s["hT_ps"], i * DC + c + 1)
                    if c == 0 and has(i, -1):
                        act.wait_ge(s["hid"], i * HC)
                    act.activation(hT[:, c, 0], hT_ps[:, c], ACT.Identity).then_inc(s["hT_hi"], 1)

            act.wait_ge(s["att_in0"], 16)
            act.activation(att_s[:, 0, 0, 0:HP], att_in[:, 0], ACT.Identity).then_inc(s["att_hi"], 1)
            act.wait_ge(s["att_in1"], 16)
            act.activation(att_s[:, 0, 0, HP:PAIRS], att_in[:, 1], ACT.Identity).then_inc(s["att_hi"], 1)
            act.wait_ge(s["w_in"], 16 * NW)
            act.activation(wo[:, 0], wo_in[:], ACT.Identity).then_inc(s["w_hi"], 1)
            act.activation(w2[:, 0], w2_in[:], ACT.Identity).then_inc(s["w_hi"], 1)
            act.wait_ge(s["w1_scaled"], 1)
            act.activation(w1[:, 0], w1_in[:], ACT.Identity).then_inc(s["w_hi"], 1)
            for half in range(2):
                att_hi(1, 1, half)
            act.wait_ge(s["w_ready"], 3)

            def body(i, par):
                if has(i, -1):
                    gelu(i - 1, 0)
                    for hc in range(1, HC):
                        gelu(i - 1, hc)
                        hid_hi(i - 1, hc - 1)
                    hid_hi(i - 1, HC - 1)
                if has(i, 2):
                    att_hi(i + 2, par, 0)
                if has(i):
                    hT_hi(i)
                if has(i, 2):
                    att_hi(i + 2, par, 1)
            over_steps(act, body)

        @block.gpsimd
        def _(pool):
            pool.memset(mhalf[:], -0.5).then_inc(s["mhalf"], 1)
            pool.wait_ge(s["mhalf"], 1)
            pool.wait_ge(s["w_in"], 16 * NW)

            def add_rows(x, row):
                for t in range(NT):
                    o = pool.tensor_tensor(x[:, t], x[:, t], row[:], ALU.add)
                return o

            def z_bias(i, par):
                pool.wait_ge(s["z_in"], i * 16 + 16)
                add_rows(zin[:, par], bo).then_inc(s["zb"], 1)

            def x_bias(i, par):
                pool.wait_ge(s["x_in"], i * 16 + 16)
                add_rows(xin[:, par], b2).then_inc(s["x_b"], 1)
            z_bias(0, 0)

            def body(i, par):
                if has(i):
                    x_bias(i, par)
                    pool.wait_ge(s["stats"], i + 1)
                    stand_alone(pool, turns)
                    pool.tensor_scalar(rs[:], mv[:, :, 1], EPS, None, ALU.add).then_inc(s["veps"], 1)
                    pool.wait_ge(s["veps"], i + 1)
                    pool.tensor_tensor(rs[:], rs[:], mhalf[:], ALU.pow).then_inc(s["rstd"], 1)
                    pool.wait_ge(s["x_b"], i + 1)
                    pool.tensor_tensor(xin[:, par], xin[:, par], h[:], ALU.add).then_inc(s["x_h"], 1)
                if has(i, 1):
                    z_bias(i + 1, 1 - par)
            over_steps(pool, body)

        @block.vector
        def _(dve):
            def att_lo(i, par, half):
                dve.wait_ge(s["att_hi"], i * 2 + half + 1)
                g = slice(half * HP, (half + 1) * HP)
                dve.tensor_tensor(att_s[:, par, 1, g], att_in[:, half], att_s[:, par, 0, g].bitcast(F32),
                                  ALU.subtract).then_inc(s["att_lo"], 1)

            def hid_lo(i, hc):
                dve.wait_ge(s["hid_hi"], i * HC + hc + 1)
                dve.tensor_tensor(hid_s[:, hc, 1], act_out[:, hc], hid_s[:, hc, 0].bitcast(F32),
                                  ALU.subtract).then_inc(s["hid_lo"], 1)

            dve.sem_inc(s["res_out"], 16)
            att_lo(0, 0, 0)
            att_lo(0, 0, 1)
            dve.wait_ge(s["w_in"], 16 * NW)
            dve.wait_ge(s["w_hi"], 1)
            dve.tensor_tensor(wo[:, 1], wo_in[:], wo[:, 0].bitcast(F32), ALU.subtract).then_inc(s["w_ready"], 1)
            dve.wait_ge(s["b1_ps"], 1)
            dve.tensor_tensor(b1[:], hid[:, 0, 0:HC], b1_in[:], ALU.add)
            for c in range(DC):
                o = dve.tensor_scalar(w1_in[:, c], w1_in[:, c], ln[:, c, 0:1], None, ALU.mult)
            o.then_inc(s["w1_scaled"], 1)
            dve.wait_ge(s["w_hi"], 2)
            dve.tensor_tensor(w2[:, 1], w2_in[:], w2[:, 0].bitcast(F32), ALU.subtract).then_inc(s["w_ready"], 1)
            dve.wait_ge(s["w_hi"], 3)
            dve.tensor_tensor(w1[:, 1], w1_in[:], w1[:, 0].bitcast(F32), ALU.subtract).then_inc(s["w_ready"], 1)
            for half in range(2):
                att_lo(1, 1, half)

            def body(i, par):
                if has(i):
                    dve.wait_ge(s["proj"], i + 1)
                    dve.wait_ge(s["zb"], i + 1)
                    if has(i, -1):
                        dve.wait_ge(s["x_h"], i)
                    dve.tensor_tensor(h[:], proj[:], zin[:, par], ALU.add).then_inc(s["h"], 1)
                    dve.wait_ge(s["h"], i + 1)
                    for t in range(NT):
                        o = dve.bn_stats(st6[:, t], h[:, t])
                    o.then_inc(s["bn"], 1)
                    dve.wait_ge(s["bn"], i + 1)
                    stand_alone(dve, turns)
                    for t in range(NT):
                        o = dve.bn_aggr(mv[:, t], st6[:, t])
                    o.then_inc(s["stats"], 1)
                if has(i, -1):
                    hid_lo(i - 1, 0)
                    hid_lo(i - 1, 1)
                if has(i):
                    dve.wait_ge(s["rstd"], i + 1)
                    if has(i, -1):
                        dve.wait_ge(s["hT_ps"], i * DC)
                    for t in range(NT):
                        o = dve.tensor_scalar(hn[:, t], h[:, t], mv[:, t, 0:1], rs[:, t:t + 1],
                                              ALU.subtract, ALU.mult)
                    o.then_inc(s["hn"], 1)
                if has(i, -1):
                    hid_lo(i - 1, 2)
                    hid_lo(i - 1, 3)
                if has(i, 2):
                    att_lo(i + 2, par, 0)
                if has(i):
                    for c in range(DC):
                        dve.wait_ge(s["hT_hi"], i * DC + c + 1)
                        dve.tensor_tensor(hT[:, c, 1], hT_ps[:, c], hT[:, c, 0].bitcast(F32),
                                          ALU.subtract).then_inc(s["hT_lo"], 1)
                if has(i, 2):
                    att_lo(i + 2, par, 1)
                if has(i, -1):
                    dve.wait_ge(s["acc"], i)
                    dve.wait_ge(s["x_h"], i)
                    dve.wait_ge(s["res_out"], i * 16)
                    dve.tensor_tensor(res[:], acc[:], xin[:, 1 - par], ALU.add).then_inc(s["res"], 1)
            over_steps(dve, body)

        @block.tensor
        def _(pe):
            def project(i, par, tiles):
                for t in tiles:
                    for g in range(PAIRS):
                        for a, b in PARTS:
                            o = pe.matmul(proj[:, t], att_s[:, par, a, g, t * P:(t + 1) * P], wo[:, b, g],
                                          start=(t % 2 == 0 and g == 0 and (a, b) == (0, 0)),
                                          stop=(g == PAIRS - 1 and (a, b) == PARTS[-1]), skip_group_check=True)
                return o

            pe.wait_ge(s["w_in"], 16 * NW)
            for hc in range(HC):
                for c in range(DC):
                    o = pe.matmul(hid[:, 0, hc:hc + 1], w1_in[:, c, hc * P:(hc + 1) * P], ln[:, c, 1:2],
                                  start=(c == 0), stop=(c == DC - 1))
            o.then_inc(s["b1_ps"], 1)
            pe.wait_ge(s["att_lo"], 2)
            pe.wait_ge(s["w_ready"], 1)
            project(0, 0, range(NT)).then_inc(s["proj"], 1)
            pe.wait_ge(s["w_ready"], 3)

            def body(i, par):
                if has(i, 1):
                    pe.wait_ge(s["att_lo"], (i + 1) * 2 + 2)
                    pe.wait_ge(s["h"], i + 1)
                    project(i + 1, 1 - par, (0, 1))
                if has(i):
                    pe.wait_ge(s["hn"], i + 1)
                    if has(i, -1):
                        pe.wait_ge(s["hT_lo"], i * DC)
                    for c in range(DC):
                        for t in range(NT):
                            o = pe.transpose(hT_ps[:, c, t * P:(t + 1) * P], hn[:, t, c * P:(c + 1) * P], ident[:])
                        o.then_inc(s["hT_ps"], 1)
                if has(i, -1):
                    pe.wait_ge(s["hid_lo"], i * HC)
                    if not has(i):
                        pe.wait_ge(s["res"], i - 1)
                    for t in range(NT):
                        for hc in range(HC):
                            for a, b in PARTS:
                                o = pe.matmul(acc[:, t], hid_s[:, hc, a, t * P:(t + 1) * P], w2[:, b, hc],
                                              start=(t % 2 == 0 and hc == 0 and (a, b) == (0, 0)),
                                              stop=(hc == HC - 1 and (a, b) == PARTS[-1]), skip_group_check=True)
                    o.then_inc(s["acc"], 1)
                if has(i, 1):
                    project(i + 1, 1 - par, (2, 3)).then_inc(s["proj"], 1)
                if has(i):
                    pe.wait_ge(s["hT_lo"], i * DC + DC)
                    for hc in range(HC):
                        if hc >= 2 or has(i, -1):
                            pe.wait_ge(s["gelu"], i * HC + hc - 1)
                        n = 0
                        for c in range(DC):
                            for a, b in PARTS:
                                o = pe.matmul(hid[:, hc % 2], w1[:, a, c, hc * P:(hc + 1) * P], hT[:, c, b],
                                              start=(n == 0), stop=(n == 5))
                                n += 1
                        o.then_inc(s["hid"], 1)
            over_steps(pe, body)


def kernel(**inputs):
    import numpy as _np
    import concourse.bacc as _bacc
    from concourse import mybir as _mybir
    from concourse.bass_utils import run_bass_kernel_spmd as _run

    nc = _bacc.Bacc("TRN2", target_bir_lowering=False, num_devices=1)
    arrays, w = {}, {}

    def give(name, a):
        a = _np.ascontiguousarray(a)
        arrays[f"in_{name}"] = a
        w[name] = nc.dram_tensor(f"in_{name}", a.shape, _mybir.dt.from_np(a.dtype), kind="ExternalInput").ap()

    def scratch(name, shape, dt=F32):
        return nc.dram_tensor(name, shape, dt, kind="Internal").ap()

    i = {k: _np.asarray(v) for k, v in inputs.items()}
    rows_in = lambda a: a.reshape(a.shape[0] // P, P, -1).transpose(1, 0, 2).reshape(P, -1)
    give("x", i["L0_attn_x"].reshape(TOK, D))
    w1 = _np.concatenate([i["L0_ffn_W1"], i["L0_ffn_Ws1"][None]]).transpose(1, 0, 2).reshape(D, NE * HID)
    give("w1", rows_in(w1))
    give("w2", _np.concatenate([i["L0_ffn_W2"], i["L0_ffn_Ws2"][None]]).transpose(1, 0, 2).reshape(HID, NE * D))
    give("b1", _np.concatenate([i["L0_ffn_b1"], i["L0_ffn_bs1"][None]]).T)
    give("b2", _np.concatenate([i["L0_ffn_b2"], i["L0_ffn_bs2"][None]]))
    give("gw", rows_in(i["L0_ffn_gate_W"]))
    give("rscale", i["L0_ffn_route_scale"].reshape(1, 1))
    give("ident", _np.eye(P, dtype=_np.float32))
    give("iota", _np.tile(_np.arange(E, dtype=_np.float32), (P, 1)))
    sel = _np.zeros((P, E, P), _np.float32)
    for e in range(E):
        sel[e, e] = sel[E + e, e] = 1.0
    give("sel", sel.reshape(P, E * P))
    rows = _np.zeros((P, 2), _np.float32)
    rows[[*range(2 * E), 3 * E], 0] = 1.0
    rows[[*range(2 * E, 3 * E), 3 * E + 1], 1] = 1.0
    give("rows", rows)
    give("w_qkv", _np.stack([rows_in(i[f"L0_attn_W{c}"]).reshape(P, DC, AHD) for c in "qkv"]))
    give("ln_qkv", _np.stack([_np.stack([rows_in(i[f"L0_attn_ln{c}_{x}"][:, None]) for x in "sb"], -1) for c in "qkv"], 1))
    give("c_qkv", _np.stack([rows_in(i[f"L0_attn_b{c}"][:, None]) for c in "qkv"], 1))
    give("wo", rows_in(i["L0_attn_Wo"]).reshape(P, AHD // P, D))
    give("w1m", rows_in(i["L0_attn_W1"]).reshape(P, DC, MH))
    give("w2m", rows_in(i["L0_attn_W2"]).reshape(P, MH // P, D))
    give("ln_m", _np.stack([rows_in(i[f"L0_attn_lnm_{x}"][:, None]) for x in "sb"], -1))
    give("b1m", rows_in(i["L0_attn_b1"][:, None]))
    give("bo", i["L0_attn_bo"][None])
    give("b2m", i["L0_attn_b2"][None])
    x1, z, x2 = (scratch(n, (TOK, D)) for n in ("x1", "z", "x2"))
    zT = scratch("zT", (NB, P, DC, 2, BT))
    wqk = scratch("wqk", (AHD // P, P, 2, DC, 2, P))
    wv = scratch("wv", (AHD // P // 2, P, DC, 2, 2 * P))
    bias = scratch("bias", (P, AHD // P, 3))
    att = scratch("att", (AHD // P, P, TOK))
    out = nc.dram_tensor("out", (TOK, D), F32, kind="ExternalOutput").ap()

    with nc.semaphore("turns") as turns:
        ffn_phase(nc, turns, "f", w["x"], x1, w, {"z": z, "zT": zT})
        qkv_weights_phase(nc, "w", w, wqk, wv, bias)
        attention_phase(nc, turns, "a", w, zT, wqk, wv, bias, att)
        mlp_phase(nc, turns, "m", w, att, z, x1, x2)
        ffn_phase(nc, turns, "g", x2, out, w, None)
    r = _run(nc, [arrays], core_ids=[0])
    return r.results[0]["out"].reshape(B, S, D)
```

```python
from contextlib import ExitStack

import numpy as np

import concourse.bass as bass
from concourse import mybir

F32 = mybir.dt.float32
F32R = mybir.dt.float32r
U32 = mybir.dt.uint32
ALU = mybir.AluOpType
ACT = mybir.ActivationFunctionType
AX = mybir.AxisListType

P = 128
B, S, D = 4, 1024, 256
TOK = B * S
H, HD = 16, 64
AHD = H * HD
E, HID = 8, 128
NE = E + 1
MH = 2 * D
DC = D // P
BT = 512
NT = BT // P
NB = TOK // BT
EPS = 1e-5
MASK = -999.0
TOP = 2
E_NUM = float(np.float32(np.e))


def stand_alone(eng, turns):
    eng.sem_inc(turns, 1)


class Bank:

    def __init__(self, nc, ctx, tag):
        self.nc, self.ctx, self.tag = nc, ctx, tag

    def sb(self, name, shape, dt=F32):
        return self.ctx.enter_context(self.nc.sbuf_tensor(f"{self.tag}_{name}", shape, dt))

    def ps(self, name, shape):
        return self.ctx.enter_context(self.nc.psum_tensor(f"{self.tag}_{name}", shape, F32))

    def sem(self, name):
        return self.ctx.enter_context(self.nc.semaphore(f"{self.tag}_{name}"))


def ffn_phase(nc, turns, tag, src, dst, w, tail):
    PAIRS = AHD // P
    QS = float(D) ** -0.5
    with ExitStack() as ctx:
        m = Bank(nc, ctx, tag)
        ident = m.sb("ident", [P, P])
        sel_in = m.sb("sel_in", [P, E * P])
        sel = m.sb("sel", [P, E * P], F32R)
        w1_in = m.sb("w1_in", [P, DC * NE * HID])
        w1p = m.sb("w1p", [P, 2, DC * NE * HID], F32R)
        w2_in = m.sb("w2_in", [P, NE * D])
        w2p = m.sb("w2p", [P, 2, NE * D], F32R)
        gw_in = m.sb("gw_in", [P, DC * E])
        gwp = m.sb("gwp", [P, DC, 2, E], F32R)
        b1 = m.sb("b1", [P, NE])
        b2_in = m.sb("b2_in", [P, D])
        b2hi = m.sb("b2hi", [P, D], F32R)
        b2lo = m.sb("b2lo", [P, D], F32R)
        b2s = m.sb("b2s", [P, D], F32R)
        rows = m.sb("rows", [P, 2])
        rsc = m.sb("rsc", [P, 1])
        iota = m.sb("iota", [P, E])
        mhalf = m.sb("mhalf", [P, NT])
        ebase = m.sb("ebase", [P, NT * E])

        xin = m.sb("xin", [P, 2, NT, D])
        xres = m.sb("xres", [P, NT, D])
        st6 = m.sb("st6", [P, NT, 6])
        mv = m.sb("mv", [P, NT, 2])
        rs = m.sb("rs", [P, NT])
        xn = m.sb("xn", [P, NT, D])
        xT = m.sb("xT", [P, 2, DC, 2, BT], F32R)
        gl = m.sb("gl", [P, NT, E])
        nl = m.sb("nl", [P, NT, E])
        sg = m.sb("sg", [P, NT, E])
        top = m.sb("top", [P, NT, 8])
        idx = m.sb("idx", [P, NT, 8], U32)
        idf = m.sb("idf", [P, NT, 8])
        wt = m.sb("wt", [P, NT, TOP])
        ws = m.sb("ws", [P, NT])
        ga = m.sb("ga", [P, NT, E])
        gb_ = m.sb("gb_", [P, NT, E])
        ghi = m.sb("ghi", [P, NT, E], F32R)
        gpad = m.sb("gpad", [P, NT, P])
        gst = m.sb("gst", [P, 2, BT], F32R)
        act_out = m.sb("act_out", [P, 3, BT])
        gated = m.sb("gated", [P, 3, BT])
        hp = m.sb("hp", [P, 3, 2, BT], F32R)
        res = m.sb("res", [P, NT, D])
        if tail:
            zst6 = m.sb("zst6", [P, NT, 6])
            zmv = m.sb("zmv", [P, NT, 2])
            zrs = m.sb("zrs", [P, NT])
            zshift = m.sb("zshift", [P, NT])
            zz = m.sb("zz", [P, NT, D])
            zn = m.sb("zn", [P, NT, D])
            zT = m.sb("zT", [P, DC, 2, BT], F32R)
            qkv_in = m.sb("qkv_in", [P, 3, DC, AHD])
            qkv_s = m.sb("qkv_s", [P, DC, 2, AHD], F32R)
            ln = m.sb("ln", [P, 3, DC, 2])
            c_in = m.sb("c_in", [P, 3, PAIRS])
            bias = m.sb("bias", [P, PAIRS, 3])

        hid = m.ps("hid", [P, 2, BT])
        gbc = m.ps("gbc", [P, 2, BT])
        acc = m.ps("acc", [P, NT, D])
        aux = m.ps("aux", [P, 2, BT])

        names = ("veps gate_in w1_in w2_in zeroed gw_hi w1_hi w2_hi gw_lo w1_lo w2_lo b2_split b2_stack x_in xres bn stats rstd xn xT_ps xT_hi xT_lo logits neg expneg "
                 "gate gpad gT_ps gst hid gelu gbc gated h_hi h_lo out res res_out")
        if tail:
            names += " z_veps z_bn z_stats z_rs z_rstd z zn zT_ps zT_hi zT_lo zT_out z_out qkv_in qs qkv_hi qkv_lo qkv_out bias_ps bias"
        s = {n: m.sem(n) for n in names.split()}
        GC = 13

        def shared(e):
            return e == 0

        def weights_of(e):
            return (e - 1) % NE

        QKV_AT = {(True, 3): (0, 0), (True, 5): (0, 1), (False, 0): (1, 0), (False, 1): (1, 1),
                  (False, 6): (2, 0), (False, 7): (2, 1)}

        block = ctx.enter_context(nc.Block())

        def over_blocks(eng, body):
            body(0, 0, True, False)
            with eng.Fori(0, (NB - 2) // 2) as it:
                body(it * 2 + 1, 1, False, False)
                body(it * 2 + 2, 0, False, False)
            body(NB - 1, 1, False, True)

        def rows_of(ap, i):
            return ap.rearrange("(n t p) d -> n p t d", t=NT, p=P)[bass.ds(i, 1)].rearrange("n p t d -> p (n t) d")

        @block.sync
        def _(sp):
            sp.dma_start(xin[:, 0], rows_of(src, 0)).then_inc(s["x_in"], 16)
            for to, from_ in ((ident, w["ident"]), (gw_in, w["gw"]), (iota, w["iota"]),
                              (rsc, w["rscale"].partition_broadcast(P))):
                sp.dma_start(to[:], from_).then_inc(s["gate_in"], 16)
            for to, from_ in ((b1[:], w["b1"]), (w1_in[:], w["w1"]), (sel_in[:], w["sel"])):
                sp.dma_start(to, from_).then_inc(s["w1_in"], 16)
            sp.wait_ge(s["zeroed"], 1)
            for k in range(3):
                sp.dma_start(b2_in[k * E:(k + 1) * E], w["b2"][0:E]).then_inc(s["w2_in"], 16)
            for k in range(2):
                sp.dma_start(b2_in[3 * E + k:3 * E + k + 1], w["b2"][E:NE]).then_inc(s["w2_in"], 16)
            sp.dma_start(rows[:], w["rows"]).then_inc(s["w2_in"], 16)
            sp.dma_start(w2_in[:], w["w2"]).then_inc(s["w2_in"], 16)

            def has(i, ahead=0):
                return not isinstance(i, int) or 0 <= i + ahead < NB

            def fixed(i):
                return i if isinstance(i, int) else sp.snap(i)

            def store_zT(i, to):
                sp.wait_ge(s["zT_lo"], (i + 1) * DC)
                sp.dma_start(to, zT[:].bitcast(F32).rearrange("p c k t -> p (c k) t")).then_inc(s["zT_out"], 16)

            def zT_rows(i):
                return tail["zT"][bass.ds(i, 1)].rearrange("n p c k t -> p (n c k) t")

            def body(i, par):
                if has(i, 2):
                    ahead = rows_of(src, fixed(i + 2))
                if has(i):
                    again = rows_of(src, fixed(i))
                if has(i, -1):
                    to = rows_of(dst, fixed(i - 1))
                    if tail:
                        z_to = rows_of(tail["z"], fixed(i - 1))
                if tail and has(i, -2):
                    store_zT(i - 2, zT_rows(fixed(i - 2)))
                if has(i, -1):
                    sp.wait_ge(s["res"], i * 2)
                if has(i):
                    sp.dma_start(xres[:], again).then_inc(s["xres"], 16)
                if has(i, -1):
                    sp.dma_start(to, res[:]).then_inc(s["res_out"], 16)
                if has(i, 2):
                    sp.wait_ge(s["xn"], i + 2)
                    sp.dma_start(xin[:, par], ahead).then_inc(s["x_in"], 16)
                if tail and has(i, -1):
                    sp.wait_ge(s["z"], i)
                    sp.dma_start(z_to, zz[:]).then_inc(s["z_out"], 16)

            def store_qkv(k):
                sp.wait_ge(s["qkv_lo"], (k + 1) * DC)
                sp.dma_start(tail["w_split"][k], qkv_s[:].bitcast(F32)).then_inc(s["qkv_out"], 16)

            sp.wait_ge(s["xn"], 1)
            sp.dma_start(xin[:, 1], rows_of(src, 1)).then_inc(s["x_in"], 16)
            if tail:
                sp.dma_start(ln[:], w["ln_qkv"]).then_inc(s["qkv_in"], 16)
                sp.dma_start(c_in[:], w["c_qkv"]).then_inc(s["qkv_in"], 16)
                for k in range(3):
                    sp.dma_start(qkv_in[:, k], w["w_qkv"][k]).then_inc(s["qkv_in"], 16)
            body(0, 0)
            if tail:
                store_qkv(0)
            body(1, 1)
            with sp.Fori(0, (NB - 4) // 2) as it:
                body(it * 2 + 2, 0)
                body(it * 2 + 3, 1)
            body(NB - 2, 0)
            if tail:
                store_qkv(1)
            body(NB - 1, 1)
            if tail:
                store_qkv(2)
            body(NB, 0)
            sp.wait_ge(s["res_out"], NB * 16 + 16)
            if tail:
                store_zT(NB - 1, zT_rows(NB - 1))
                sp.wait_ge(s["bias"], 3)
                sp.dma_start(tail["bias"], bias[:]).then_inc(s["qkv_out"], 16)
                sp.wait_ge(s["qkv_out"], 16 * 4)
                sp.wait_ge(s["z_out"], NB * 16 + 16)
                sp.wait_ge(s["zT_out"], NB * 16 + 16)

        @block.scalar
        def _(act):
            if tail:
                act.sem_inc(s["z_out"], 16)
                act.sem_inc(s["zT_out"], 16)
            act.preload_act_table(ACT.Gelu)
            act.wait_ge(s["gate_in"], 64)
            act.activation(gwp[:, :, 0, :], gw_in[:].rearrange("p (c e) -> p c e", c=DC), ACT.Identity)\
                .then_inc(s["gw_hi"], 1)

            def normalise(to, x, rstd, shift_, counted):
                for t in range(NT):
                    o = act.activation(to[:, t], x[:, t], ACT.Identity, bias=shift_[:, t:t + 1], scale=rstd[:, t:t + 1])
                o.then_inc(counted, 1)

            def z_norm(i):
                act.wait_ge(s["z_rstd"], i * 2 + 1)
                act.wait_ge(s["z_out"], i * 16 + 16)
                normalise(zz, res, zrs, zshift, s["z"])

            def zn_norm(i):
                act.wait_ge(s["z_rstd"], i * 2 + 2)
                normalise(zn, zz, zrs, zshift, s["zn"])

            def qkv_hi(k, c):
                if k == 0 and c == 0:
                    act.wait_ge(s["qkv_in"], 80)
                    act.wait_ge(s["qs"], 1)
                if k > 0 and c == 0:
                    act.wait_ge(s["qkv_out"], k * 16)
                act.activation(qkv_s[:, c, 0], qkv_in[:, k, c], ACT.Identity, scale=ln[:, k, c, 0:1])\
                    .then_inc(s["qkv_hi"], 1)

            def xt_hi(i, par):
                for c in range(DC):
                    act.wait_ge(s["xT_ps"], i * DC + c + 1)
                    act.activation(xT[:, par, c, 0], aux[:, c], ACT.Identity).then_inc(s["xT_hi"], 1)

            def zt_hi(i):
                for c in range(DC):
                    act.wait_ge(s["zT_ps"], i * DC + c + 1)
                    if c == 0:
                        act.wait_ge(s["zT_out"], i * 16 + 16)
                    act.activation(zT[:, c, 0], aux[:, c], ACT.Identity).then_inc(s["zT_hi"], 1)

            def hi(i, e, first):
                if e >= 3 or not first:
                    act.wait_ge(s["out"], i * NE + e - 2)
                if shared(e):
                    act.wait_ge(s["gelu"], i * NE + e + 1)
                    from_ = act_out
                else:
                    act.wait_ge(s["gated"], i * E + e)
                    from_ = gated
                act.activation(hp[:, e % 3, 0], from_[:, e % 3], ACT.Identity).then_inc(s["h_hi"], 1)

            def body(i, par, first, last):
                for e in range(NE):
                    act.wait_ge(s["hid"], i * NE + e + 1)
                    if e >= 3 or not first:
                        act.wait_ge(s["h_lo"], i * NE + e - 2)
                    act.activation(act_out[:, e % 3], hid[:, (par + e) % 2], ACT.Gelu,
                                   bias=b1[:, weights_of(e):weights_of(e) + 1]).then_inc(s["gelu"], 1)
                    if e > 0:
                        hi(i, e - 1, first)
                    elif not first:
                        hi(i - 1, E, False)
                    if e == 2 and not last:
                        xt_hi(i + 1, 1 - par)
                    if e == 4 and tail and not first:
                        z_norm(i - 1)
                    if e == 7 and tail and not first:
                        zn_norm(i - 1)
                    if e == 8 and tail and not first:
                        zt_hi(i - 1)
                    if tail and (first or last) and (first, e) in QKV_AT:
                        qkv_hi(*QKV_AT[first, e])
            xt_hi(0, 0)
            act.wait_ge(s["w1_in"], 48)
            act.activation(w1p[:, 0], w1_in[:], ACT.Identity)
            act.activation(sel[:], sel_in[:], ACT.Identity).then_inc(s["w1_hi"], 1)
            act.wait_ge(s["w2_in"], 112)
            act.activation(b2hi[:], b2_in[:], ACT.Identity)
            act.activation(w2p[:, 0], w2_in[:], ACT.Identity).then_inc(s["w2_hi"], 1)
            over_blocks(act, body)
            hi(NB - 1, E, False)
            if tail:
                z_norm(NB - 1)
                zn_norm(NB - 1)
                zt_hi(NB - 1)

        @block.gpsimd
        def _(pool):
            pool.memset(b2_in[:], 0.0).then_inc(s["zeroed"], 1)
            pool.memset(gpad[:], 0.0).then_inc(s["zeroed"], 1)
            pool.wait_ge(s["zeroed"], 2)
            pool.memset(gpad[:, :, 3 * E:3 * E + 2], 1.0)
            pool.memset(mhalf[:], -0.5)
            pool.memset(ebase[:], E_NUM).then_inc(s["zeroed"], 1)
            pool.wait_ge(s["zeroed"], 3)


            def rstds(stats, ready, rstd, veps, powed, n, minus_mean=None):
                pool.wait_ge(ready, n)
                stand_alone(pool, turns)
                if minus_mean is not None:
                    pool.tensor_scalar(minus_mean[:], stats[:, :, 0], -1.0, 0.0, ALU.mult, ALU.add)
                pool.tensor_scalar(rstd[:], stats[:, :, 1], EPS, None, ALU.add).then_inc(veps, 1)
                pool.wait_ge(veps, n)
                pool.tensor_tensor(rstd[:], rstd[:], mhalf[:], ALU.pow).then_inc(powed, 1)

            def x_rstd(i):
                rstds(mv, s["stats"], rs, s["veps"], s["rstd"], i + 1)

            def z_rstds(i, which):
                n = i * 2 + which + 1
                rstds(zmv, s["z_stats"], zrs, s["z_veps"], s["z_rs"], n, zshift)
                pool.wait_ge(s["z_rs"], n)
                pool.tensor_tensor(zshift[:], zshift[:], zrs[:], ALU.mult).then_inc(s["z_rstd"], 1)

            def expneg(i):
                pool.wait_ge(s["neg"], i + 1)
                pool.tensor_tensor(nl[:].rearrange("p t e -> p (t e)"), ebase[:],
                                   nl[:].rearrange("p t e -> p (t e)"), ALU.pow).then_inc(s["expneg"], 1)

            def body(i, par, first, last):
                if not last:
                    x_rstd(i + 1)
                if tail and not first:
                    z_rstds(i - 1, 0)
                if not last:
                    expneg(i + 1)
                if tail and not first:
                    z_rstds(i - 1, 1)
            x_rstd(0)
            expneg(0)
            over_blocks(pool, body)
            if tail:
                z_rstds(NB - 1, 0)
                z_rstds(NB - 1, 1)

        @block.vector
        def _(dve):
            def norm_stats(x, t6, out, bn, stats, nbn):
                for t in range(NT):
                    o = dve.bn_stats(t6[:, t], x[:, t])
                o.then_inc(bn, 1)
                dve.wait_ge(bn, nbn)
                stand_alone(dve, turns)
                for t in range(NT):
                    o = dve.bn_aggr(out[:, t], t6[:, t])
                o.then_inc(stats, 1)

            def x_stats(i, par):
                dve.wait_ge(s["x_in"], i * 16 + 16)
                norm_stats(xin[:, par], st6, mv, s["bn"], s["stats"], i + 1)

            def x_norm(i, par, first):
                dve.wait_ge(s["rstd"], i + 1)
                if not first:
                    dve.wait_ge(s["xT_ps"], i * DC)
                for t in range(NT):
                    o = dve.tensor_scalar(xn[:, t], xin[:, par, t], mv[:, t, 0:1], rs[:, t:t + 1],
                                          ALU.subtract, ALU.mult)
                o.then_inc(s["xn"], 1)

            def xt_lo(i, par):
                for c in range(DC):
                    dve.wait_ge(s["xT_hi"], i * DC + c + 1)
                    dve.tensor_tensor(xT[:, par, c, 1], aux[:, c], xT[:, par, c, 0].bitcast(F32),
                                      ALU.subtract).then_inc(s["xT_lo"], 1)

            def neg_logits(i):
                ps = aux[:, 0, 0:NT * 2 * E].rearrange("p (t k e) -> p t k e", t=NT, k=2)
                dve.wait_ge(s["logits"], i + 1)
                dve.tensor_scalar(gl[:], ps[:, :, 1], -1.0, None, ALU.mult).then_inc(s["gate"], 1)
                dve.wait_ge(s["gate"], i * GC + 1)
                dve.scalar_tensor_tensor(out=nl[:], in0=ps[:, :, 0], scalar=-1.0, in1=gl[:],
                                         op0=ALU.mult, op1=ALU.add).then_inc(s["neg"], 1)

            def linker(n):
                count = [n]

                def link(o):
                    o.then_inc(s["gate"], 1)
                    count[0] = count[0] + 1
                    dve.wait_ge(s["gate"], count[0])
                return link

            def choices(i):
                link = linker(i * GC + 1)
                dve.wait_ge(s["expneg"], i + 1)
                link(dve.tensor_scalar(sg[:], nl[:], 1.0, None, ALU.add))
                link(dve.reciprocal(sg[:], sg[:]))
                link(dve.tensor_scalar(sg[:], sg[:], rsc[:, 0:1], None, ALU.mult))
                stand_alone(dve, turns)
                for t in range(NT):
                    o = dve.max(top[:, t], sg[:, t])
                link(o)
                stand_alone(dve, turns)
                for t in range(NT):
                    o = dve.max_index(idx[:, t], top[:, t], sg[:, t])
                link(o)

            def gates(i):
                link = linker(i * GC + 6)
                dve.tensor_tensor(ws[:], top[:, :, 0], top[:, :, 1], ALU.add)
                link(dve.tensor_copy(idf[:], idx[:]))
                link(dve.reciprocal(ws[:], ws[:]))
                for k in range(TOP):
                    o = dve.tensor_tensor(wt[:, :, k], top[:, :, k], ws[:], ALU.mult)
                link(o)
                places = iota[:].unsqueeze(1).broadcast_to([P, NT, E])
                dve.tensor_tensor(ga[:], places, idf[:, :, 0:1].broadcast_to([P, NT, E]), ALU.is_equal)
                link(dve.tensor_tensor(gb_[:], places, idf[:, :, 1:2].broadcast_to([P, NT, E]), ALU.is_equal))
                dve.tensor_tensor(ga[:], ga[:], wt[:, :, 0:1].broadcast_to([P, NT, E]), ALU.mult)
                link(dve.tensor_tensor(gb_[:], gb_[:], wt[:, :, 1:2].broadcast_to([P, NT, E]), ALU.mult))
                link(dve.tensor_tensor(ga[:], ga[:], gb_[:], ALU.add))
                dve.tensor_copy(ghi[:], ga[:]).then_inc(s["gate"], 1)
                dve.wait_ge(s["gate"], (i + 1) * GC)
                g = ghi[:].bitcast(F32)
                dve.tensor_copy(gpad[:, :, 0:E], g)
                dve.tensor_copy(gpad[:, :, 2 * E:3 * E], g)
                dve.tensor_tensor(gpad[:, :, E:2 * E], ga[:], g, ALU.subtract).then_inc(s["gpad"], 1)

            def gate_stack(i, par):
                dve.wait_ge(s["gT_ps"], i + 1)
                dve.tensor_copy(gst[:, par], aux[:, 1]).then_inc(s["gst"], 1)

            def gating(i, e):
                dve.wait_ge(s["gelu"], i * NE + e + 1)
                dve.wait_ge(s["gbc"], i * E + e)
                dve.tensor_tensor(gated[:, e % 3], gbc[:, (e - 1) % 2], act_out[:, e % 3],
                                  ALU.mult).then_inc(s["gated"], 1)

            def lo(i, e):
                dve.wait_ge(s["h_hi"], i * NE + e + 1)
                from_ = act_out if shared(e) else gated
                dve.tensor_tensor(hp[:, e % 3, 1], from_[:, e % 3], hp[:, e % 3, 0].bitcast(F32),
                                  ALU.subtract).then_inc(s["h_lo"], 1)

            def result(i):
                dve.wait_ge(s["out"], i * NE + NE)
                dve.wait_ge(s["xres"], i * 16 + 16)
                dve.wait_ge(s["res_out"], i * 16 + 16)
                for h in range(2):
                    t = slice(2 * h, 2 * h + 2)
                    dve.scalar_tensor_tensor(out=res[:, t], in0=acc[:, t], scalar=0.5,
                                             in1=xres[:, t], op0=ALU.mult, op1=ALU.add).then_inc(s["res"], 1)

            def z_stats(i):
                dve.wait_ge(s["res"], i * 2 + 2)
                norm_stats(res, zst6, zmv, s["z_bn"], s["z_stats"], i * 2 + 1)

            def zz_stats(i):
                dve.wait_ge(s["z"], i + 1)
                norm_stats(zz, zst6, zmv, s["z_bn"], s["z_stats"], i * 2 + 2)

            def qkv_lo(k, c):
                dve.wait_ge(s["qkv_hi"], k * DC + c + 1)
                dve.scalar_tensor_tensor(out=qkv_s[:, c, 1], in0=qkv_in[:, k, c], scalar=ln[:, k, c, 0:1],
                                         in1=qkv_s[:, c, 0].bitcast(F32), op0=ALU.mult, op1=ALU.subtract)\
                    .then_inc(s["qkv_lo"], 1)

            def zt_lo(i):
                for c in range(DC):
                    dve.wait_ge(s["zT_hi"], i * DC + c + 1)
                    dve.tensor_tensor(zT[:, c, 1], aux[:, c], zT[:, c, 0].bitcast(F32),
                                      ALU.subtract).then_inc(s["zT_lo"], 1)

            dve.sem_inc(s["res_out"], 16)
            x_stats(0, 0)
            x_norm(0, 0, True)
            dve.wait_ge(s["gw_hi"], 1)
            dve.tensor_tensor(gwp[:, :, 1, :], gw_in[:].rearrange("p (c e) -> p c e", c=DC),
                              gwp[:, :, 0, :].bitcast(F32), ALU.subtract).then_inc(s["gw_lo"], 1)
            xt_lo(0, 0)
            dve.wait_ge(s["w1_hi"], 1)
            dve.tensor_tensor(w1p[:, 1], w1_in[:], w1p[:, 0].bitcast(F32), ALU.subtract).then_inc(s["w1_lo"], 1)
            neg_logits(0)
            dve.wait_ge(s["w2_hi"], 1)
            dve.tensor_tensor(w2p[:, 1], w2_in[:], w2p[:, 0].bitcast(F32), ALU.subtract).then_inc(s["w2_lo"], 1)
            dve.tensor_tensor(b2lo[:], b2_in[:], b2hi[:].bitcast(F32), ALU.subtract).then_inc(s["b2_split"], 1)
            dve.wait_ge(s["b2_split"], 1)
            dve.tensor_scalar(b2_in[:], b2lo[:].bitcast(F32), rows[:, 1:2], None, ALU.mult).then_inc(s["b2_split"], 1)
            dve.wait_ge(s["b2_split"], 2)
            dve.scalar_tensor_tensor(out=b2s[:], in0=b2hi[:].bitcast(F32), scalar=rows[:, 0:1], in1=b2_in[:],
                                     op0=ALU.mult, op1=ALU.add).then_inc(s["b2_stack"], 1)
            dve.wait_ge(s["zeroed"], 3)
            choices(0)
            gates(0)

            def body(i, par, first, last):
                for e in range(NE):
                    if not shared(e):
                        gating(i, e)
                    if e == 1 and not first:
                        result(i - 1)
                    if e > 0:
                        lo(i, e - 1)
                    elif not first:
                        lo(i - 1, NE - 1)
                    if e == 0:
                        gate_stack(i, par)
                    if not last:
                        if e == 0:
                            x_stats(i + 1, 1 - par)
                        if e == 1:
                            x_norm(i + 1, 1 - par, False)
                        if e == 2:
                            xt_lo(i + 1, 1 - par)
                        if e == 4:
                            neg_logits(i + 1)
                    if tail and not first:
                        if e == 3:
                            z_stats(i - 1)
                        if e == 5:
                            zz_stats(i - 1)
                    if not last:
                        if e == 7:
                            choices(i + 1)
                        if e == 8:
                            gates(i + 1)
                    if tail and not first and e == 8:
                        zt_lo(i - 1)
                    if tail and first and e == 2:
                        dve.wait_ge(s["qkv_in"], 80)
                        dve.tensor_scalar(ln[:, 0, :, 0], ln[:, 0, :, 0], QS, None, ALU.mult).then_inc(s["qs"], 1)
                        dve.wait_ge(s["qs"], 1)
                    if tail and (first or last) and (first, e) in QKV_AT:
                        qkv_lo(*QKV_AT[first, e])
            over_blocks(dve, body)
            lo(NB - 1, E)
            result(NB - 1)
            if tail:
                z_stats(NB - 1)
                zz_stats(NB - 1)
                zt_lo(NB - 1)
                dve.wait_ge(s["bias_ps"], 1)
                for k in range(3):
                    o = dve.tensor_tensor(bias[:, :, k], gbc[:, 0, k * PAIRS:(k + 1) * PAIRS], c_in[:, k], ALU.add)
                o.then_inc(s["bias"], 1)
                dve.wait_ge(s["bias"], 1)
                dve.tensor_scalar(bias[:, :, 0], bias[:, :, 0], QS, None, ALU.mult).then_inc(s["bias"], 2)

        @block.tensor
        def _(pe):
            def transposes(i, from_, ready, done):
                pe.wait_ge(ready, i + 1)
                for c in range(DC):
                    for t in range(NT):
                        o = pe.transpose(aux[:, c, t * P:(t + 1) * P], from_[:, t, c * P:(c + 1) * P], ident[:])
                    o.then_inc(done, 1)

            def logits(i, par):
                pe.wait_ge(s["xT_lo"], i * DC + DC)
                for t in range(NT):
                    for c in range(DC):
                        for k in range(2):
                            n = 2 * E if k == 0 else E
                            o = pe.matmul(aux[:, 0, t * 2 * E:t * 2 * E + n],
                                          xT[:, par, c, k, t * P:(t + 1) * P],
                                          gwp[:, c].rearrange("p k e -> p (k e)")[:, 0:n],
                                          start=(t == 0 and c == 0 and k == 0), stop=(c == DC - 1 and k == 1),
                                          skip_group_check=True)
                o.then_inc(s["logits"], 1)

            def gates_up(i):
                pe.wait_ge(s["gpad"], i + 1)
                for t in range(NT):
                    o = pe.transpose(aux[:, 1, t * P:(t + 1) * P], gpad[:, t], ident[:])
                o.then_inc(s["gT_ps"], 1)

            PARTS = ((0, 0), (0, 1), (1, 0))

            def first_layer(i, e, par, first):
                if e >= 2 or not first:
                    pe.wait_ge(s["gelu"], i * NE + e - 1)
                n = 0
                x = weights_of(e)
                for c in range(DC):
                    for a, b in PARTS:
                        o = pe.matmul(hid[:, (par + e) % 2], w1p[:, a, (c * NE + x) * HID:(c * NE + x + 1) * HID],
                                      xT[:, par, c, b], start=(n == 0), stop=(n == 5))
                        n += 1
                o.then_inc(s["hid"], 1)

            def gate(i, e, par, first):
                if shared(e):
                    return
                if e == 1:
                    pe.wait_ge(s["gst"], i + 1)
                if e >= 3 or not first:
                    pe.wait_ge(s["gated"], i * E + e - 2)
                pe.matmul(gbc[:, (e - 1) % 2], sel[:, (e - 1) * P:e * P], gst[:, par],
                          start=True, stop=True).then_inc(s["gbc"], 1)

            def second_layer(i, e, par, first):
                if e == 0:
                    if first:
                        pe.wait_ge(s["w2_lo"], 1)
                        pe.wait_ge(s["b2_stack"], 1)
                    for t in range(NT):
                        if not first and t % 2 == 0:
                            pe.wait_ge(s["res"], i * 2 - 1 + t // 2)
                        pe.matmul(acc[:, t], gst[:, par, t * P:(t + 1) * P], b2s[:],
                                  start=(t % 2 == 0), stop=False, skip_group_check=True)
                pe.wait_ge(s["h_lo"], i * NE + e + 1)
                x = weights_of(e)
                for t in range(NT):
                    for a, b in PARTS:
                        o = pe.matmul(acc[:, t], hp[:, e % 3, a, t * P:(t + 1) * P],
                                      w2p[:, b, x * D:(x + 1) * D], start=False, stop=(e == NE - 1 and (a, b) == (1, 0)),
                                      skip_group_check=True)
                o.then_inc(s["out"], 1)

            def body(i, par, first, last):
                for e in range(NE):
                    first_layer(i, e, par, first)
                    if e != 1:
                        gate(i, e, par, first)
                    if e >= 2:
                        second_layer(i, e - 2, par, first)
                    elif not first:
                        second_layer(i - 1, E - 1 + e, 1 - par, False)
                    if e == 1:
                        gates_up(i)
                        gate(i, e, par, first)
                    if not last:
                        if e == 2:
                            transposes(i + 1, xn, s["xn"], s["xT_ps"])
                        if e == 3:
                            logits(i + 1, 1 - par)
                    if e == 8 and tail and not first:
                        if not last:
                            pe.wait_ge(s["neg"], i + 2)
                        transposes(i - 1, zn, s["zn"], s["zT_ps"])

            pe.wait_ge(s["gate_in"], 64)
            transposes(0, xn, s["xn"], s["xT_ps"])
            pe.wait_ge(s["gw_lo"], 1)
            logits(0, 0)
            pe.wait_ge(s["w1_lo"], 1)
            over_blocks(pe, body)
            second_layer(NB - 1, E - 1, 1, False)
            second_layer(NB - 1, E, 1, False)
            if tail:
                for k in range(3):
                    for g in range(PAIRS):
                        for c in range(DC):
                            o = pe.matmul(gbc[:, 0, k * PAIRS + g:k * PAIRS + g + 1],
                                          qkv_in[:, k, c, g * P:(g + 1) * P], ln[:, k, c, 1:2],
                                          start=(c == 0), stop=(c == DC - 1))
                o.then_inc(s["bias_ps"], 1)
                pe.wait_ge(s["zT_lo"], (NB - 1) * DC)
                transposes(NB - 1, zn, s["zn"], s["zT_ps"])


def attention_phase(nc, turns, tag, w, zT, w_split, bias, att):
    PAIRS = AHD // P
    STEPS = 16
    ITER = 2 * STEPS
    NIT = B * PAIRS // 2
    LAG = 3
    QT = S // P
    NP = 4
    BLOCKS = 8
    with ExitStack() as ctx:
        m = Bank(nc, ctx, tag)
        ident = m.sb("ident", [P, P])
        bsb = m.sb("bsb", [P, PAIRS, 3])
        bqk_s = m.sb("bqk_s", [P, 2])
        wqk_s = m.sb("wqk_s", [P, 2, DC, 2, P], F32R)
        wv_s = m.sb("wv_s", [P, DC, 2, 2 * P], F32R)
        z_s = m.sb("z_s", [P, DC * 2, 2, BT], F32R)
        staged = m.sb("staged", [P, 2, BT])
        q_s = m.sb("q_s", [P, 2, 2, S], F32R)
        k_s = m.sb("k_s", [P, 2, 2, 2, S], F32R)
        v_s = m.sb("v_s", [P, 2, QT, 4, HD], F32R)
        v_b = m.sb("v_b", [P, QT, 4, HD], F32R)
        pr = m.sb("pr", [P, NP, S])
        nmax = m.sb("nmax", [P, NP])
        den = m.sb("den", [P, NP])
        rden = m.sb("rden", [P, NP])
        pT = m.sb("pT", [P, 2, 2, QT, BT], F32R)
        half = m.sb("half", [P, 2, BT])
        ao = m.sb("ao", [P, 2, 2, BT])
        sc = m.ps("sc", [P, 2, S])
        tr = m.ps("tr", [P, 2, BT])
        pj = m.ps("pj", [P, BT])
        ov = m.ps("ov", [P, BT])

        s = {n: m.sem(n) for n in (
            "const first_z z_in wqk_in wv_in v_in k_dup sc masked negmax exp rden normed tr tr_hi tr_lo "
            "pj staged head0_hi head1_hi head0_lo v_hi first_split split pv half ov_read att att_out").split()}

        PROJ = {2: ("Q", 0), 5: ("Q", 1), 8: ("K", 0), 11: ("K", 1)}
        VALS = {7: ("V", 0), 9: ("V", 1), 12: ("V", 2), 14: ("V", 3)}
        FIRST = [("Q", 0), ("Q", 1), ("K", 0), ("K", 1), ("V", 0), ("V", 1), ("V", 2), ("V", 3)]
        PLAN = [PROJ.get(k % STEPS) or (VALS.get(k % STEPS) if k >= STEPS else None) for k in range(ITER)]
        PER = sum(x is not None for x in PLAN)
        assert PER % 2 == 0 and len(FIRST) % 2 == 0

        def before(it, k):
            return it * PER + len(FIRST) + sum(x is not None for x in PLAN[:k])

        def ends(it):
            return isinstance(it, int) and it == NIT - 1

        def piece_at(it, k):
            return PLAN[k] and not (ends(it) and k >= STEPS) and (*PLAN[k], before(it, k), (before(0, k)) % 2)

        def over_iterations(eng, body):
            body(0, True, False)
            with eng.Fori(1, NIT - 1) as it:
                body(it, False, False)
            body(NIT - 1, False, False)
            body(NIT, False, True)

        def steps(last):
            return range(LAG + 5 if last else ITER)

        def transposes_at(k, first, last):
            return not (first and k < LAG) and not (last and k >= LAG)

        def values_at(k, first):
            j = k - LAG - 4
            if first and j < 0:
                return None
            block = j // 4
            return (block // 4) % 2, (block // 2) % 2, block, j % 4

        def finished_at(k, first):
            v = values_at(k - 1, first) if k > 0 or not first else None
            return v if v and v[3] == 3 else None

        def bank_of(n, start):
            return ov if start and n % 2 else pj

        block_ = ctx.enter_context(nc.Block())

        def pair_of(it, slot):
            return it // 4, (it % 4) * 2 + slot

        def after(it):
            return (it + 1) % NIT

        @block_.sync
        def _(sp):
            def fixed(x):
                return x if isinstance(x, int) else sp.snap(x)

            def load_z(it):
                b = fixed((it // 4) * 2)
                for half_ in range(2):
                    sp.dma_start(z_s[:, :, half_].bitcast(F32),
                                 zT[bass.ds(b + half_, 1)].rearrange("h p c k t -> p (h c k) t")).then_inc(s["z_in"], 16)

            def load_wqk(it, slot):
                g = fixed((it % 4) * 2 + slot)
                f = fixed(g * P)
                for k in range(2):
                    sp.dma_start(wqk_s[:, k].bitcast(F32).rearrange("p c l f -> p (c l) f"),
                                 w_split[k].rearrange("p c l f -> p (c l) f")[:, :, bass.ds(f, P)]).then_inc(s["wqk_in"], 16)
                sp.dma_start(bqk_s[:], bias[:, bass.ds(g, 1), 0:2].rearrange("p g k -> p (g k)"))\
                    .then_inc(s["wqk_in"], 16)

            def load_wv(it):
                f = fixed((it % 4) * 2 * P)
                sp.dma_start(wv_s[:].bitcast(F32).rearrange("p c l f -> p (c l) f"),
                             w_split[2].rearrange("p c l f -> p (c l) f")[:, :, bass.ds(f, 2 * P)]).then_inc(s["wv_in"], 16)

            def double_k(slot):
                for head, (a, b) in enumerate(((0, HD), (HD, 0))):
                    sp.dma_start(k_s[b:b + HD, slot, head].bitcast(F32), k_s[a:a + HD, slot, head].bitcast(F32))\
                        .then_inc(s["k_dup"], 16)

            def move_v():
                sp.dma_start(v_s[:, 1].bitcast(F32).rearrange("p t k f -> p (t k f)"),
                             v_b[:].bitcast(F32).rearrange("p t k f -> p (t k f)")).then_inc(s["v_in"], 16)

            def store(it, slot, pairs):
                b, hp = pair_of(it, slot)
                to = att[bass.ds(fixed(hp), 1), :, bass.ds(fixed(b * S), S)].rearrange("g p t -> p (g t)")
                sp.wait_ge(s["att"], pairs)
                sp.dma_start(to, ao[:, slot].rearrange("p h t -> p (h t)")).then_inc(s["att_out"], 16)

            sp.dma_start(ident[:], w["ident"]).then_inc(s["const"], 16)
            sp.dma_start(bsb[:], bias).then_inc(s["const"], 16)
            load_wqk(0, 0)
            for half_, landed in enumerate(("first_z", "z_in")):
                sp.dma_start(z_s[:, :, half_].bitcast(F32), zT[half_].rearrange("p c k t -> p (c k) t"))\
                    .then_inc(s[landed], 16)
            load_wv(0)
            sp.wait_ge(s["first_split"], 4)
            double_k(0)
            load_wqk(0, 1)
            sp.wait_ge(s["split"], 8)
            load_wv(1)
            move_v()

            def body(it, first, last):
                if not first:
                    if not last:
                        sp.wait_ge(s["pv"], it * BLOCKS)
                        move_v()
                    store(it - 1, 1, it * 2)
                if last:
                    return
                sp.wait_ge(s["split"], before(it, STEPS))
                double_k(1)
                if not ends(it):
                    load_wqk(after(it), 0)
                    load_z(after(it))
                store(it, 0, it * 2 + 1)
                if ends(it):
                    return
                sp.wait_ge(s["split"], before(it, STEPS + 12))
                double_k(0)
                load_wqk(after(it), 1)
                sp.wait_ge(s["split"], before(it, ITER))
                load_wv(after(it + 1))
            over_iterations(sp, body)
            sp.wait_ge(s["att_out"], 16 * B * PAIRS)
            sp.wait_ge(s["wv_in"], 16 * (NIT + 1))
            sp.wait_ge(s["wqk_in"], 48 * 2 * NIT)
            sp.wait_ge(s["z_in"], 32 * (NIT - 1) + 16)
            sp.wait_ge(s["k_dup"], 32 * 2 * NIT)

        def rows_of_head(head):
            return slice(head * HD, head * HD + HD)

        def parts_of(kind, part, slot, pair_slot):
            cols = slice(part * BT, part * BT + BT)
            r0, r1 = rows_of_head(0), rows_of_head(1)
            if kind == "Q":
                hi = [q_s[r0, pair_slot, 0, cols], q_s[r1, pair_slot, 1, cols]]
                lo = [q_s[r1, pair_slot, 0, cols], q_s[r0, pair_slot, 1, cols]]
            else:
                hi = [k_s[r0, pair_slot, 0, 0, cols], k_s[r1, pair_slot, 1, 0, cols]]
                lo = [k_s[r0, pair_slot, 0, 1, cols], k_s[r1, pair_slot, 1, 1, cols]]
            return (staged[r0, slot], staged[r1, slot]), hi, lo

        @block_.scalar
        def _(act):
            act.preload_act_table(ACT.Exp)
            act.wait_ge(s["const"], 32)

            def stage(kind, n, slot, start):
                act.wait_ge(s["pj"], n + 1)
                if not start or n > 5:
                    act.wait_ge(s["split"], n - 1)
                elif n >= 2:
                    act.wait_ge(s["first_split"], n - 1)
                if kind == "V":
                    o = act.activation(staged[:, slot], bank_of(n, start)[:], ACT.Identity)
                else:
                    o = act.activation(staged[:, slot], bank_of(n, start)[:], ACT.Identity, bias=bqk_s[:, "QK".index(kind):"QK".index(kind) + 1])
                o.then_inc(s["staged"], 1)

            act.wait_ge(s["wqk_in"], 48)
            for n, (kind, part) in enumerate(FIRST):
                stage(kind, n, n % 2, True)

            def body(it, first, last):
                for k in steps(last):
                    tile = it * ITER + k - LAG
                    v = finished_at(k, first)
                    if v:
                        vslot, vhead, blk, _ = v
                        r = rows_of_head(vhead)
                        n = it * BLOCKS + blk
                        act.wait_ge(s["pv"], n + 1)
                        if blk % 4 == 0 and not first:
                            act.wait_ge(s["att_out"], it * 32 + (blk // 4) * 16 - 16)
                        stand_alone(act, turns)
                        g = (2 * it + blk // 4) % PAIRS
                        act.activation(ao[r, vslot, blk % 2], ov[r], ACT.Identity,
                                       bias=bsb[r, g, 2:3] if isinstance(g, int) else bsb[r, bass.ds(g, 1), 2])\
                            .then_inc(s["ov_read"], 1)
                    if transposes_at(k, first, last):
                        for part in range(2):
                            act.wait_ge(s["tr"], 2 * tile + part + 1)
                            u = (k - LAG) % ITER
                            act.activation(pT[:, (u // 4) % 2, 0, 4 * part:4 * part + 4, (u % 4) * P:(u % 4 + 1) * P],
                                           tr[:, part].rearrange("p (t q) -> p t q", t=4), ACT.Identity)\
                                .then_inc(s["tr_hi"], 1)
                    if not last:
                        u = it * ITER + k
                        act.wait_ge(s["negmax"], u + 1)
                        act.activation(pr[:, k % NP], sc[:, k % 2], ACT.Exp, bias=nmax[:, k % NP:k % NP + 1],
                                       accum_out=den[:, k % NP:k % NP + 1]).then_inc(s["exp"], 1)
                        if piece_at(it, k):
                            kind, _, n, slot = piece_at(it, k)
                            stage(kind, n, slot, False)
            over_iterations(act, body)

        @block_.gpsimd
        def _(pool):
            def v_parts(slot, t):
                to = (v_s[:, 0] if slot == 0 else v_b[:])[:, 2 * t:2 * t + 2]
                return to[:, :, 0::3], to[:, :, 1:3]

            def split_values(part, n, slot, nv):
                from_ = staged[:, slot].rearrange("p (t s h f) -> p t s h f", t=2, s=2, h=2)
                pool.wait_ge(s["staged"], n + 1)
                stand_alone(pool, turns)
                for x in range(2):
                    o = pool.tensor_scalar(v_parts(x, part)[0], from_[:, :, x], 1.0, 1.0, ALU.mult, ALU.mult)
                o.then_inc(s["v_hi"], 1)
                pool.wait_ge(s["v_hi"], nv + 1)
                for x in range(2):
                    hi, lo = v_parts(x, part)
                    o = pool.tensor_tensor(lo, from_[:, :, x], hi.bitcast(F32), ALU.subtract)
                o.then_inc(s["split"], 1)

            def split_qk(kind, part, n, slot, pair_slot, nqk, hi_only=False):
                (x0, x1), hi, lo = parts_of(kind, part, slot, pair_slot)
                pool.wait_ge(s["staged"], n + 1)
                stand_alone(pool, turns)
                pool.tensor_scalar(hi[0], x0, 1.0, 1.0, ALU.mult, ALU.mult).then_inc(s["head0_hi"], 1)
                pool.wait_ge(s["head0_hi"], nqk + 1)
                stand_alone(pool, turns)
                pool.tensor_scalar(hi[1], x1, 1.0, 1.0, ALU.mult, ALU.mult).then_inc(s["head1_hi"], 1)
                pool.wait_ge(s["head1_hi"], nqk + 1)
                if hi_only:
                    return
                pool.tensor_tensor(lo[0], x0, hi[0].bitcast(F32), ALU.subtract).then_inc(s["head0_lo"], 1)
                pool.wait_ge(s["head0_lo"], nqk + 1)
                pool.tensor_tensor(lo[1], x1, hi[1].bitcast(F32), ALU.subtract).then_inc(s["split"], 1)
                pool.wait_ge(s["split"], n + 1)

            for n, (kind, part) in enumerate(FIRST):
                if n == 4:
                    pool.wait_ge(s["first_split"], 4)
                    pool.sem_inc(s["split"], 4)
                if kind == "V":
                    split_values(part, n, n % 2, n - 4)
                else:
                    split_qk(kind, part, n, n % 2, 0, n, hi_only=True)

            def normalise(u, k):
                pool.wait_ge(s["rden"], u + 1)
                stand_alone(pool, turns)
                pool.tensor_scalar(pr[:, k % NP], pr[:, k % NP], rden[:, k % NP:k % NP + 1], 1.0,
                                   ALU.mult, ALU.mult).then_inc(s["normed"], 1)

            def body(it, first, last):
                for k in steps(last):
                    if (k > 0 and not last) or (k == 0 and not first):
                        normalise(it * ITER + k - 1, (k - 1) % ITER)
                    v = finished_at(k, first)
                    if v and v[2] % 4 == 3:
                        pool.wait_ge(s["ov_read"], it * BLOCKS + v[2] + 1)
                        pool.wait_ge(s["half"], it * BLOCKS + v[2] + 1)
                        pool.tensor_tensor(ao[:, v[0]], ao[:, v[0]], half[:], ALU.add).then_inc(s["att"], 1)
                    if not last and piece_at(it, k):
                        kind, part, n, slot = piece_at(it, k)
                        kinds = [x and x[0] == "V" for x in PLAN[:k]]
                        nv = sum(x is True for x in kinds)
                        if kind == "V":
                            split_values(part, n, slot, it * 4 + 4 + nv)
                        else:
                            pool.wait_ge(s["normed"], it * ITER + k)
                            split_qk(kind, part, n, slot, (k // STEPS + 1) % 2, it * 8 + 4 + sum(x is False for x in kinds))
            over_iterations(pool, body)

        @block_.vector
        def _(dve):
            for n, (kind, part) in enumerate(FIRST):
                if kind != "V":
                    xs, hi, lo = parts_of(kind, part, n % 2, 0)
                    for x in range(2):
                        dve.wait_ge(s["head%d_hi" % x], n + 1)
                        dve.tensor_tensor(lo[x], xs[x], hi[x].bitcast(F32), ALU.subtract)\
                            .then_inc(s["first_split" if x else "head0_lo"], 1)

            def body(it, first, last):
                for k in steps(last):
                    u = it * ITER + k
                    v = finished_at(k, first)
                    if v:
                        _, vhead, blk, _ = v
                        dve.wait_ge(s["pv"], it * BLOCKS + blk + 1)
                        if blk % 4 == 0 and not (first and blk < 4):
                            dve.wait_ge(s["att"], it * 2 + blk // 4)
                        dve.tensor_copy(half[rows_of_head(vhead), blk % 2], ov[rows_of_head(1 - vhead)])\
                            .then_inc(s["half"], 1)
                    if not last:
                        dve.wait_ge(s["sc"], u + 1)
                        if k % QT == 0:
                            dve.tensor_scalar(sc[0:1, k % 2, S - 1:S], sc[0:1, k % 2, S - 1:S], MASK, None,
                                              ALU.add).then_inc(s["masked"], 1)
                            dve.wait_ge(s["masked"], it * (ITER // QT) + k // QT + 1)
                        dve.tensor_reduce(nmax[:, k % NP:k % NP + 1], sc[:, k % 2], AX.X, ALU.max,
                                          negate=True).then_inc(s["negmax"], 1)
                    if (k == 0 and not first) or (k > 0 and not last):
                        j = (k - 1) % NP
                        dve.wait_ge(s["exp"], u)
                        dve.reciprocal(rden[:, j:j + 1], den[:, j:j + 1]).then_inc(s["rden"], 1)
                    if transposes_at(k, first, last):
                        t = (k - LAG) % ITER
                        for part in range(2):
                            dve.wait_ge(s["tr_hi"], 2 * (u - LAG) + part + 1)
                            to = pT[:, (t // 4) % 2, :, 4 * part:4 * part + 4, (t % 4) * P:(t % 4 + 1) * P]
                            dve.tensor_tensor(to[:, 1], tr[:, part].rearrange("p (t q) -> p t q", t=4),
                                              to[:, 0].bitcast(F32), ALU.subtract).then_inc(s["tr_lo"], 1)
            over_iterations(dve, body)

        @block_.tensor
        def _(pe):
            PARTS = ((0, 0), (0, 1), (1, 0))
            pe.wait_ge(s["const"], 32)

            def project(kind, part, n, start):
                bank = bank_of(n, start)
                if not start:
                    pe.wait_ge(s["staged"], n)
                elif n >= 2:
                    pe.wait_ge(s["staged"], n - 1)
                if kind in "QK":
                    i = 0
                    for c in range(DC):
                        for a, b in PARTS:
                            o = pe.matmul(bank[:], wqk_s[:, "QK".index(kind), c, a], z_s[:, c * 2 + b, part],
                                          start=(i == 0), stop=(i == 5))
                            i += 1
                else:
                    for t in range(2):
                        col = ((2 * part + t) % NT) * P
                        i = 0
                        for c in range(DC):
                            for a, b in PARTS:
                                o = pe.matmul(bank[:, t * 2 * P:(t + 1) * 2 * P],
                                              z_s[:, c * 2 + a, part // 2, col:col + P], wv_s[:, c, b],
                                              start=(i == 0), stop=(i == 5))
                                i += 1
                o.then_inc(s["pj"], 1)

            pe.wait_ge(s["wqk_in"], 48)
            pe.wait_ge(s["first_z"], 16)
            for n, (kind, part) in enumerate(FIRST):
                if n == 1:
                    pe.wait_ge(s["z_in"], 16)
                if n == 4:
                    pe.wait_ge(s["wv_in"], 16)
                project(kind, part, n, True)

            def body(it, first, last):
                for k in steps(last):
                    u = it * ITER + k
                    slot, head, tile = k // STEPS, (k // QT) % 2, k % QT
                    if not last:
                        if k % STEPS == 0:
                            pe.wait_ge(s["k_dup"], it * 64 + slot * 32 + 32)
                        if not (first and k < 2):
                            pe.wait_ge(s["exp"], u - 1)
                        for kb in range(S // BT):
                            for a in range(2):
                                o = pe.matmul(sc[:, k % 2, kb * BT:(kb + 1) * BT],
                                              q_s[:, slot, head, tile * P:(tile + 1) * P],
                                              k_s[:, slot, head, a, kb * BT:(kb + 1) * BT],
                                              start=(a == 0), stop=(a == 1))
                        o.then_inc(s["sc"], 1)
                    if transposes_at(k, first, last):
                        pe.wait_ge(s["normed"], u - LAG + 1)
                        for part in range(2):
                            if not (first and k == LAG):
                                pe.wait_ge(s["tr_lo"], 2 * (u - LAG) + part - 1)
                            for j in range(4):
                                o = pe.transpose(tr[:, part, j * P:(j + 1) * P],
                                                 pr[:, (k - LAG) % NP, (4 * part + j) * P:(4 * part + j + 1) * P], ident[:])
                            o.then_inc(s["tr"], 1)
                    v = values_at(k, first)
                    if v and not (last and v[2] >= 0):
                        vslot, vhead, blk, q = v
                        if q == 0:
                            pe.wait_ge(s["tr_lo"], 2 * (u - LAG))
                            if blk == 0:
                                pe.wait_ge(s["split"], before(it, 0))
                            if blk == 4:
                                pe.wait_ge(s["v_in"], it * 16 + 16)
                            if not (first and blk == 0):
                                pe.wait_ge(s["ov_read"], it * BLOCKS + blk)
                                pe.wait_ge(s["half"], it * BLOCKS + blk)
                        for kt in (2 * q, 2 * q + 1):
                            for a in range(2):
                                o = pe.matmul(ov[:], v_s[:, vslot, kt, 2 * vhead:2 * vhead + 2]
                                              .rearrange("p k f -> p (k f)"), pT[:, blk % 2, a, kt],
                                              start=(kt == 0 and a == 0), stop=(kt == QT - 1 and a == 1))
                        if q == 3:
                            o.then_inc(s["pv"], 1)
                    if not last and piece_at(it, k):
                        kind, part, n, _ = piece_at(it, k)
                        if kind == "Q" and part == 0:
                            pe.wait_ge(s["wqk_in"], it * 96 + (k // STEPS) * 48 + 96)
                            if k >= STEPS:
                                pe.wait_ge(s["z_in"], it * 32 + 48)
                        if kind == "V" and part == 0:
                            pe.wait_ge(s["wv_in"], it * 16 + 32)
                        project(kind, part, n, False)
            over_iterations(pe, body)


def mlp_phase(nc, turns, tag, w, att, z, x1, x2):
    PAIRS = AHD // P
    HP = PAIRS // 2
    HC = MH // P
    PARTS = ((0, 0), (0, 1), (1, 0))
    with ExitStack() as ctx:
        m = Bank(nc, ctx, tag)
        ident = m.sb("ident", [P, P])
        wo_in = m.sb("wo_in", [P, PAIRS, D])
        wo = m.sb("wo", [P, 2, PAIRS, D], F32R)
        w1_in = m.sb("w1_in", [P, DC, MH])
        w1 = m.sb("w1", [P, 2, DC, MH], F32R)
        w2_in = m.sb("w2_in", [P, HC, D])
        w2 = m.sb("w2", [P, 2, HC, D], F32R)
        ln = m.sb("ln", [P, DC, 2])
        b1_in = m.sb("b1_in", [P, HC])
        b1 = m.sb("b1", [P, HC])
        bo = m.sb("bo", [P, D])
        b2 = m.sb("b2", [P, D])
        mhalf = m.sb("mhalf", [P, NT])

        att_in = m.sb("att_in", [P, 2, HP, BT])
        att_s = m.sb("att_s", [P, 2, 2, PAIRS, BT], F32R)
        zin = m.sb("zin", [P, 2, NT, D])
        xin = m.sb("xin", [P, 2, NT, D])
        h = m.sb("h", [P, NT, D])
        st6 = m.sb("st6", [P, NT, 6])
        mv = m.sb("mv", [P, NT, 2])
        rs = m.sb("rs", [P, NT])
        hn = m.sb("hn", [P, NT, D])
        hT = m.sb("hT", [P, DC, 2, BT], F32R)
        act_out = m.sb("act_out", [P, HC, BT])
        hid_s = m.sb("hid_s", [P, HC, 2, BT], F32R)
        res = m.sb("res", [P, NT, D])
        proj = m.ps("proj", [P, NT, D])
        hT_ps = m.ps("hT_ps", [P, DC, BT])
        hid = m.ps("hid", [P, 2, BT])
        acc = m.ps("acc", [P, NT, D])

        s = {n: m.sem(n) for n in (
            "w_in mhalf w1_scaled w_hi w_ready b1_ps att_in0 att_in1 att_hi att_lo z_in x_in zb x_b proj h bn stats "
            "veps rstd hn hT_ps hT_hi hT_lo hid gelu hid_hi hid_lo acc x_h res res_out").split()}
        NW = 8
        block = ctx.enter_context(nc.Block())

        def over_steps(eng, body):
            body(0, 0)
            with eng.Fori(0, (NB - 4) // 2) as it:
                body(it * 2 + 1, 1)
                body(it * 2 + 2, 0)
            for i in range(NB - 3, NB + 1):
                body(i, i % 2)

        def has(i, ahead=0):
            return not isinstance(i, int) or 0 <= i + ahead < NB

        @block.sync
        def _(sp):
            def fixed(i):
                return i if isinstance(i, int) else sp.snap(i)

            def rows_of(ap, i):
                return ap.rearrange("(n t p) d -> n p t d", t=NT, p=P)[bass.ds(i, 1)].rearrange("n p t d -> p (n t) d")

            def load_att(token, half):
                from_ = att[half * HP:(half + 1) * HP, :, bass.ds(token, BT)].rearrange("g p t -> p g t")
                sp.dma_start(att_in[:, half], from_).then_inc(s["att_in%d" % half], 16)

            load_att(0, 0)
            load_att(0, 1)
            sp.dma_start(wo_in[:], w["wo"]).then_inc(s["w_in"], 16)
            sp.dma_start(ln[:], w["ln_m"]).then_inc(s["w_in"], 16)
            sp.dma_start(bo[:], w["bo"].partition_broadcast(P)).then_inc(s["w_in"], 16)
            sp.dma_start(b2[:], w["b2m"].partition_broadcast(P)).then_inc(s["w_in"], 16)
            sp.dma_start(b1_in[:], w["b1m"]).then_inc(s["w_in"], 16)
            sp.dma_start(ident[:], w["ident"]).then_inc(s["w_in"], 16)
            sp.dma_start(w1_in[:], w["w1m"]).then_inc(s["w_in"], 16)
            sp.dma_start(w2_in[:], w["w2m"]).then_inc(s["w_in"], 16)
            sp.dma_start(zin[:, 0], rows_of(z, 0)).then_inc(s["z_in"], 16)
            sp.dma_start(xin[:, 0], rows_of(x1, 0)).then_inc(s["x_in"], 16)
            for half in range(2):
                sp.wait_ge(s["att_lo"], half + 1)
                load_att(BT, half)
            for half in range(2):
                sp.wait_ge(s["att_lo"], 2 + half + 1)
                load_att(2 * BT, half)

            def body(i, par):
                if has(i, 3):
                    ahead = fixed((i + 3) * BT)
                if has(i, -1):
                    to = rows_of(x2, fixed(i - 1))
                if has(i, 1):
                    z_from, x_from = rows_of(z, fixed(i + 1)), rows_of(x1, fixed(i + 1))
                    sp.wait_ge(s["h"], i + 1)
                    sp.dma_start(zin[:, 1 - par], z_from).then_inc(s["z_in"], 16)
                if has(i, 3):
                    for half in range(2):
                        sp.wait_ge(s["att_lo"], (i + 2) * 2 + half + 1)
                        load_att(ahead, half)
                if has(i, -1):
                    sp.wait_ge(s["res"], i)
                    sp.dma_start(to, res[:]).then_inc(s["res_out"], 16)
                if has(i, 1):
                    sp.wait_ge(s["x_b"], i + 1)
                    sp.dma_start(xin[:, 1 - par], x_from).then_inc(s["x_in"], 16)
            over_steps(sp, body)
            sp.wait_ge(s["res_out"], NB * 16 + 16)

        @block.scalar
        def _(act):
            act.preload_act_table(ACT.Gelu_apprx_tanh)

            def att_hi(i, par, half):
                act.wait_ge(s["att_in%d" % half], i * 16 + 16)
                if has(i, -2):
                    act.wait_ge(s["proj"], i - 1)
                act.activation(att_s[:, par, 0, half * HP:(half + 1) * HP], att_in[:, half],
                               ACT.Identity).then_inc(s["att_hi"], 1)

            def gelu(i, hc):
                act.wait_ge(s["hid"], i * HC + hc + 1)
                act.activation(act_out[:, hc], hid[:, hc % 2], ACT.Gelu_apprx_tanh,
                               bias=b1[:, hc:hc + 1]).then_inc(s["gelu"], 1)

            def hid_hi(i, hc):
                act.wait_ge(s["gelu"], i * HC + hc + 1)
                if has(i, -1):
                    act.wait_ge(s["acc"], i)
                act.activation(hid_s[:, hc, 0], act_out[:, hc], ACT.Identity).then_inc(s["hid_hi"], 1)

            def hT_hi(i):
                for c in range(DC):
                    act.wait_ge(s["hT_ps"], i * DC + c + 1)
                    if c == 0 and has(i, -1):
                        act.wait_ge(s["hid"], i * HC)
                    act.activation(hT[:, c, 0], hT_ps[:, c], ACT.Identity).then_inc(s["hT_hi"], 1)

            act.wait_ge(s["att_in0"], 16)
            act.activation(att_s[:, 0, 0, 0:HP], att_in[:, 0], ACT.Identity).then_inc(s["att_hi"], 1)
            act.wait_ge(s["att_in1"], 16)
            act.activation(att_s[:, 0, 0, HP:PAIRS], att_in[:, 1], ACT.Identity).then_inc(s["att_hi"], 1)
            act.wait_ge(s["w_in"], 16 * NW)
            act.activation(wo[:, 0], wo_in[:], ACT.Identity).then_inc(s["w_hi"], 1)
            act.activation(w2[:, 0], w2_in[:], ACT.Identity).then_inc(s["w_hi"], 1)
            act.wait_ge(s["w1_scaled"], 1)
            act.activation(w1[:, 0], w1_in[:], ACT.Identity).then_inc(s["w_hi"], 1)
            for half in range(2):
                att_hi(1, 1, half)
            act.wait_ge(s["w_ready"], 3)

            def body(i, par):
                if has(i, -1):
                    gelu(i - 1, 0)
                    for hc in range(1, HC):
                        gelu(i - 1, hc)
                        hid_hi(i - 1, hc - 1)
                    hid_hi(i - 1, HC - 1)
                if has(i, 2):
                    att_hi(i + 2, par, 0)
                if has(i):
                    hT_hi(i)
                if has(i, 2):
                    att_hi(i + 2, par, 1)
            over_steps(act, body)

        @block.gpsimd
        def _(pool):
            pool.memset(mhalf[:], -0.5).then_inc(s["mhalf"], 1)
            pool.wait_ge(s["mhalf"], 1)
            pool.wait_ge(s["w_in"], 16 * NW)

            def add_rows(x, row):
                for t in range(NT):
                    o = pool.tensor_tensor(x[:, t], x[:, t], row[:], ALU.add)
                return o

            def z_bias(i, par):
                pool.wait_ge(s["z_in"], i * 16 + 16)
                add_rows(zin[:, par], bo).then_inc(s["zb"], 1)

            def x_bias(i, par):
                pool.wait_ge(s["x_in"], i * 16 + 16)
                add_rows(xin[:, par], b2).then_inc(s["x_b"], 1)
            z_bias(0, 0)

            def body(i, par):
                if has(i):
                    x_bias(i, par)
                    pool.wait_ge(s["stats"], i + 1)
                    stand_alone(pool, turns)
                    pool.tensor_scalar(rs[:], mv[:, :, 1], EPS, None, ALU.add).then_inc(s["veps"], 1)
                    pool.wait_ge(s["veps"], i + 1)
                    pool.tensor_tensor(rs[:], rs[:], mhalf[:], ALU.pow).then_inc(s["rstd"], 1)
                    pool.wait_ge(s["x_b"], i + 1)
                    pool.tensor_tensor(xin[:, par], xin[:, par], h[:], ALU.add).then_inc(s["x_h"], 1)
                if has(i, 1):
                    z_bias(i + 1, 1 - par)
            over_steps(pool, body)

        @block.vector
        def _(dve):
            def att_lo(i, par, half):
                dve.wait_ge(s["att_hi"], i * 2 + half + 1)
                g = slice(half * HP, (half + 1) * HP)
                dve.tensor_tensor(att_s[:, par, 1, g], att_in[:, half], att_s[:, par, 0, g].bitcast(F32),
                                  ALU.subtract).then_inc(s["att_lo"], 1)

            def hid_lo(i, hc):
                dve.wait_ge(s["hid_hi"], i * HC + hc + 1)
                dve.tensor_tensor(hid_s[:, hc, 1], act_out[:, hc], hid_s[:, hc, 0].bitcast(F32),
                                  ALU.subtract).then_inc(s["hid_lo"], 1)

            dve.sem_inc(s["res_out"], 16)
            att_lo(0, 0, 0)
            att_lo(0, 0, 1)
            dve.wait_ge(s["w_in"], 16 * NW)
            dve.wait_ge(s["w_hi"], 1)
            dve.tensor_tensor(wo[:, 1], wo_in[:], wo[:, 0].bitcast(F32), ALU.subtract).then_inc(s["w_ready"], 1)
            dve.wait_ge(s["b1_ps"], 1)
            dve.tensor_tensor(b1[:], hid[:, 0, 0:HC], b1_in[:], ALU.add)
            for c in range(DC):
                o = dve.tensor_scalar(w1_in[:, c], w1_in[:, c], ln[:, c, 0:1], None, ALU.mult)
            o.then_inc(s["w1_scaled"], 1)
            dve.wait_ge(s["w_hi"], 2)
            dve.tensor_tensor(w2[:, 1], w2_in[:], w2[:, 0].bitcast(F32), ALU.subtract).then_inc(s["w_ready"], 1)
            dve.wait_ge(s["w_hi"], 3)
            dve.tensor_tensor(w1[:, 1], w1_in[:], w1[:, 0].bitcast(F32), ALU.subtract).then_inc(s["w_ready"], 1)
            for half in range(2):
                att_lo(1, 1, half)

            def body(i, par):
                if has(i):
                    dve.wait_ge(s["proj"], i + 1)
                    dve.wait_ge(s["zb"], i + 1)
                    if has(i, -1):
                        dve.wait_ge(s["x_h"], i)
                    dve.tensor_tensor(h[:], proj[:], zin[:, par], ALU.add).then_inc(s["h"], 1)
                    dve.wait_ge(s["h"], i + 1)
                    for t in range(NT):
                        o = dve.bn_stats(st6[:, t], h[:, t])
                    o.then_inc(s["bn"], 1)
                    dve.wait_ge(s["bn"], i + 1)
                    stand_alone(dve, turns)
                    for t in range(NT):
                        o = dve.bn_aggr(mv[:, t], st6[:, t])
                    o.then_inc(s["stats"], 1)
                if has(i, -1):
                    hid_lo(i - 1, 0)
                    hid_lo(i - 1, 1)
                if has(i):
                    dve.wait_ge(s["rstd"], i + 1)
                    if has(i, -1):
                        dve.wait_ge(s["hT_ps"], i * DC)
                    for t in range(NT):
                        o = dve.tensor_scalar(hn[:, t], h[:, t], mv[:, t, 0:1], rs[:, t:t + 1],
                                              ALU.subtract, ALU.mult)
                    o.then_inc(s["hn"], 1)
                if has(i, -1):
                    hid_lo(i - 1, 2)
                    hid_lo(i - 1, 3)
                if has(i, 2):
                    att_lo(i + 2, par, 0)
                if has(i):
                    for c in range(DC):
                        dve.wait_ge(s["hT_hi"], i * DC + c + 1)
                        dve.tensor_tensor(hT[:, c, 1], hT_ps[:, c], hT[:, c, 0].bitcast(F32),
                                          ALU.subtract).then_inc(s["hT_lo"], 1)
                if has(i, 2):
                    att_lo(i + 2, par, 1)
                if has(i, -1):
                    dve.wait_ge(s["acc"], i)
                    dve.wait_ge(s["x_h"], i)
                    dve.wait_ge(s["res_out"], i * 16)
                    dve.tensor_tensor(res[:], acc[:], xin[:, 1 - par], ALU.add).then_inc(s["res"], 1)
            over_steps(dve, body)

        @block.tensor
        def _(pe):
            def project(i, par, tiles):
                for t in tiles:
                    for g in range(PAIRS):
                        for a, b in PARTS:
                            o = pe.matmul(proj[:, t], att_s[:, par, a, g, t * P:(t + 1) * P], wo[:, b, g],
                                          start=(t % 2 == 0 and g == 0 and (a, b) == (0, 0)),
                                          stop=(g == PAIRS - 1 and (a, b) == PARTS[-1]), skip_group_check=True)
                return o

            pe.wait_ge(s["w_in"], 16 * NW)
            for hc in range(HC):
                for c in range(DC):
                    o = pe.matmul(hid[:, 0, hc:hc + 1], w1_in[:, c, hc * P:(hc + 1) * P], ln[:, c, 1:2],
                                  start=(c == 0), stop=(c == DC - 1))
            o.then_inc(s["b1_ps"], 1)
            pe.wait_ge(s["att_lo"], 2)
            pe.wait_ge(s["w_ready"], 1)
            project(0, 0, range(NT)).then_inc(s["proj"], 1)
            pe.wait_ge(s["w_ready"], 3)

            def body(i, par):
                if has(i, 1):
                    pe.wait_ge(s["att_lo"], (i + 1) * 2 + 2)
                    pe.wait_ge(s["h"], i + 1)
                    project(i + 1, 1 - par, (0, 1))
                if has(i):
                    pe.wait_ge(s["hn"], i + 1)
                    if has(i, -1):
                        pe.wait_ge(s["hT_lo"], i * DC)
                    for c in range(DC):
                        for t in range(NT):
                            o = pe.transpose(hT_ps[:, c, t * P:(t + 1) * P], hn[:, t, c * P:(c + 1) * P], ident[:])
                        o.then_inc(s["hT_ps"], 1)
                if has(i, -1):
                    pe.wait_ge(s["hid_lo"], i * HC)
                    if not has(i):
                        pe.wait_ge(s["res"], i - 1)
                    for t in range(NT):
                        for hc in range(HC):
                            for a, b in PARTS:
                                o = pe.matmul(acc[:, t], hid_s[:, hc, a, t * P:(t + 1) * P], w2[:, b, hc],
                                              start=(t % 2 == 0 and hc == 0 and (a, b) == (0, 0)),
                                              stop=(hc == HC - 1 and (a, b) == PARTS[-1]), skip_group_check=True)
                    o.then_inc(s["acc"], 1)
                if has(i, 1):
                    project(i + 1, 1 - par, (2, 3)).then_inc(s["proj"], 1)
                if has(i):
                    pe.wait_ge(s["hT_lo"], i * DC + DC)
                    for hc in range(HC):
                        if hc >= 2 or has(i, -1):
                            pe.wait_ge(s["gelu"], i * HC + hc - 1)
                        n = 0
                        for c in range(DC):
                            for a, b in PARTS:
                                o = pe.matmul(hid[:, hc % 2], w1[:, a, c, hc * P:(hc + 1) * P], hT[:, c, b],
                                              start=(n == 0), stop=(n == 5))
                                n += 1
                        o.then_inc(s["hid"], 1)
            over_steps(pe, body)


def kernel(**inputs):
    import numpy as _np
    import concourse.bacc as _bacc
    from concourse import mybir as _mybir
    from concourse.bass_utils import run_bass_kernel_spmd as _run

    nc = _bacc.Bacc("TRN2", target_bir_lowering=False, num_devices=1)
    arrays, w = {}, {}

    def give(name, a):
        a = _np.ascontiguousarray(a)
        arrays[f"in_{name}"] = a
        w[name] = nc.dram_tensor(f"in_{name}", a.shape, _mybir.dt.from_np(a.dtype), kind="ExternalInput").ap()

    def scratch(name, shape, dt=F32):
        return nc.dram_tensor(name, shape, dt, kind="Internal").ap()

    i = {k: _np.asarray(v) for k, v in inputs.items()}
    rows_in = lambda a: a.reshape(a.shape[0] // P, P, -1).transpose(1, 0, 2).reshape(P, -1)
    give("x", i["L0_attn_x"].reshape(TOK, D))
    w1 = _np.concatenate([i["L0_ffn_W1"], i["L0_ffn_Ws1"][None]]).transpose(1, 0, 2).reshape(D, NE * HID)
    give("w1", rows_in(w1))
    give("w2", _np.concatenate([i["L0_ffn_W2"], i["L0_ffn_Ws2"][None]]).transpose(1, 0, 2).reshape(HID, NE * D))
    give("b1", _np.concatenate([i["L0_ffn_b1"], i["L0_ffn_bs1"][None]]).T)
    give("b2", _np.concatenate([i["L0_ffn_b2"], i["L0_ffn_bs2"][None]]))
    give("gw", rows_in(i["L0_ffn_gate_W"]))
    give("rscale", i["L0_ffn_route_scale"].reshape(1, 1))
    give("ident", _np.eye(P, dtype=_np.float32))
    give("iota", _np.tile(_np.arange(E, dtype=_np.float32), (P, 1)))
    sel = _np.zeros((P, E, P), _np.float32)
    for e in range(E):
        sel[e, e] = sel[E + e, e] = 1.0
    give("sel", sel.reshape(P, E * P))
    rows = _np.zeros((P, 2), _np.float32)
    rows[[*range(2 * E), 3 * E], 0] = 1.0
    rows[[*range(2 * E, 3 * E), 3 * E + 1], 1] = 1.0
    give("rows", rows)
    give("w_qkv", _np.stack([rows_in(i[f"L0_attn_W{c}"]).reshape(P, DC, AHD) for c in "qkv"]))
    give("ln_qkv", _np.stack([_np.stack([rows_in(i[f"L0_attn_ln{c}_{x}"][:, None]) for x in "sb"], -1) for c in "qkv"], 1))
    give("c_qkv", _np.stack([rows_in(i[f"L0_attn_b{c}"][:, None]) for c in "qkv"], 1))
    give("wo", rows_in(i["L0_attn_Wo"]).reshape(P, AHD // P, D))
    give("w1m", rows_in(i["L0_attn_W1"]).reshape(P, DC, MH))
    give("w2m", rows_in(i["L0_attn_W2"]).reshape(P, MH // P, D))
    give("ln_m", _np.stack([rows_in(i[f"L0_attn_lnm_{x}"][:, None]) for x in "sb"], -1))
    give("b1m", rows_in(i["L0_attn_b1"][:, None]))
    give("bo", i["L0_attn_bo"][None])
    give("b2m", i["L0_attn_b2"][None])
    x1, z, x2 = (scratch(n, (TOK, D)) for n in ("x1", "z", "x2"))
    zT = scratch("zT", (NB, P, DC, 2, BT))
    w_split = scratch("w_split", (3, P, DC, 2, AHD))
    bias = scratch("bias", (P, AHD // P, 3))
    att = scratch("att", (AHD // P, P, TOK))
    out = nc.dram_tensor("out", (TOK, D), F32, kind="ExternalOutput").ap()

    with nc.semaphore("turns") as turns:
        ffn_phase(nc, turns, "f", w["x"], x1, w, {"z": z, "zT": zT, "w_split": w_split, "bias": bias})
        attention_phase(nc, turns, "a", w, zT, w_split, bias, att)
        mlp_phase(nc, turns, "m", w, att, z, x1, x2)
        ffn_phase(nc, turns, "g", x2, out, w, None)
    r = _run(nc, [arrays], core_ids=[0])
    return r.results[0]["out"].reshape(B, S, D)
```
